# Optimizing a Trainium2 kernel written in Bass

```python
import numpy as np
import jax
import jax.numpy as jnp

def _softmax(x, axis=-1):
    return jax.nn.softmax(x, axis=axis)

def _gelu(x):
    return jax.nn.gelu(x, approximate=True)

def _silu(x):
    return jax.nn.silu(x)

def _sigmoid(x):
    return jax.nn.sigmoid(x)

def _layernorm(x, axis=-1, eps=1e-05):
    m = jnp.mean(x, axis=axis, keepdims=True)
    v = jnp.var(x, axis=axis, keepdims=True)
    return (x - m) / jnp.sqrt(v + eps)

def _scatter_add(tgt, idx, src, axis=0):
    return tgt.at[idx].add(src)

def _segment_sum(src, seg, n):
    return jax.ops.segment_sum(src, seg, n)
kernel_name = 'mk_gnn_ffn_d1_gnn_r8_c6151d'

def setup_inputs(seed: int=0):
    np.random.seed(seed)
    _w = jnp.asarray

    def _rec_inputs():
        import jax
        import jax.numpy as jnp
        _gk = jax.random.key(seed)
        x = -0.0001126 + 1 * jax.random.normal(jax.random.fold_in(_gk, 1), (3750, 256), jnp.float32)
        src = jax.random.randint(jax.random.fold_in(_gk, 2), (60000,), 0, 3750, jnp.int32)
        dst = jax.random.randint(jax.random.fold_in(_gk, 3), (60000,), 0, 3750, jnp.int32)
        _o = jnp.argsort(dst, stable=True)
        src = src[_o]
        dst = dst[_o]
        edge_type_8 = jax.random.randint(jax.random.fold_in(_gk, 12), (60000,), 0, 8, jnp.int32)
        return (x, src, dst, edge_type_8)
    x, src, dst, edge_type_8 = _rec_inputs()

    def _L0_gnn_setup():
        import jax, jax.numpy as jnp
        import numpy as np
        N_NODES = 3750
        N_EDGES = 60000
        IN_FEAT = 256
        OUT_FEAT = 256
        N_RELS = 8
        N_HEADS = 4
        HEAD_DIM = OUT_FEAT // N_HEADS
        LEAKY_SLOPE = 0.2
        key = jax.random.key(seed)
        ks = jax.random.split(key, 8)
        inputs = jax.random.normal(ks[0], (N_NODES, IN_FEAT), dtype=jnp.float32)
        conv_weights = jax.random.normal(ks[1], (N_RELS, N_HEADS, IN_FEAT, HEAD_DIM), dtype=jnp.float32) * (1.0 / np.sqrt(IN_FEAT))
        attn_l = jax.random.normal(ks[2], (N_RELS, N_HEADS, HEAD_DIM), dtype=jnp.float32) * 0.1
        attn_r = jax.random.normal(ks[3], (N_RELS, N_HEADS, HEAD_DIM), dtype=jnp.float32) * 0.1
        h_bias = jax.random.normal(ks[4], (OUT_FEAT,), dtype=jnp.float32) * 0.02
        edge_src = jax.random.randint(ks[5], (N_EDGES,), 0, N_NODES, dtype=jnp.int32)
        edge_dst = jax.random.randint(ks[6], (N_EDGES,), 0, N_NODES, dtype=jnp.int32)
        edge_type = jax.random.randint(ks[7], (N_EDGES,), 0, N_RELS, dtype=jnp.int32)
        return {'inputs': inputs, 'conv_weights': conv_weights, 'attn_l': attn_l, 'attn_r': attn_r, 'h_bias': h_bias, 'edge_src': edge_src, 'edge_dst': edge_dst, 'edge_type': edge_type}
    _L0_gnn_all = _L0_gnn_setup()
    _L0_gnn_in = {k: v for k, v in _L0_gnn_all.items() if k in ('conv_weights', 'attn_l', 'attn_r', 'h_bias')}
    del _L0_gnn_all

    def _L0_ffn_setup():
        import jax, jax.numpy as jnp
        import numpy as np
        NUM_EXPERTS = 8
        TOP_K = 2
        B, S, D = (8, 1024, 256)

        def _moe(tokens, router_w, w1, b1, w2, b2):
            N = tokens.shape[0]
            E = router_w.shape[0]
            logits = tokens.astype(jnp.float32) @ router_w.astype(jnp.float32).T
            probs = jax.nn.softmax(logits, axis=-1)
            rw, re = jax.lax.top_k(probs, TOP_K)
            if TOP_K > 1:
                rw = rw / jnp.maximum(rw.sum(-1, keepdims=True), 1e-12)
            rw = rw.astype(tokens.dtype)
            combine = jnp.zeros((N, E), tokens.dtype).at[jnp.arange(N)[:, None], re].set(rw)
            out = tokens
            for e in range(E):
                h = jax.nn.gelu(tokens @ w1[e] + b1[e], approximate=False)
                y = h @ w2[e] + b2[e]
                out = out + combine[:, e:e + 1] * y
            return out
        key = jax.random.key(seed)
        ks = jax.random.split(key, 4)
        scale = 1.0 / np.sqrt(D).astype(np.float32)
        return {'input_embeddings': jax.random.normal(ks[0], (B, S, D), jnp.float32), 'router_w': jax.random.normal(ks[1], (NUM_EXPERTS, D), jnp.float32) * scale, 'w1': jax.random.normal(ks[2], (NUM_EXPERTS, D, D), jnp.float32) * scale, 'b1': jnp.zeros((NUM_EXPERTS, D), jnp.float32), 'w2': jax.random.normal(ks[3], (NUM_EXPERTS, D, D), jnp.float32) * scale, 'b2': jnp.zeros((NUM_EXPERTS, D), jnp.float32)}
    _L0_ffn_all = _L0_ffn_setup()
    _L0_ffn_in = {k: v for k, v in _L0_ffn_all.items() if k in ('router_w', 'w1', 'b1', 'w2', 'b2')}
    del _L0_ffn_all
    return {'x': x, 'src': src, 'dst': dst, 'edge_type_8': edge_type_8, 'L0_gnn_conv_weights': _L0_gnn_in['conv_weights'], 'L0_gnn_attn_l': _L0_gnn_in['attn_l'], 'L0_gnn_attn_r': _L0_gnn_in['attn_r'], 'L0_gnn_h_bias': _L0_gnn_in['h_bias'], 'L0_ffn_router_w': _L0_ffn_in['router_w'], 'L0_ffn_w1': _L0_ffn_in['w1'], 'L0_ffn_b1': _L0_ffn_in['b1'], 'L0_ffn_w2': _L0_ffn_in['w2'], 'L0_ffn_b2': _L0_ffn_in['b2']}

def reference(x, src, dst, edge_type_8, L0_gnn_conv_weights, L0_gnn_attn_l, L0_gnn_attn_r, L0_gnn_h_bias, L0_ffn_router_w, L0_ffn_w1, L0_ffn_b1, L0_ffn_w2, L0_ffn_b2):
    import jax
    import jax.numpy as jnp

    def _L0_gnn_ref(inputs, conv_weights, attn_l, attn_r, h_bias, edge_src, edge_dst, edge_type):
        import jax, jax.numpy as jnp
        import numpy as np
        N_NODES = 3750
        N_EDGES = 60000
        IN_FEAT = 256
        OUT_FEAT = 256
        N_RELS = 8
        N_HEADS = 4
        HEAD_DIM = OUT_FEAT // N_HEADS
        LEAKY_SLOPE = 0.2
        feat_all = jnp.einsum('ni,rhid->rnhd', inputs, conv_weights)
        feat_src_e = feat_all[edge_type, edge_src]
        feat_dst_e = feat_all[edge_type, edge_dst]
        el = jnp.sum(feat_src_e * attn_l[edge_type], axis=-1)
        er = jnp.sum(feat_dst_e * attn_r[edge_type], axis=-1)
        e = jax.nn.leaky_relu(el + er, negative_slope=LEAKY_SLOPE)
        m = jax.ops.segment_max(e, edge_dst, num_segments=N_NODES)
        ex = jnp.exp(e - m[edge_dst])
        denom = jax.ops.segment_sum(ex, edge_dst, num_segments=N_NODES)
        alpha = ex / denom[edge_dst]
        h = jax.ops.segment_sum(alpha[..., None] * feat_src_e, edge_dst, num_segments=N_NODES)
        h = h.reshape(N_NODES, OUT_FEAT) + h_bias
        return h

    def _L0_ffn_ref(input_embeddings, router_w, w1, b1, w2, b2):
        import jax, jax.numpy as jnp
        import numpy as np
        NUM_EXPERTS = 8
        TOP_K = 2
        B, S, D = (8, 1024, 256)

        def _moe(tokens, router_w, w1, b1, w2, b2):
            N = tokens.shape[0]
            E = router_w.shape[0]
            logits = tokens.astype(jnp.float32) @ router_w.astype(jnp.float32).T
            probs = jax.nn.softmax(logits, axis=-1)
            rw, re = jax.lax.top_k(probs, TOP_K)
            if TOP_K > 1:
                rw = rw / jnp.maximum(rw.sum(-1, keepdims=True), 1e-12)
            rw = rw.astype(tokens.dtype)
            combine = jnp.zeros((N, E), tokens.dtype).at[jnp.arange(N)[:, None], re].set(rw)
            out = tokens
            for e in range(E):
                h = jax.nn.gelu(tokens @ w1[e] + b1[e], approximate=False)
                y = h @ w2[e] + b2[e]
                out = out + combine[:, e:e + 1] * y
            return out
        b, s, d = input_embeddings.shape
        tokens = input_embeddings.reshape(b * s, d)
        return _moe(tokens, router_w, w1, b1, w2, b2).reshape(b, s, d)
    x = x + _L0_gnn_ref(_layernorm(x, axis=-1), L0_gnn_conv_weights, L0_gnn_attn_l, L0_gnn_attn_r, L0_gnn_h_bias, src, dst, edge_type_8)
    x = x + _L0_ffn_ref(_layernorm(x, axis=-1)[None], L0_ffn_router_w, L0_ffn_w1, L0_ffn_b1, L0_ffn_w2, L0_ffn_b2)[0]
    return x

_drawn_inputs = setup_inputs


def setup_inputs(seed=0):
    import zlib

    import numpy as np

    out = dict(_drawn_inputs(seed))
    spreads = {'L0_ffn_b1': (0.0, 0.334), 'L0_ffn_b2': (0.0, 0.1)}
    factors = {}
    for name, (base, spread) in spreads.items():
        noise = np.random.default_rng([zlib.crc32(name.encode()), seed]).standard_normal(out[name].shape)
        drawn = base * np.exp(spread * noise) if base else spread * noise
        out[name] = jnp.asarray(drawn.astype(out[name].dtype))
    for name, factor in factors.items():
        out[name] = (out[name] * factor).astype(out[name].dtype)
    return out
```

```python
import concourse.bass as bass
from concourse import mybir
from contextlib import ExitStack

F32 = mybir.dt.float32
I32 = mybir.dt.int32
U32 = mybir.dt.uint32
ALU = mybir.AluOpType
ACT = mybir.ActivationFunctionType
AX = mybir.AxisListType

P = 128
N, D = 3750, 256
NT = (N + P - 1) // P
NP_ = NT * P
NLAST = N - (NT - 1) * P
E = 60000
R, H, HD = 8, 4, 64
RH, RHD = R * H, R * H * HD
KC = D // P
ET = (E + P - 1) // P
ELAST = E - (ET - 1) * P
C, J = 32, 15
ETP = C * J
L = J * P
G = 3
W = 32
NG = (ET + G - 1) // G
RING = 12
GPI = RING // G
TURNS = (ET - 1) // RING
EPS = 1e-5
BIG = 1e30
X = 8
TC = 3
NC = NT // TC
TOK = TC * P
SG = 6
WORK = 15400


def gnn_moe(nc, x, src, dst, etype, conv_w, attn_l, attn_r, h_bias, router_w, w1, b1, w2, b2, out):
    assert ET - 1 == RING * TURNS and RING % G == 0 and NT % 6 == 0 and ETP >= ET
    ctx = ExitStack()
    with ctx:
        ctx.enter_context(nc.allow_non_contiguous_dma(reason="a few hundred window bases and small weights"))

        def sb(name, shape, dt=F32):
            return ctx.enter_context(nc.sbuf_tensor(name, shape, dt))

        def sem(name):
            return ctx.enter_context(nc.semaphore(name))

        ds = bass.ds
        feat_tab = nc.dram_tensor("feat_tab", [NP_ * R, D], F32)
        el_tab = nc.dram_tensor("el_tab", [NP_ * R, H], F32)
        er_tab = nc.dram_tensor("er_tab", [NP_ * R, H], F32)

        ident = sb("ident", [P, P])
        ones = sb("ones", [P, P])
        x_sb = sb("x_sb", [P, NT * D])
        acc = sb("acc", [P, KC * NP_])
        weights = sb("weights", [P, KC * RHD + 2 * RHD])
        work = sb("work", [P, WORK])
        alpha = sb("alpha", [P, ETP * H])
        el = sb("el", [P, ETP * H])
        er = sb("er", [P, 5 * NT * 8])
        score_ring = sb("score_ring", [P, 4 * SG * H])
        idx_l = sb("idx_l", [P, 4 * P], I32)
        idx_r = sb("idx_r", [P, 4 * P], I32)
        idx_ring = sb("idx_ring", [P, 4 * SG], I32)
        dst_t = sb("dst_t", [P, 4 * P])
        rel = sb("rel", [P, ETP])
        base_i = sb("base_i", [1, NG], I32)
        base_f = sb("base_f", [1, NG])
        stats = sb("stats", [P, NT * 6])
        mv = sb("mv", [P, NT * 2])
        rstd = sb("rstd", [P, NT])
        iota_w = sb("iota_w", [P, W])
        hb = sb("hb", [P, KC])
        b1_sb = sb("b1_sb", [P, X * KC])
        b2_sb = sb("b2_sb", [X, D])
        rw_sb = sb("rw_sb", [X, D])
        rwT = sb("rwT", [P, KC * X])

        psum = [ctx.enter_context(nc.psum_tensor(f"bank{i}", [P, 512], F32)) for i in range(8)]

        def carve(start, n):
            return work[:, start:start + n], start + n

        wconv = weights[:, 0:KC * RHD]
        fout = weights[:, KC * RHD:KC * RHD + 2 * RHD]
        att_l, o = carve(0, RHD)
        att_r, o = carve(o, RHD)
        prod, o = carve(o, RHD)
        wa, o = carve(o, KC * 2 * RH)
        rowi_f, o = carve(o, 3 * 4 * P)
        rowi = rowi_f.bitcast(I32)
        rowf, o = carve(o, 3 * 4 * P)
        rowx, o = carve(o, 2 * 4 * P)
        xn, o = carve(o, 2 * D)
        xT, o = carve(o, 2 * D)
        elr, o = carve(o, NT * 2 * RH)
        assert o <= WORK, o
        dsti_f, o = carve(0, L + 2)
        dsti = dsti_f.bitcast(I32)
        dstf, o = carve(o, L + 2)
        same, o = carve(o, L + 2)
        pen, o = carve(o, L + 2)
        ebulk, o = carve(o, L)
        fwd, o = carve(o, L)
        bwd, o = carve(o, L)
        e_ht, o = carve(o, L)
        assert o <= WORK, o
        edge_col = sb("edge_col", [P, 4])
        edge_row = sb("edge_row", [1, 4 * P])
        scan_row = sb("scan_row", [1, 2 * (P + 2)])
        carry = sb("carry", [P, 2])

        const_done = sem("const_done")
        pool_step = sem("pool_step")
        x_in = sem("x_in")
        w_in = sem("w_in")
        attn_in = sem("attn_in")
        rows_in = sem("rows_in")
        base_in = sem("base_in")
        dstb_in = sem("dstb_in")
        small_in = sem("small_in")
        dve_step = sem("dve_step")
        xn_done = sem("xn_done")
        var_done = sem("var_done")
        std_done = sem("std_done")
        rows_done = sem("rows_done")
        rowsT_done = sem("rowsT_done")
        idx_done = sem("idx_done")
        rel_done = sem("rel_done")
        wa_done = sem("wa_done")
        xn_done2 = sem("xn_done2")
        xt_done2 = sem("xt_done2")
        xt_copied2 = sem("xt_copied2")
        xt_done = sem("xt_done")
        xt_copied = sem("xt_copied")
        el_done = sem("el_done")
        el_copied = sem("el_copied")
        tab_out = sem("tab_out")
        feat_done = sem("feat_done")
        feat_act = sem("feat_act")
        feat_dve = sem("feat_dve")
        feat_out = [sem(f"feat_out{u}") for u in range(2)]
        gathered = [sem(f"gathered{s}") for s in range(2)]
        scores_done = sem("scores_done")
        idx_copied = sem("idx_copied")
        dstb_clear = sem("dstb_clear")
        eht_done = sem("eht_done")
        ebulk_psum = sem("ebulk_psum")
        ebulk_done = sem("ebulk_done")
        cols_done = sem("cols_done")
        rows_psum = sem("rows_psum")
        srow_done = sem("srow_done")
        carry_psum = sem("carry_psum")
        shifted = sem("shifted")
        exp_done = sem("exp_done")
        alpha_bulk = sem("alpha_bulk")
        alpha_psum = sem("alpha_psum")

        x_tiles = x[0:(NT - 1) * P, :].rearrange("(t p) d -> p t d", p=P)

        with nc.Block() as block:
            @block.sync
            def _(sp):
                sp.wait_ge(const_done, 1)
                sp.dma_start(x_sb[:, 0:(NT - 1) * D].rearrange("p (t d) -> p t d", d=D), x_tiles).then_inc(x_in, 16)
                sp.dma_start(x_sb[0:NLAST, (NT - 1) * D:NT * D], x[(NT - 1) * P:N, :]).then_inc(x_in, 16)
                for s, a in enumerate((src, dst, etype)):
                    full = rowi[:, s * 4 * P:s * 4 * P + 3 * P].rearrange("t (b p) -> t b p", p=P)
                    sp.dma_start(full, a[0:3 * P * P].rearrange("(b t p) -> t b p", b=3, p=P)).then_inc(rows_in, 16)
                    rest = ET - 1 - 3 * P
                    last = rowi[:, (s * 4 + 3) * P:(s * 4 + 4) * P]
                    sp.dma_start(last[0:rest, :], a[3 * P * P:(ET - 1) * P].rearrange("(t p) -> t p", p=P))\
                      .then_inc(rows_in, 16)
                    sp.dma_start(last[rest:rest + 1, 0:ELAST], a[(ET - 1) * P:E].rearrange("(t p) -> t p", t=1))\
                      .then_inc(rows_in, 16)
                step = G * P
                sp.dma_start(base_i[0:1, 0:NG - 1], dst[0:(NG - 1) * step].rearrange("(g e) -> e g", e=step)[0:1, :])\
                  .then_inc(base_in, 16)
                sp.dma_start(base_i[0:1, NG - 1:NG], dst[(NG - 1) * step:(NG - 1) * step + 1]
                             .rearrange("(a b) -> a b", a=1)).then_inc(base_in, 16)
                sp.dma_start(att_l, attn_l.rearrange("r h d -> (r h d)").partition_broadcast(P)).then_inc(attn_in, 16)
                sp.dma_start(att_r, attn_r.rearrange("r h d -> (r h d)").partition_broadcast(P)).then_inc(attn_in, 16)
                for r in range(R):
                    for k in range(KC):
                        o = k * RHD + r * H * HD
                        sp.dma_start(wconv[:, o:o + H * HD].rearrange("p (h d) -> p h d", d=HD),
                                     conv_w[r, :, k * P:(k + 1) * P, :].rearrange("h p d -> p h d")).then_inc(w_in, 16)
                sp.dma_start(hb[:, :], h_bias.rearrange("(k p) -> p k", p=P)).then_inc(small_in, 16)
                sp.dma_start(b1_sb[:, :].rearrange("p (e k) -> p e k", k=KC), b1.rearrange("e (k p) -> p e k", p=P))\
                  .then_inc(small_in, 16)
                sp.dma_start(b2_sb[:, :], b2).then_inc(small_in, 16)
                sp.dma_start(rw_sb[:, :], router_w).then_inc(small_in, 16)
                sp.wait_ge(small_in, 64)
                sp.wait_ge(el_copied, NT)
                for k, tab in enumerate((el_tab, er_tab)):
                    part = elr.rearrange("p (t s c) -> p t s c", s=2, c=RH)[:, :, k, :]
                    sp.dma_start(tab[:, :].rearrange("(t p r) h -> p t (r h)", p=P, r=R), part).then_inc(tab_out, 16)
                with sp.Fori(0, NT // 2) as i:
                    for u in range(2):
                        sp.wait_ge(feat_act, i * 4 + 2 * u + 2)
                        sp.wait_ge(feat_dve, i * 4 + 2 * u + 2)
                        sp.dma_start(feat_tab[ds(i * (2 * P * R) + u * P * R, P * R), :]
                                     .rearrange("(p r) d -> p (r d)", r=R),
                                     fout[:, u * RHD:(u + 1) * RHD]).then_inc(feat_out[u], 16)
                for u in range(2):
                    sp.wait_ge(feat_out[u], 16 * (NT // 2))
                sp.wait_ge(tab_out, 32)
                sp.wait_ge(dstb_clear, 1)

                def row(a, b):
                    return dst[a:b].rearrange("(o n) -> o n", o=1)

                for h in range(H):
                    p = h * C
                    for to, frm in (
                        (dsti[p:p + 1, 1:L + 2], row(0, L + 1)),
                        (dsti[p + 1:p + C - 1, 0:L], dst[L - 1:(C - 1) * L - 1].rearrange("(c l) -> c l", l=L)),
                        (dsti[p + 1:p + C - 1, L:L + 1],
                         dst[L:(C - 1) * L].rearrange("(c l) -> c l", l=L)[:, L - 1:L]),
                        (dsti[p + 1:p + C - 2, L + 1:L + 2],
                         dst[2 * L:(C - 1) * L].rearrange("(c l) -> c l", l=L)[:, 0:1]),
                        (dsti[p + C - 2:p + C - 1, L + 1:L + 2], row((C - 1) * L, (C - 1) * L + 1)),
                        (dsti[p + C - 1:p + C, 0:E - (C - 1) * L + 1], row((C - 1) * L - 1, E)),
                    ):
                        sp.dma_start(to, frm).then_inc(dstb_in, 16)

            @block.gpsimd
            def _(pool):
                pool.memset(x_sb[:, (NT - 1) * D:NT * D], 0.0)
                pool.memset(rowi, 0).then_inc(const_done, 1)
                pool.memset(ident[:, :], 0.0).then_inc(pool_step, 1)
                pool.memset(ones[:, :], 1.0)
                pool.iota(iota_w[:, :], pattern=[[1, W]], base=0, channel_multiplier=0,
                          allow_small_or_imprecise_dtypes=True)
                pool.wait_ge(pool_step, 1)
                pool.affine_select(out=ident[:, :], in_=ident[:, :], compare_op=ALU.not_equal, fill=1.0, base=0,
                                   pattern=[[-1, P]], channel_multiplier=1)
                tail = (ET - 1) * H
                pool.memset(el[:, tail:], 0.0).then_inc(const_done, 1)
                pool.wait_ge(const_done, 2)
                pool.wait_ge(tab_out, 32)
                pool.wait_ge(idx_done, 1)


                def gather_turn(i, first):
                    for s in range(2):
                        n = i * (2 * SG) + s * SG
                        if not first:
                            add_scores(i, s, n - 2 * SG)
                        for k, idx in enumerate((idx_l, idx_r)):
                            pool.tensor_copy(idx_ring[:, (2 * s + k) * SG:(2 * s + k + 1) * SG], idx[:, ds(n, SG)])\
                                .then_inc(idx_copied, 1)
                        pool.wait_ge(idx_copied, i * 4 + (2 * s + 2))
                        pool.nop(nofuse=True)
                        for k, table in enumerate((el_tab, er_tab)):
                            for j in range(SG):
                                c = (2 * s + k) * SG + j
                                pool.indirect_dma_start(score_ring[:, c * H:(c + 1) * H], None, table[:, :],
                                                        bass.IndirectOffsetOnAxis(ap=idx_ring[:, c:c + 1], axis=0))\
                                    .then_inc(gathered[s], 16)

                def add_scores(i, s, n):
                    pool.wait_ge(gathered[s], i * (32 * SG))
                    o = 2 * s * SG * H
                    pool.tensor_tensor(el[:, ds(n * H, SG * H)], score_ring[:, o:o + SG * H],
                                       score_ring[:, o + SG * H:o + 2 * SG * H], ALU.add).then_inc(scores_done, 1)

                turns = (ET - 1) // (2 * SG)
                gather_turn(0, True)
                with pool.Fori(1, turns) as i:
                    gather_turn(i, False)
                for s in range(2):
                    add_scores(turns, s, ET - 1 - 2 * SG + s * SG)
                pool.wait_ge(scores_done, 2 * turns)
                for k, (table, idx) in enumerate(((el_tab, idx_l), (er_tab, idx_r))):
                    pool.indirect_dma_start(score_ring[0:ELAST, k * H:(k + 1) * H], None, table[:, :],
                                            bass.IndirectOffsetOnAxis(ap=idx[0:ELAST, ET - 1:ET], axis=0))\
                        .then_inc(gathered[0], 16)
                pool.wait_ge(gathered[0], turns * (32 * SG) + 32)
                pool.tensor_tensor(el[0:ELAST, tail:tail + H], score_ring[0:ELAST, 0:H],
                                   score_ring[0:ELAST, H:2 * H], ALU.add).then_inc(scores_done, 1)

            @block.scalar
            def _(act):
                act.wait_ge(var_done, 1)
                act.activation(rstd[:, :], rstd[:, :], ACT.Sqrt).then_inc(std_done, 1)
                with act.Fori(0, NT // 2) as i:
                    for u in range(2):
                        act.wait_ge(xt_done, i * 2 + (u + 1))
                        act.activation(xT[:, u * D:(u + 1) * D], psum[4 + u][:, 0:D], ACT.Copy).then_inc(xt_copied, 1)
                    for u in range(2):
                        act.wait_ge(el_done, i * 2 + (u + 1))
                        act.activation(elr[:, ds(i * (4 * RH) + u * 2 * RH, 2 * RH)], psum[6 + u][:, 0:2 * RH],
                                       ACT.Copy).then_inc(el_copied, 1)

                def copy_xt(n, u):
                    act.wait_ge(xt_done2, n + 1)
                    act.activation(xT[:, u * D:(u + 1) * D], psum[6 + u][:, 0:D], ACT.Copy).then_inc(xt_copied2, 1)

                def turn(i, first, last):
                    for u in range(2):
                        if not first:
                            act.wait_ge(feat_out[u], i * 16)
                        for b in range(2):
                            act.wait_ge(feat_done, i * 8 + (4 * u + b + 1))
                            act.activation(fout[:, u * RHD + b * 512:u * RHD + (b + 1) * 512],
                                           psum[b][:, :], ACT.Copy).then_inc(feat_act, 1)
                        if not (last and u == 1):
                            copy_xt(i * 2 + (u + 1), (u + 1) % 2)

                copy_xt(0, 0)
                turn(0, True, False)
                with act.Fori(1, NT // 2 - 1) as i:
                    turn(i, False, False)
                turn(NT // 2 - 1, False, True)
                for b in range(4):
                    act.wait_ge(ebulk_psum, b + 1)
                    n = min(4, J - 4 * b) * P
                    act.activation(ebulk[:, b * 512:b * 512 + n], psum[b][:, 0:n], ACT.Copy).then_inc(ebulk_done, 1)
                act.wait_ge(shifted, 1)
                act.activation(bwd, ebulk, ACT.Exp).then_inc(exp_done, 1)

            @block.vector
            def _(dve):
                step = [0]

                def link(ins):
                    step[0] += 1
                    ins.then_inc(dve_step, 1)
                    dve.wait_ge(dve_step, step[0])

                dve.wait_ge(x_in, 32)
                with dve.Fori(0, NT - 1) as t:
                    dve.bn_stats(stats[:, ds(t * 6, 6)], x_sb[:, ds(t * D, D)])
                link(dve.bn_stats(stats[:, (NT - 1) * 6:], x_sb[:, (NT - 1) * D:]))
                for t in range(NT):
                    last = dve.bn_aggr(mv[:, t * 2:t * 2 + 2], stats[:, t * 6:t * 6 + 6])
                link(last)
                mvv = mv[:, :].rearrange("p (t two) -> p t two", two=2)
                dve.tensor_scalar(rstd[:, :], mvv[:, :, 1], EPS, None, ALU.add).then_inc(var_done, 1)
                dve.wait_ge(std_done, 1)
                link(dve.reciprocal(rstd[:, :], rstd[:, :]))
                dve.wait_ge(rows_in, 144)
                link(dve.tensor_copy(rowf, rowi))
                q = 4 * P
                dve.wait_ge(base_in, 32)
                link(dve.tensor_copy(base_f[:, :], base_i[:, :]))
                link(dve.scalar_tensor_tensor(rowx[:, 0:q], rowf[:, 0:q], float(R), rowf[:, 2 * q:3 * q],
                                              ALU.mult, ALU.add))
                dve.scalar_tensor_tensor(rowx[:, q:2 * q], rowf[:, q:2 * q], float(R), rowf[:, 2 * q:3 * q],
                                         ALU.mult, ALU.add).then_inc(rows_done, 1)
                dve.wait_ge(attn_in, 32)
                dve.wait_ge(w_in, 16 * R * KC)
                for k in range(KC):
                    for s, att in enumerate((att_l, att_r)):
                        link(dve.tensor_tensor(prod, wconv[:, k * RHD:(k + 1) * RHD], att, ALU.mult))
                        o = (k * 2 + s) * RH
                        link(dve.tensor_reduce(wa[:, o:o + RH], prod.rearrange("p (c d) -> p c d", d=HD), AX.X, ALU.add))

                def normalise(t, u, done):
                    dve.tensor_scalar(xn[:, u * D:(u + 1) * D], x_sb[:, ds(t * D, D)], mv[:, ds(t * 2, 1)],
                                      rstd[:, ds(t, 1)], ALU.subtract, ALU.mult).then_inc(done, 1)

                for u in range(2):
                    normalise(u, u, xn_done)
                with dve.Fori(1, NT // 2) as i:
                    for u in range(2):
                        dve.wait_ge(xt_done, i * 2 + (u - 1))
                        normalise(i * 2 + u, u, xn_done)
                dve.wait_ge(rowsT_done, 4)
                link(dve.tensor_copy(idx_l[:, :], psum[0][:, :]))
                dve.tensor_copy(idx_r[:, :], psum[1][:, :]).then_inc(idx_done, 1)
                link(dve.tensor_copy(dst_t[:, :], psum[2][:, :]))
                m = NG - 1
                dve.memset(rel[:, ET:], 0.0)
                link(dve.tensor_tensor(rel[:, 0:m * G].rearrange("p (g j) -> p g j", j=G),
                                       dst_t[:, 0:m * G].rearrange("p (g j) -> p g j", j=G),
                                       psum[3][:, 0:m].unsqueeze(2).to_broadcast([P, m, G]), ALU.subtract))
                dve.tensor_tensor(rel[:, m * G:ET], dst_t[:, m * G:ET], psum[3][:, m:NG], ALU.subtract)\
                   .then_inc(rel_done, 1)
                dve.wait_ge(xt_done, NT)
                for u in range(2):
                    normalise(u, u, xn_done2)

                def turn(i, first, last):
                    for u in range(2):
                        if not last:
                            dve.wait_ge(xt_done2, i * 2 + (u + 1))
                            normalise(i * 2 + (u + 2), u, xn_done2)
                        if not first:
                            dve.wait_ge(feat_out[u], i * 16)
                        for b in range(2, 4):
                            dve.wait_ge(feat_done, i * 8 + (4 * u + b + 1))
                            dve.tensor_copy(fout[:, u * RHD + b * 512:u * RHD + (b + 1) * 512],
                                            psum[b][:, :]).then_inc(feat_dve, 1)

                turn(0, True, False)
                with dve.Fori(1, NT // 2 - 1) as i:
                    turn(i, False, False)
                turn(NT // 2 - 1, False, True)
                dve.wait_ge(tab_out, 32)
                dve.wait_ge(xt_copied2, NT)
                dve.wait_ge(feat_act, 2 * NT)
                dve.memset(dsti, -1).then_inc(dstb_clear, 1)
                dve.wait_ge(dstb_in, 16 * 6 * H)
                link(dve.tensor_copy(dstf, dsti))
                link(dve.tensor_tensor(same[:, 0:L + 1], dstf[:, 0:L + 1], dstf[:, 1:L + 2], ALU.is_equal))
                link(dve.tensor_scalar(pen[:, 0:L + 1], same[:, 0:L + 1], -1.0, BIG, ALU.add, ALU.mult))
                dve.wait_ge(scores_done, (ET - 1) // SG + 1)
                ev = el[:, :].rearrange("p (t h) -> p h t", h=H)
                dve.scalar_tensor_tensor(e_ht.rearrange("p (h t) -> p h t", h=H), ev, 0.2, ev, ALU.mult, ALU.max)\
                   .then_inc(eht_done, 1)
                dve.wait_ge(ebulk_done, 4)

                def segment_scans(n, near, data, op0, op1, start, fo, bo):
                    nxt = near[:, 1:L + 1]
                    link(dve.tensor_tensor_scan(fo, near[:, 0:L], data, start, op0, op1))
                    link(dve.tensor_tensor_scan(bo[:, ::-1], nxt[:, ::-1], data[:, ::-1], start, op0, op1))
                    link(dve.tensor_copy(edge_col[:, 0:1], fo[:, L - 1:L]))
                    link(dve.tensor_reduce(edge_col[:, 1:2], near[:, 0:L], AX.X, ALU.min))
                    link(dve.tensor_copy(edge_col[:, 2:3], bo[:, 0:1]))
                    dve.tensor_reduce(edge_col[:, 3:4], nxt, AX.X, ALU.min).then_inc(cols_done, 1)
                    dve.wait_ge(rows_psum, n)
                    link(dve.tensor_copy(edge_row[:, :], psum[4][0:1, :]))
                    r = edge_row[:, :].rearrange("o (k p) -> o k p", p=P)
                    link(dve.memset(scan_row[:, :], start))
                    link(dve.tensor_tensor_scan(scan_row[:, 1:P + 1], r[:, 1, :], r[:, 0, :], start, op0, op1))
                    back = scan_row[:, P + 2:2 * P + 2]
                    dve.tensor_tensor_scan(back[:, ::-1], r[:, 3, ::-1], r[:, 2, ::-1], start, op0, op1)\
                       .then_inc(srow_done, 1)
                    dve.wait_ge(carry_psum, n)
                    link(dve.tensor_copy(carry[:, :], psum[5][:, 0:2]))
                    link(dve.tensor_tensor_scan(fo, near[:, 0:L], data, carry[:, 0:1], op0, op1))
                    link(dve.tensor_tensor_scan(bo[:, ::-1], nxt[:, ::-1], data[:, ::-1], carry[:, 1:2], op0, op1))

                segment_scans(1, pen, ebulk, ALU.add, ALU.max, -BIG, fwd, bwd)
                link(dve.tensor_tensor(fwd, fwd, bwd, ALU.max))
                dve.tensor_tensor(ebulk, ebulk, fwd, ALU.subtract).then_inc(shifted, 1)
                dve.wait_ge(exp_done, 1)
                segment_scans(2, same, bwd, ALU.mult, ALU.add, 0.0, fwd, ebulk)
                link(dve.tensor_tensor(fwd, fwd, ebulk, ALU.add))
                link(dve.tensor_tensor(fwd, fwd, bwd, ALU.subtract))
                link(dve.reciprocal(ebulk, fwd))
                dve.tensor_tensor(fwd, bwd, ebulk, ALU.mult).then_inc(alpha_bulk, 1)
                av = alpha[:, :].rearrange("p (c j h) -> p j h c", j=J, h=H)
                for j in range(J):
                    dve.wait_ge(alpha_psum, j // 4 + 1)
                    ap = psum[j // 4][:, (j % 4) * P:(j % 4 + 1) * P].rearrange("p (h c) -> p h c", h=H)
                    dve.tensor_copy(av[:, j], ap)

            @block.tensor
            def _(pe):
                pe.wait_ge(const_done, 2)
                pe.wait_ge(rows_done, 1)
                for k, s in enumerate((rowx[:, 0:512], rowx[:, 512:1024], rowf[:, 512:1024])):
                    for b in range(4):
                        last = pe.transpose(psum[k][:, b * P:(b + 1) * P], s[:, b * P:(b + 1) * P], ident[:, :])
                    last.then_inc(rowsT_done, 1)
                pe.matmul(psum[3][:, 0:NG], ones[0:1, :], base_f[0:1, :], start=True, stop=True).then_inc(rowsT_done, 1)

                def el_turn(i, first):
                    for u in range(2):
                        pe.wait_ge(xn_done, i * 2 + (u + 1))
                        if not first:
                            pe.wait_ge(xt_copied, i * 2 + (u - 1))
                        for k in range(KC):
                            last = pe.transpose(psum[4 + u][:, k * P:(k + 1) * P],
                                                xn[:, u * D + k * P:u * D + (k + 1) * P], ident[:, :])
                        last.then_inc(xt_done, 1)
                    for u in range(2):
                        pe.wait_ge(xt_copied, i * 2 + (u + 1))
                        if not first:
                            pe.wait_ge(el_copied, i * 2 + (u - 1))
                        for k in range(KC):
                            last = pe.matmul(psum[6 + u][:, 0:2 * RH], xT[:, u * D + k * P:u * D + (k + 1) * P],
                                             wa[:, k * 2 * RH:(k + 1) * 2 * RH], start=k == 0, stop=k == KC - 1)
                        last.then_inc(el_done, 1)

                el_turn(0, True)
                with pe.Fori(1, NT // 2) as i:
                    el_turn(i, False)

                def transposes(n, u, first):
                    pe.wait_ge(xn_done2, n + 1)
                    if not first:
                        pe.wait_ge(xt_copied2, n - 1)
                    for k in range(KC):
                        last = pe.transpose(psum[6 + u][:, k * P:(k + 1) * P],
                                            xn[:, u * D + k * P:u * D + (k + 1) * P], ident[:, :])
                    last.then_inc(xt_done2, 1)

                def turn(i, first, last_turn):
                    for u in range(2):
                        pe.wait_ge(xt_copied2, i * 2 + (u + 1))
                        for b in range(4):
                            if b == 2 and not (last_turn and u == 1):
                                transposes(i * 2 + (u + 1), (u + 1) % 2, first and u == 0)
                            if not (first and u == 0):
                                pe.wait_ge(feat_act if b < 2 else feat_dve, i * 4 + (2 * u + b % 2 - 1))
                            for k in range(KC):
                                o = k * RHD + b * 512
                                last = pe.matmul(psum[b][:, :], xT[:, u * D + k * P:u * D + (k + 1) * P],
                                                 wconv[:, o:o + 512], start=k == 0, stop=k == KC - 1)
                            last.then_inc(feat_done, 1)

                pe.wait_ge(idx_done, 1)
                pe.wait_ge(rel_done, 1)
                pe.wait_ge(el_copied, NT)
                transposes(0, 0, True)
                turn(0, True, False)
                with pe.Fori(1, NT // 2 - 1) as i:
                    turn(i, False, False)
                turn(NT // 2 - 1, False, True)
                pe.wait_ge(feat_act, 2 * NT)
                pe.wait_ge(feat_dve, 2 * NT)
                pe.wait_ge(eht_done, 1)
                for j in range(J):
                    last = pe.transpose(psum[j // 4][:, (j % 4) * P:(j % 4 + 1) * P], e_ht[:, j::J], ident[:, :])
                    if j % 4 == 3 or j == J - 1:
                        last.then_inc(ebulk_psum, 1)
                for n in (1, 2):
                    pe.wait_ge(cols_done, n)
                    for k in range(4):
                        last = pe.transpose(psum[4][0:1, k * P:(k + 1) * P], edge_col[:, k:k + 1], ident[:, :])
                    last.then_inc(rows_psum, 1)
                    pe.wait_ge(srow_done, n)
                    pe.matmul(psum[5][:, 0:1], scan_row[0:1, 0:P], ones[0:1, 0:1], start=True, stop=True)
                    pe.matmul(psum[5][:, 1:2], scan_row[0:1, P + 3:2 * P + 3], ones[0:1, 0:1], start=True, stop=True)\
                      .then_inc(carry_psum, 1)
                pe.wait_ge(alpha_bulk, 1)
                pe.wait_ge(ebulk_done, 4)
                for j in range(J):
                    last = pe.transpose(psum[j // 4][:, (j % 4) * P:(j % 4 + 1) * P], fwd[:, j * P:(j + 1) * P], ident[:, :])
                    if j % 4 == 3 or j == J - 1:
                        last.then_inc(alpha_psum, 1)

        feats, o = carve(0, RING * D)
        hot, o = carve(o, 2 * G * W)
        hot_a, o = carve(o, GPI * G * H * W)
        WIN = 480
        iota_n, o = carve(o, WIN)
        hot_n, o = carve(o, 2 * WIN)
        far_a, o = carve(o, H)
        far_d, o = carve(o, NP_ // WIN)
        assert o <= WORK and NP_ % WIN == 0
        w1_sb = weights[:, 0:X * KC * D]
        w2_sb = weights[:, X * KC * D:2 * X * KC * D]
        far_col = sb("far_col", [P, 1])
        far_row = sb("far_row", [1, 1])
        far_i = sb("far_i", [1, 1], I32)

        acc_clear = sem("acc_clear")
        experts_in = sem("experts_in")
        feats_in = [sem(f"feats_in{k}") for k in range(RING)]
        feat_idx = sem("feat_idx")
        hot_done = sem("hot_done")
        hot_a_done = sem("hot_a_done")
        agg_done = sem("agg_done")
        acc_step = sem("acc_step")
        far_step = sem("far_step")
        far_psum = sem("far_psum")
        iota_n_done = sem("iota_n_done")
        accv = acc[:, :].rearrange("p (k n) -> p k n", k=KC)

        with nc.Block() as block:
            @block.sync
            def _(sp):
                for e in range(X):
                    for w, to in ((w1, w1_sb), (w2, w2_sb)):
                        o = e * KC * D
                        sp.dma_start(to[:, o:o + KC * D].rearrange("p (k f) -> p k f", k=KC),
                                     w[e].rearrange("(k p) f -> p k f", p=P)).then_inc(experts_in, 16)
                sp.wait_ge(experts_in, 32 * X)

            @block.gpsimd
            def _(pool):
                def gather_turn(i):
                    for k in range(RING):
                        if k % G == 0:
                            pool.wait_ge(feat_idx, i * GPI + (k // G + 1))
                            pool.nop(nofuse=True)
                        pool.indirect_dma_start(feats[:, k * D:(k + 1) * D], None, feat_tab[:, :],
                                                bass.IndirectOffsetOnAxis(ap=idx_ring[:, k:k + 1], axis=0))\
                            .then_inc(feats_in[k], 16)

                with pool.Fori(0, TURNS) as i:
                    gather_turn(i)
                pool.wait_ge(agg_done, (TURNS - 1) * GPI + 1)
                pool.indirect_dma_start(feats[0:ELAST, 0:D], None, feat_tab[:, :],
                                        bass.IndirectOffsetOnAxis(ap=idx_l[0:ELAST, ET - 1:ET], axis=0))\
                    .then_inc(feats_in[0], 16)
                pool.iota(iota_n, pattern=[[1, WIN]], base=0, channel_multiplier=0,
                          allow_small_or_imprecise_dtypes=True).then_inc(iota_n_done, 1)

            @block.scalar
            def _(act):
                def indices(i, first):
                    for s in range(GPI):
                        if not first:
                            act.wait_ge(agg_done, i * GPI + (s + 1 - GPI))
                        act.activation(idx_ring[:, s * G:(s + 1) * G], idx_l[:, ds(i * RING + s * G, G)], ACT.Copy)\
                           .then_inc(feat_idx, 1)
                indices(0, True)
                with act.Fori(1, TURNS) as i:
                    indices(i, False)

            @block.vector
            def _(dve):
                dve.memset(acc[:, :], 0.0).then_inc(acc_clear, 1)
                dve.tensor_reduce(far_col[:, :], rel[:, 0:ET], AX.X, ALU.max).then_inc(far_step, 1)
                dve.wait_ge(acc_clear, 1)

                def build(g, s):
                    o = (s % 2) * G * W
                    hv = hot[:, o:o + G * W].rearrange("p (j w) -> p j w", j=G)
                    dve.tensor_tensor(hv, iota_w[:, :].unsqueeze(1).to_broadcast([P, G, W]),
                                      rel[:, ds(g * G, G)].unsqueeze(2).to_broadcast([P, G, W]), ALU.is_equal)\
                       .then_inc(hot_done, 1)
                    dve.wait_ge(hot_done, g + 1)
                    o = s * G * H * W
                    dve.tensor_tensor(hot_a[:, o:o + G * H * W].rearrange("p (j h w) -> p j h w", j=G, h=H),
                                      hv.unsqueeze(2).to_broadcast([P, G, H, W]),
                                      alpha[:, ds(g * (G * H), G * H)].rearrange("p (j h) -> p j h", h=H).unsqueeze(3)
                                      .to_broadcast([P, G, H, W]), ALU.mult).then_inc(hot_a_done, 1)

                def add_window(g, s):
                    base = dve.value_load(base_i[0:1, ds(g, 1)], min_val=0, max_val=N - 1)
                    dve.wait_ge(agg_done, g + 1)
                    dve.wait_ge(acc_step, g * 2)
                    pv = psum[s % 2][:, 0:2 * KC * W].rearrange("p (k h w) -> p k h w", k=KC, h=2)
                    for half in range(2):
                        q = slice(half * HD, half * HD + HD)
                        dve.tensor_tensor(accv[q, :, ds(base, W)], accv[q, :, ds(base, W)], pv[q, :, half, :], ALU.add)\
                           .then_inc(acc_step, 1)

                build(0, 0)

                def turn(i, first):
                    for s in range(GPI):
                        if not (first and s < GPI - 1):
                            dve.wait_ge(agg_done, i * GPI + (s + 2 - GPI))
                        build(i * GPI + (s + 1), (s + 1) % GPI)
                        add_window(i * GPI + s, s)

                turn(0, True)
                with dve.Fori(1, TURNS) as i:
                    turn(i, False)
                add_window(NG - 1, 0)
                dve.wait_ge(far_psum, 1)
                dve.tensor_reduce(far_row[:, :], psum[2][0:1, 0:P], AX.X, ALU.max).then_inc(far_step, 1)
                dve.wait_ge(far_step, 2)
                dve.tensor_scalar(far_i[:, :], far_row[:, :], float(W), None, ALU.is_ge).then_inc(far_step, 1)
                dve.wait_ge(far_step, 3)
                dve.wait_ge(acc_step, 2 * NG)

            @block.tensor
            def _(pe):
                def sum_window(g, s, i, first, tiles=G, rows=P):
                    pe.wait_ge(hot_a_done, g + 1)
                    for j in range(tiles):
                        pe.wait_ge(feats_in[s * G + j], i * 16 + 16)
                    if not (first and s < 2):
                        pe.wait_ge(acc_step, g * 2 - 2)
                    for q in range(KC):
                        for j in range(tiles):
                            k = s * G + j
                            o = (k * H + 2 * q) * W
                            last = pe.matmul(psum[s % 2][:, q * 2 * W:(q + 1) * 2 * W],
                                             feats[0:rows, k * D + q * P:k * D + (q + 1) * P],
                                             hot_a[0:rows, o:o + 2 * W], start=j == 0, stop=j == tiles - 1)
                    last.then_inc(agg_done, 1)

                for s in range(GPI):
                    sum_window(s, s, 0, True)
                with pe.Fori(1, TURNS) as i:
                    for s in range(GPI):
                        sum_window(i * GPI + s, s, i, False)
                sum_window(NG - 1, 0, TURNS, False, 1, ELAST)
                pe.wait_ge(far_step, 1)
                pe.transpose(psum[2][0:1, 0:P], far_col[:, :], ident[:, :]).then_inc(far_psum, 1)

        far_in = sem("far_in")
        far_idx = sem("far_idx")
        far_mask = sem("far_mask")
        far_hot = sem("far_hot")
        far_sum = sem("far_sum")
        far_add = sem("far_add")
        NW = NP_ // WIN
        with nc.Block() as block:
            def beyond(eng):
                return eng.value_load(far_i[0:1, 0:1], min_val=0, max_val=1)

            @block.scalar
            def _(act):
                with act.If(beyond(act) == 1):
                    with act.Fori(0, ET) as t:
                        act.wait_ge(far_sum, t * (NW * H) + 1)
                        act.activation(idx_ring[:, 0:1], idx_l[:, ds(t, 1)], ACT.Copy).then_inc(far_idx, 1)

            @block.gpsimd
            def _(pool):
                with pool.If(beyond(pool) == 1):
                    with pool.Fori(0, ET) as t:
                        pool.wait_ge(far_idx, t + 1)
                        pool.nop(nofuse=True)
                        pool.indirect_dma_start(feats[:, 0:D], None, feat_tab[:, :],
                                                bass.IndirectOffsetOnAxis(ap=idx_ring[:, 0:1], axis=0))\
                            .then_inc(far_in, 16)

            @block.vector
            def _(dve):
                with dve.If(beyond(dve) == 1):
                    with dve.Fori(0, ET) as t:
                        dve.wait_ge(far_sum, t * (NW * H) + 1)
                        dve.tensor_scalar(far_d[:, 0:1], rel[:, ds(t, 1)], float(W), None, ALU.is_ge).then_inc(far_mask, 1)
                        dve.wait_ge(far_mask, t * (NW + 2) + 1)
                        dve.tensor_scalar(far_a, alpha[:, ds(t * H, H)], far_d[:, 0:1], None, ALU.mult)\
                           .then_inc(far_mask, 1)
                        dve.wait_ge(far_mask, t * (NW + 2) + 2)
                        for w in range(NW):
                            dve.tensor_scalar(far_d[:, w:w + 1], dst_t[:, ds(t, 1)], float(-w * WIN), None, ALU.add)\
                               .then_inc(far_mask, 1)
                        dve.wait_ge(far_mask, t * (NW + 2) + (NW + 2))
                        for w in range(NW):
                            for h in range(H):
                                n = w * H + h
                                b = n % 2
                                if n >= 2:
                                    dve.wait_ge(far_sum, t * (NW * H) + n)
                                dve.tensor_scalar(hot_n[:, b * WIN:(b + 1) * WIN], iota_n, far_d[:, w:w + 1],
                                                  far_a[:, h:h + 1], ALU.is_equal, ALU.mult).then_inc(far_hot, 1)
                                dve.wait_ge(far_sum, t * (NW * H) + (n + 2))
                                q = slice((h % 2) * HD, (h % 2 + 1) * HD)
                                to = accv[q, h // 2, w * WIN:(w + 1) * WIN]
                                dve.wait_ge(far_add, t * (NW * H) + (n + 1))
                                dve.tensor_tensor(to, to, psum[b][q, 0:WIN], ALU.add).then_inc(far_add, 1)

            @block.tensor
            def _(pe):
                with pe.If(beyond(pe) == 1):
                    pe.transpose(psum[2][0:1, 0:P], far_col[:, :], ident[:, :]).then_inc(far_sum, 1)
                    pe.transpose(psum[2][0:1, 0:P], far_col[:, :], ident[:, :]).then_inc(far_add, 1)
                    with pe.Fori(0, ET) as t:
                        pe.wait_ge(far_in, t * 16 + 16)
                        for w in range(NW):
                            for h in range(H):
                                n = w * H + h
                                b = n % 2
                                pe.wait_ge(far_hot, t * (NW * H) + (n + 1))
                                pe.wait_ge(far_add, t * (NW * H) + (n if n else 1))
                                o = (h // 2) * P
                                pe.matmul(psum[b][:, 0:WIN], feats[:, o:o + P], hot_n[:, b * WIN:(b + 1) * WIN],
                                          start=True, stop=True).then_inc(far_sum, 1)

        xlT, o = carve(0, KC * NP_)
        hs, o = carve(o, KC * 2 * P)
        x2, o = carve(o, 2 * D)
        xl, o = carve(o, 2 * D)
        hT, o = carve(o, 4 * TOK)
        rowsT, o = carve(o, NP_)
        assert o <= WORK
        mv2 = sb("mv2", [P, 4])
        st2 = sb("st2", [P, 12])
        rs2 = sb("rs2", [P, 2])
        probs = el[:, 0:NT * X]
        top = el[:, NT * X:2 * NT * X]
        comb = el[:, 2 * NT * X:3 * NT * X]
        comb2 = el[:, 3 * NT * X:4 * NT * X]
        expo = el[:, 4 * NT * X:5 * NT * X]
        top_i = er[:, 0:NT * X].bitcast(U32)
        top_f = er[:, NT * X:2 * NT * X]
        mx = er[:, 2 * NT * X:2 * NT * X + NT]
        sm = er[:, 3 * NT * X:3 * NT * X + NT]
        wt = er[:, 4 * NT * X:4 * NT * X + 2 * NT]
        xlTv = xlT.rearrange("p (k n) -> p k n", k=KC)

        prep_step = sem("prep_step")
        hs_done = sem("hs_done")
        x2_psum = sem("x2_psum")
        x2_done = sem("x2_done")
        stats_done = sem("stats_done")
        mv_done = sem("mv_done")
        rs_done = sem("rs_done")
        var2_done = sem("var2_done")
        std2_done = sem("std2_done")
        xl_done = sem("xl_done")
        base_done = sem("base_done")
        xlT_psum = sem("xlT_psum")
        xlT_done = sem("xlT_done")
        rwT_psum = sem("rwT_psum")
        rwT_done = sem("rwT_done")
        score_psum = sem("score_psum")
        score_done = sem("score_done")
        scoreT = sem("scoreT")
        score_shift = sem("score_shift")
        score_exp = sem("score_exp")
        comb_done = sem("comb_done")
        combT_psum = sem("combT_psum")
        combT_done = sem("combT_done")
        b2_psum = sem("b2_psum")
        b2_done = sem("b2_done")
        h_psum = sem("h_psum")
        h_done = sem("h_done")
        y_psum = sem("y_psum")
        y_done = sem("y_done")
        out_done = sem("out_done")
        PT = NT // 2
        SC = NP_ // WIN

        with nc.Block() as block:
            @block.sync
            def _(sp):
                def store(c, sems):
                    sp.wait_ge(y_done, c * (X * TC) + X * TC)
                    sp.dma_start(out[ds(c * TOK, TOK), :].rearrange("(t p) d -> p t d", p=P),
                                 x_sb[:, ds(c * (TC * D), TC * D)].rearrange("p (t d) -> p t d", d=D)).then_inc(sems, 16)
                with sp.Fori(0, NC - 1) as c:
                    store(c, out_done)
                sp.wait_ge(y_done, NC * X * TC)
                n = (NC - 1) * TC
                sp.dma_start(out[n * P:(NT - 1) * P, :].rearrange("(t p) d -> p t d", p=P),
                             x_sb[:, n * D:(NT - 1) * D].rearrange("p (t d) -> p t d", d=D)).then_inc(out_done, 16)
                sp.dma_start(out[(NT - 1) * P:N, :], x_sb[0:NLAST, (NT - 1) * D:NT * D]).then_inc(out_done, 16)
                sp.wait_ge(out_done, 16 * (NC + 1))

            @block.scalar
            def _(act):
                def copy_h(i, first):
                    if not first:
                        act.wait_ge(x2_psum, i)
                    for k in range(KC):
                        act.activation(hs[:, k * 2 * P:(k + 1) * 2 * P], acc[:, ds(i * (2 * P) + k * NP_, 2 * P)],
                                       ACT.Identity, bias=hb[:, k:k + 1]).then_inc(hs_done, 1)

                def copy_xlT(i):
                    act.wait_ge(xlT_psum, i + 1)
                    act.activation(xlTv[:, :, ds(i * (2 * P), 2 * P)],
                                   psum[1][:, :].rearrange("p (k n) -> p k n", k=KC), ACT.Copy).then_inc(xlT_done, 1)

                def std(i):
                    act.wait_ge(var2_done, i + 1)
                    act.activation(rs2[:, :], rs2[:, :], ACT.Sqrt).then_inc(std2_done, 1)

                copy_h(0, True)
                with act.Fori(0, PT - 1) as i:
                    copy_h(i + 1, False)
                    std(i)
                    copy_xlT(i)
                std(PT - 1)
                copy_xlT(PT - 1)
                act.wait_ge(rwT_psum, 1)
                act.activation(rwT[:, :], psum[2][:, 0:KC * X], ACT.Copy).then_inc(rwT_done, 1)
                for c in range(SC):
                    act.wait_ge(score_psum, c + 1)
                    act.activation(rowsT[0:X, c * WIN:(c + 1) * WIN], psum[4 + c % 2][0:X, 0:WIN], ACT.Copy)\
                       .then_inc(score_done, 1)
                act.wait_ge(score_shift, 1)
                act.activation(expo, expo, ACT.Exp).then_inc(score_exp, 1)
                for b in range(8):
                    act.wait_ge(combT_psum, b + 1)
                    n = min(4, NT - 4 * b) * P
                    act.activation(rowsT[0:X, b * 512:b * 512 + n], psum[b][0:X, 0:n], ACT.Copy).then_inc(combT_done, 1)

                def chunk(c, first):
                    for e in range(X):
                        for f in range(KC):
                            act.wait_ge(h_psum, c * (2 * X) + (2 * e + f + 1))
                            if not (first and e < 2):
                                act.wait_ge(y_psum, c * (TC * X) + TC * (e - 1))
                            o = (e % 2 * 2 + f) * TOK
                            act.activation(hT[:, o:o + TOK], psum[e % 2 * 2 + f][:, 0:TOK], ACT.Gelu,
                                           bias=b1_sb[:, e * KC + f:e * KC + f + 1]).then_inc(h_done, 1)
                chunk(0, True)
                with act.Fori(1, NC) as c:
                    chunk(c, False)

            @block.vector
            def _(dve):
                step = [0]

                def link(ins):
                    step[0] += 1
                    ins.then_inc(prep_step, 1)
                    dve.wait_ge(prep_step, step[0])

                def pair(i, first):
                    dve.wait_ge(x2_psum, i + 1)
                    if not first:
                        dve.wait_ge(base_done, i)
                    dve.tensor_tensor(x2, psum[0][:, :], x_sb[:, ds(i * (2 * D), 2 * D)], ALU.add).then_inc(x2_done, 1)
                    dve.wait_ge(x2_done, i + 1)
                    for j in range(2):
                        dve.bn_stats(st2[:, 6 * j:6 * j + 6], x2[:, j * D:(j + 1) * D]).then_inc(stats_done, 1)
                    for j in range(2):
                        dve.wait_ge(stats_done, i * 2 + (j + 1))
                        dve.nop(nofuse=True)
                        dve.bn_aggr(mv2[:, 2 * j:2 * j + 2], st2[:, 6 * j:6 * j + 6]).then_inc(mv_done, 1)
                    dve.wait_ge(mv_done, i * 2 + 2)
                    dve.tensor_scalar(rs2[:, :], mv2[:, 1:4:2], EPS, None, ALU.add).then_inc(var2_done, 1)
                    dve.wait_ge(std2_done, i + 1)
                    dve.reciprocal(rs2[:, :], rs2[:, :]).then_inc(rs_done, 1)
                    dve.wait_ge(rs_done, i + 1)
                    if not first:
                        dve.wait_ge(xlT_psum, i)
                    for j in range(2):
                        dve.tensor_scalar(xl[:, j * D:(j + 1) * D], x2[:, j * D:(j + 1) * D], mv2[:, 2 * j:2 * j + 1],
                                          rs2[:, j:j + 1], ALU.subtract, ALU.mult).then_inc(xl_done, 1)
                    dve.wait_ge(xl_done, i * 2 + 2)
                    dve.tensor_tensor(x_sb[:, ds(i * (2 * D), 2 * D)], x2, xl, ALU.add).then_inc(base_done, 1)
                pair(0, True)
                with dve.Fori(1, PT) as i:
                    pair(i, False)
                dve.wait_ge(scoreT, 1)

                def v(a):
                    return a.rearrange("p (t e) -> p t e", e=X)

                def wide(a):
                    return a.unsqueeze(2).to_broadcast([P, NT, X])

                sc = v(psum[6][:, 0:NT * X])
                link(dve.tensor_reduce(mx, sc, AX.X, ALU.max))
                dve.tensor_tensor(v(expo), sc, wide(mx), ALU.subtract).then_inc(score_shift, 1)
                dve.wait_ge(score_exp, 1)
                link(dve.tensor_reduce(sm, v(expo), AX.X, ALU.add))
                link(dve.reciprocal(sm, sm))
                link(dve.tensor_tensor(v(probs), v(expo), wide(sm), ALU.mult))
                for t in range(NT):
                    last = dve.max(top[:, t * X:(t + 1) * X], probs[:, t * X:(t + 1) * X])
                    if t == NT - 1:
                        link(last)
                for t in range(NT):
                    last = dve.max_index(top_i[:, t * X:(t + 1) * X], top[:, t * X:(t + 1) * X],
                                         probs[:, t * X:(t + 1) * X])
                    if t == NT - 1:
                        link(last)
                link(dve.tensor_copy(top_f, top_i))
                tv, iv = v(top), v(top_f)
                link(dve.tensor_tensor(mx, tv[:, :, 0], tv[:, :, 1], ALU.add))
                link(dve.tensor_scalar(mx, mx, 1e-12, None, ALU.max))
                link(dve.reciprocal(mx, mx))
                for k, c in enumerate((comb, comb2)):
                    w = wt[:, k * NT:(k + 1) * NT]
                    link(dve.tensor_tensor(w, tv[:, :, k], mx, ALU.mult))
                    link(dve.tensor_tensor(v(c), iota_w[:, 0:X].unsqueeze(1).to_broadcast([P, NT, X]),
                                           wide(iv[:, :, k]), ALU.is_equal))
                    link(dve.tensor_tensor(v(c), v(c), wide(w), ALU.mult))
                dve.tensor_tensor(comb, comb, comb2, ALU.add).then_inc(comb_done, 1)
                for i in range(PT):
                    dve.wait_ge(b2_psum, i + 1)
                    dve.tensor_tensor(x_sb[:, i * 2 * D:(i + 1) * 2 * D], psum[i % 4][:, :],
                                      x_sb[:, i * 2 * D:(i + 1) * 2 * D], ALU.add).then_inc(b2_done, 1)
                dve.wait_ge(b2_done, PT)

                def chunk(c, first):
                    for e in range(X):
                        for j in range(TC):
                            dve.wait_ge(y_psum, c * (TC * X) + (TC * e + j + 1))
                            if not (first and e == 0):
                                dve.wait_ge(y_done, c * (TC * X) + (TC * (e - 1) + j + 1))
                            to = x_sb[:, ds(c * (TC * D) + j * D, D)]
                            dve.scalar_tensor_tensor(to, psum[4 + j][:, 0:D], comb[:, ds(c * (TC * X) + (j * X + e), 1)],
                                                     to, ALU.mult, ALU.add).then_inc(y_done, 1)
                chunk(0, True)
                with dve.Fori(1, NC) as c:
                    chunk(c, False)

            @block.tensor
            def _(pe):
                def transpose_h(i, first):
                    pe.wait_ge(hs_done, i * 2 + 2)
                    if not first:
                        pe.wait_ge(x2_done, i)
                    for j in range(2):
                        for k in range(KC):
                            last = pe.transpose(psum[0][:, j * D + k * P:j * D + (k + 1) * P],
                                                hs[:, k * 2 * P + j * P:k * 2 * P + (j + 1) * P], ident[:, :])
                    last.then_inc(x2_psum, 1)

                def transpose_xl(i, first):
                    pe.wait_ge(xl_done, i * 2 + 2)
                    if not first:
                        pe.wait_ge(xlT_done, i)
                    for j in range(2):
                        for k in range(KC):
                            last = pe.transpose(psum[1][:, k * 2 * P + j * P:k * 2 * P + (j + 1) * P],
                                                xl[:, j * D + k * P:j * D + (k + 1) * P], ident[:, :])
                    last.then_inc(xlT_psum, 1)

                transpose_h(0, True)
                transpose_h(1, False)
                transpose_xl(0, True)
                with pe.Fori(1, PT - 1) as i:
                    transpose_h(i + 1, False)
                    transpose_xl(i, False)
                transpose_xl(PT - 1, False)
                for k in range(KC):
                    last = pe.transpose(psum[2][:, k * X:(k + 1) * X], rw_sb[:, k * P:(k + 1) * P], ident[0:X, 0:X])
                last.then_inc(rwT_psum, 1)
                pe.wait_ge(rwT_done, 1)
                pe.wait_ge(xlT_done, PT)
                for c in range(SC):
                    if c >= 2:
                        pe.wait_ge(score_done, c - 1)
                    for k in range(KC):
                        last = pe.matmul(psum[4 + c % 2][0:X, 0:WIN], rwT[:, k * X:(k + 1) * X],
                                         xlTv[:, k, c * WIN:(c + 1) * WIN], start=k == 0, stop=k == KC - 1)
                    last.then_inc(score_psum, 1)
                pe.wait_ge(score_done, SC)
                for t in range(NT):
                    last = pe.transpose(psum[6][:, t * X:(t + 1) * X], rowsT[0:X, t * P:(t + 1) * P], ident[0:X, 0:X])
                last.then_inc(scoreT, 1)
                pe.wait_ge(comb_done, 1)
                for t in range(NT):
                    last = pe.transpose(psum[t // 4][0:X, (t % 4) * P:(t % 4 + 1) * P], comb[:, t * X:(t + 1) * X],
                                        ident[:, :])
                    if t % 4 == 3 or t == NT - 1:
                        last.then_inc(combT_psum, 1)
                pe.wait_ge(combT_done, 8)
                for i in range(PT):
                    if i >= 4:
                        pe.wait_ge(b2_done, i - 3)
                    for j in range(2):
                        t = 2 * i + j
                        last = pe.matmul(psum[i % 4][:, j * D:(j + 1) * D], rowsT[0:X, t * P:(t + 1) * P], b2_sb[:, :],
                                         start=True, stop=True)
                    last.then_inc(b2_psum, 1)
                pe.wait_ge(b2_done, PT)

                def up(c, e, first):
                    for f in range(KC):
                        if not (first and e < 2):
                            pe.wait_ge(h_done, c * (2 * X) + (2 * e + f - 3))
                        for k in range(KC):
                            o = (e % X * KC + k) * D + f * P
                            last = pe.matmul(psum[e % 2 * 2 + f][:, 0:TOK], w1_sb[:, o:o + P],
                                             xlT[:, ds(c * TOK + (e // X * TOK + k * NP_), TOK)],
                                             start=k == 0, stop=k == KC - 1)
                        last.then_inc(h_psum, 1)

                def down(c, e, first):
                    pe.wait_ge(h_done, c * (2 * X) + (2 * e + 2))
                    for j in range(TC):
                        if not (first and e == 0):
                            pe.wait_ge(y_done, c * (TC * X) + (TC * (e - 1) + j + 1))
                        for f in range(KC):
                            o = (e % 2 * 2 + f) * TOK + j * P
                            last = pe.matmul(psum[4 + j][:, 0:D], hT[:, o:o + P],
                                             w2_sb[:, (e * KC + f) * D:(e * KC + f + 1) * D],
                                             start=f == 0, stop=f == KC - 1)
                        last.then_inc(y_psum, 1)

                def chunk(c, first, last):
                    for e in range(X):
                        if not (last and e == X - 1):
                            up(c, e + 1, first)
                        down(c, e, first)

                up(0, 0, True)
                chunk(0, True, False)
                with pe.Fori(1, NC - 1) as c:
                    chunk(c, False, False)
                chunk(NC - 1, False, True)

_INS = ["x", "src", "dst", "edge_type_8", "L0_gnn_conv_weights", "L0_gnn_attn_l", "L0_gnn_attn_r", "L0_gnn_h_bias",
        "L0_ffn_router_w", "L0_ffn_w1", "L0_ffn_b1", "L0_ffn_w2", "L0_ffn_b2"]


def kernel(**inputs):
    import numpy as _np
    import concourse.bacc as _bacc
    from concourse import mybir as _mybir
    from concourse.bass_utils import run_bass_kernel_spmd as _run

    nc = _bacc.Bacc("TRN2", target_bir_lowering=False, num_devices=1)
    arrays, args = {}, []
    for name in _INS:
        a = _np.ascontiguousarray(inputs[name])
        arrays[f"in_{name}_dram"] = a
        args.append(nc.dram_tensor(f"in_{name}_dram", a.shape, _mybir.dt.from_np(a.dtype), kind="ExternalInput").ap())
    args.append(nc.dram_tensor("out_0_dram", (N, D), _mybir.dt.float32, kind="ExternalOutput").ap())
    gnn_moe(nc, *args)
    r = _run(nc, [arrays], core_ids=[0])
    return r.results[0]["out_0_dram"]
```

```python
import concourse.bass as bass
from concourse import mybir
from contextlib import ExitStack

F32 = mybir.dt.float32
I32 = mybir.dt.int32
U32 = mybir.dt.uint32
ALU = mybir.AluOpType
ACT = mybir.ActivationFunctionType
AX = mybir.AxisListType

P = 128
N, D = 3750, 256
NT = (N + P - 1) // P
NP_ = NT * P
NLAST = N - (NT - 1) * P
E = 60000
R, H, HD = 8, 4, 64
RH, RHD = R * H, R * H * HD
KC = D // P
ET = (E + P - 1) // P
ELAST = E - (ET - 1) * P
C, J = 32, 15
ETP = C * J
L = J * P
G = 3
W = 32
NG = (ET + G - 1) // G
GPI = 4
RING = GPI * G
TURNS2 = ETP // RING
HOTS = 4
ST = 16
NS = (NG + ST - 1) // ST
LAG = 4
FR = ST * G
EARLY = 32
EPS = 1e-5
BIG = 1e30
X = 8
TC = 3
NC = NT // TC
TOK = TC * P
SG = 6
WORK = 18640


def gnn_moe(nc, x, src, dst, etype, conv_w, attn_l, attn_r, h_bias, router_w, w1, b1, w2, b2, out):
    assert TURNS2 % 2 == 0 and GPI * W == P and (ET - 1) % G == 0 and NT % 6 == 0 and ETP >= ET
    ctx = ExitStack()
    with ctx:
        ctx.enter_context(nc.allow_non_contiguous_dma(reason="a few hundred window bases and small weights"))

        def sb(name, shape, dt=F32):
            return ctx.enter_context(nc.sbuf_tensor(name, shape, dt))

        def sem(name):
            return ctx.enter_context(nc.semaphore(name))

        ds = bass.ds
        feat_tab = nc.dram_tensor("feat_tab", [NP_ * R, D], F32)
        el_tab = nc.dram_tensor("el_tab", [NP_ * R, H], F32)
        er_tab = nc.dram_tensor("er_tab", [NP_ * R, H], F32)

        ident = sb("ident", [P, P])
        ones = sb("ones", [P, P])
        x_sb = sb("x_sb", [P, NT * D])
        acc = sb("acc", [P, KC * NP_])
        weights = sb("weights", [P, KC * RHD + 2 * RHD])
        work = sb("work", [P, WORK])
        alpha = sb("alpha", [P, ETP * H])
        feat_rows = sb("feat_rows", [P, FR], I32)
        el = sb("el", [P, ETP * H])
        er = sb("er", [P, ETP * H])
        far_col = sb("far_col", [P, 1])
        far_row = sb("far_row", [1, NS])
        far_i = sb("far_i", [1, 1], I32)
        score_ring = sb("score_ring", [P, 4 * SG * H])
        idx_l = sb("idx_l", [P, 4 * P], I32)
        idx_r = sb("idx_r", [P, 4 * P], I32)
        idx_ring = sb("idx_ring", [P, 4 * SG], I32)
        dst_t = sb("dst_t", [P, 4 * P])
        rel = sb("rel", [P, ETP])
        base_i = sb("base_i", [1, TURNS2 * GPI], I32)
        base_f = sb("base_f", [1, NG])
        stats = sb("stats", [P, NT * 6])
        mv = sb("mv", [P, NT * 2])
        rstd = sb("rstd", [P, NT])
        iota_w = sb("iota_w", [P, W])
        hb = sb("hb", [P, KC])
        b1_sb = sb("b1_sb", [P, X * KC])
        b2_sb = sb("b2_sb", [X, D])
        rw_sb = sb("rw_sb", [X, D])
        rwT = sb("rwT", [P, KC * X])

        psum = [ctx.enter_context(nc.psum_tensor(f"bank{i}", [P, 512], F32)) for i in range(8)]

        def carve(start, n):
            return work[:, start:start + n], start + n

        late_feats, _ = carve(WORK - (FR - EARLY) * D, (FR - EARLY) * D)

        wconv = weights[:, 0:KC * RHD]
        fout = weights[:, KC * RHD:KC * RHD + 2 * RHD]
        att_l, o = carve(0, RHD)
        att_r, o = carve(o, RHD)
        prod, o = carve(o, RHD)
        wa, o = carve(o, KC * 2 * RH)
        rowi_f, o = carve(o, 3 * 4 * P)
        rowi = rowi_f.bitcast(I32)
        rowf, o = carve(o, 3 * 4 * P)
        rowx, o = carve(o, 2 * 4 * P)
        xn, o = carve(o, 2 * D)
        xT, o = carve(o, 2 * D)
        elr, o = carve(o, NT * 2 * RH)
        hot_e, o = carve(o, 2 * G * P)
        hotT, o = carve(o, 2 * G * P)
        er_win, o = carve(o, 2 * P)
        rel_mask, o = carve(o, RING * R)
        er_all, o = carve(o, RING * RH)
        typ, o = carve(o, 4 * P)
        assert o <= WORK, o
        dsti_f, o = carve(0, L + 2)
        dsti = dsti_f.bitcast(I32)
        dstf, o = carve(o, L + 2)
        same, o = carve(o, L + 2)
        pen, o = carve(o, L + 2)
        ebulk, o = carve(o, L)
        fwd, o = carve(o, L)
        bwd, o = carve(o, L)
        e_ht, o = carve(o, L)
        assert o <= WORK, o
        edge_col = sb("edge_col", [P, 4])
        edge_row = sb("edge_row", [1, 4 * P])
        scan_row = sb("scan_row", [1, 2 * (P + 2)])
        carry = sb("carry", [P, 2])

        const_done = sem("const_done")
        pool_step = sem("pool_step")
        x_in = sem("x_in")
        w_in = sem("w_in")
        attn_in = sem("attn_in")
        rows_in = sem("rows_in")
        base_in = sem("base_in")
        dstb_in = sem("dstb_in")
        small_in = sem("small_in")
        dve_step = sem("dve_step")
        xn_done = sem("xn_done")
        var_done = sem("var_done")
        std_done = sem("std_done")
        rows_done = sem("rows_done")
        rowsT_done = sem("rowsT_done")
        idx_done = sem("idx_done")
        rel_done = sem("rel_done")
        far_col_done = sem("far_col_done")
        far_psum = sem("far_psum")
        flag_done = sem("flag_done")
        wa_done = sem("wa_done")
        xn_done2 = sem("xn_done2")
        xt_done2 = sem("xt_done2")
        xt_copied2 = sem("xt_copied2")
        xt_done = sem("xt_done")
        xt_copied = sem("xt_copied")
        el_done = sem("el_done")
        el_copied = sem("el_copied")
        tab_out = sem("tab_out")
        feat_done = sem("feat_done")
        feat_act = sem("feat_act")
        feat_dve = sem("feat_dve")
        feat_out = [sem(f"feat_out{u}") for u in range(2)]
        (er_win_clear, typ_psum, hot_e_done, hotT_psum, hotT_done, er_psum, mask_done, er_picked, er_done, score_sum,
         far_er_idx, far_er_in, far_er_done) = [sem(n) for n in """er_win_clear typ_psum hot_e_done hotT_psum hotT_done
            er_psum mask_done er_picked er_done score_sum far_er_idx far_er_in far_er_done""".split()]
        er_win_in = [sem(f"er_win_in{u}") for u in range(2)]
        gathered = [sem(f"gathered{s}") for s in range(2)]
        scores_done = sem("scores_done")
        idx_copied = sem("idx_copied")
        dstb_clear = sem("dstb_clear")
        eht_done = sem("eht_done")
        ebulk_psum = sem("ebulk_psum")
        ebulk_done = sem("ebulk_done")
        cols_done = sem("cols_done")
        rows_psum = sem("rows_psum")
        srow_done = sem("srow_done")
        carry_psum = sem("carry_psum")
        shifted = sem("shifted")
        exp_done = sem("exp_done")
        alpha_bulk = sem("alpha_bulk")
        alpha_psum = sem("alpha_psum")

        rows_copied = sem("rows_copied")
        feats_in = [sem(f"feats_in{k}") for k in range(ST)]

        def feats(k):
            if k < EARLY:
                return weights[:, k * D:(k + 1) * D]
            return late_feats[:, (k - EARLY) * D:(k - EARLY + 1) * D]

        def gather_feats(pool, k, n):
            pool.indirect_dma_start(feats(k)[0:n, :], None, feat_tab[:, :],
                                    bass.IndirectOffsetOnAxis(ap=feat_rows[0:n, k:k + 1], axis=0))\
                .then_inc(feats_in[k // G], 16)

        x_tiles = x[0:(NT - 1) * P, :].rearrange("(t p) d -> p t d", p=P)

        def irregular(eng):
            return eng.value_load(far_i[0:1, 0:1], min_val=0, max_val=1)

        with nc.Block() as block:
            @block.sync
            def _(sp):
                sp.wait_ge(const_done, 1)
                sp.dma_start(x_sb[:, 0:(NT - 1) * D].rearrange("p (t d) -> p t d", d=D), x_tiles).then_inc(x_in, 16)
                sp.dma_start(x_sb[0:NLAST, (NT - 1) * D:NT * D], x[(NT - 1) * P:N, :]).then_inc(x_in, 16)
                for s, a in enumerate((src, dst, etype)):
                    full = rowi[:, s * 4 * P:s * 4 * P + 3 * P].rearrange("t (b p) -> t b p", p=P)
                    sp.dma_start(full, a[0:3 * P * P].rearrange("(b t p) -> t b p", b=3, p=P)).then_inc(rows_in, 16)
                    rest = ET - 1 - 3 * P
                    last = rowi[:, (s * 4 + 3) * P:(s * 4 + 4) * P]
                    sp.dma_start(last[0:rest, :], a[3 * P * P:(ET - 1) * P].rearrange("(t p) -> t p", p=P))\
                      .then_inc(rows_in, 16)
                    sp.dma_start(last[rest:rest + 1, 0:ELAST], a[(ET - 1) * P:E].rearrange("(t p) -> t p", t=1))\
                      .then_inc(rows_in, 16)
                step = G * P
                sp.dma_start(base_i[0:1, 0:NG - 1], dst[0:(NG - 1) * step].rearrange("(g e) -> e g", e=step)[0:1, :])\
                  .then_inc(base_in, 16)
                sp.dma_start(base_i[0:1, NG - 1:NG], dst[(NG - 1) * step:(NG - 1) * step + 1]
                             .rearrange("(a b) -> a b", a=1)).then_inc(base_in, 16)
                sp.dma_start(att_l, attn_l.rearrange("r h d -> (r h d)").partition_broadcast(P)).then_inc(attn_in, 16)
                sp.dma_start(att_r, attn_r.rearrange("r h d -> (r h d)").partition_broadcast(P)).then_inc(attn_in, 16)
                for r in range(R):
                    for k in range(KC):
                        o = k * RHD + r * H * HD
                        sp.dma_start(wconv[:, o:o + H * HD].rearrange("p (h d) -> p h d", d=HD),
                                     conv_w[r, :, k * P:(k + 1) * P, :].rearrange("h p d -> p h d")).then_inc(w_in, 16)
                sp.dma_start(hb[:, :], h_bias.rearrange("(k p) -> p k", p=P)).then_inc(small_in, 16)
                sp.dma_start(b1_sb[:, :].rearrange("p (e k) -> p e k", k=KC), b1.rearrange("e (k p) -> p e k", p=P))\
                  .then_inc(small_in, 16)
                sp.dma_start(b2_sb[:, :], b2).then_inc(small_in, 16)
                sp.dma_start(rw_sb[:, :], router_w).then_inc(small_in, 16)
                sp.wait_ge(small_in, 64)
                sp.wait_ge(el_copied, NT)
                for k, tab in enumerate((el_tab, er_tab)):
                    part = elr.rearrange("p (t s c) -> p t s c", s=2, c=RH)[:, :, k, :]
                    sp.dma_start(tab[:, :].rearrange("(t p r) h -> p t (r h)", p=P, r=R), part).then_inc(tab_out, 16)
                with sp.Fori(0, NT // 2) as i:
                    for u in range(2):
                        sp.wait_ge(feat_act, i * 4 + 2 * u + 2)
                        sp.wait_ge(feat_dve, i * 4 + 2 * u + 2)
                        sp.dma_start(feat_tab[ds(i * (2 * P * R) + u * P * R, P * R), :]
                                     .rearrange("(p r) d -> p (r d)", r=R),
                                     fout[:, u * RHD:(u + 1) * RHD]).then_inc(feat_out[u], 16)
                for u in range(2):
                    sp.wait_ge(feat_out[u], 16 * (NT // 2))
                sp.wait_ge(tab_out, 32)
                sp.wait_ge(er_win_clear, 1)

                def er_windows(i, first):
                    for u in range(2):
                        if not first:
                            sp.wait_ge(er_psum, i * 2 + (u - 1))
                        for s in range(GPI):
                            base = sp.value_load(base_i[0:1, ds(i * (2 * GPI) + (u * GPI + s), 1)], min_val=0, max_val=N - 1)
                            sp.dma_start(er_win[s * W:(s + 1) * W, u * P + s * W:u * P + (s + 1) * W],
                                         er_tab[:, :].rearrange("(n r) h -> n (r h)", r=R)[ds(base, W), :])\
                              .then_inc(er_win_in[u], 16)

                er_windows(0, True)
                with sp.Fori(1, TURNS2 // 2) as i:
                    er_windows(i, False)
                sp.wait_ge(dstb_clear, 1)

                def row(a, b):
                    return dst[a:b].rearrange("(o n) -> o n", o=1)

                for h in range(H):
                    p = h * C
                    for to, frm in (
                        (dsti[p:p + 1, 1:L + 2], row(0, L + 1)),
                        (dsti[p + 1:p + C - 1, 0:L], dst[L - 1:(C - 1) * L - 1].rearrange("(c l) -> c l", l=L)),
                        (dsti[p + 1:p + C - 1, L:L + 1],
                         dst[L:(C - 1) * L].rearrange("(c l) -> c l", l=L)[:, L - 1:L]),
                        (dsti[p + 1:p + C - 2, L + 1:L + 2],
                         dst[2 * L:(C - 1) * L].rearrange("(c l) -> c l", l=L)[:, 0:1]),
                        (dsti[p + C - 2:p + C - 1, L + 1:L + 2], row((C - 1) * L, (C - 1) * L + 1)),
                        (dsti[p + C - 1:p + C, 0:E - (C - 1) * L + 1], row((C - 1) * L - 1, E)),
                    ):
                        sp.dma_start(to, frm).then_inc(dstb_in, 16)

            @block.gpsimd
            def _(pool):
                pool.memset(x_sb[:, (NT - 1) * D:NT * D], 0.0)
                pool.memset(base_i[:, :], 0)
                pool.memset(rowi, 0).then_inc(const_done, 1)
                pool.memset(ident[:, :], 0.0).then_inc(pool_step, 1)
                pool.memset(ones[:, :], 1.0)
                pool.iota(iota_w[:, :], pattern=[[1, W]], base=0, channel_multiplier=0,
                          allow_small_or_imprecise_dtypes=True)
                pool.wait_ge(pool_step, 1)
                pool.affine_select(out=ident[:, :], in_=ident[:, :], compare_op=ALU.not_equal, fill=1.0, base=0,
                                   pattern=[[-1, P]], channel_multiplier=1)
                tail = (ET - 1) * H
                pool.memset(el[:, tail:], 0.0).then_inc(const_done, 1)
                pool.wait_ge(const_done, 2)
                pool.wait_ge(tab_out, 32)
                pool.wait_ge(idx_done, 1)


                def gather_turn(i, first):
                    for s in range(2):
                        n = i * (2 * SG) + s * SG
                        o = s * SG
                        if not first:
                            keep_scores(i, s, n - 2 * SG)
                        pool.tensor_copy(idx_ring[:, o:o + SG], idx_l[:, ds(n, SG)]).then_inc(idx_copied, 1)
                        pool.wait_ge(idx_copied, i * 2 + (s + 1))
                        pool.nop(nofuse=True)
                        for j in range(SG):
                            c = o + j
                            pool.indirect_dma_start(score_ring[:, c * H:(c + 1) * H], None, el_tab[:, :],
                                                    bass.IndirectOffsetOnAxis(ap=idx_ring[:, c:c + 1], axis=0))\
                                .then_inc(gathered[s], 16)

                def keep_scores(i, s, n):
                    pool.wait_ge(gathered[s], i * (16 * SG))
                    pool.tensor_copy(el[:, ds(n * H, SG * H)], score_ring[:, s * SG * H:(s + 1) * SG * H])\
                        .then_inc(scores_done, 1)

                turns = (ET - 1) // (2 * SG)
                gather_turn(0, True)
                with pool.Fori(1, turns) as i:
                    gather_turn(i, False)
                for s in range(2):
                    keep_scores(turns, s, ET - 1 - 2 * SG + s * SG)
                pool.indirect_dma_start(el[0:ELAST, tail:tail + H], None, el_tab[:, :],
                                        bass.IndirectOffsetOnAxis(ap=idx_l[0:ELAST, ET - 1:ET], axis=0))\
                    .then_inc(gathered[0], 16)
                pool.wait_ge(rows_copied, 1)
                for u in range(2):
                    pool.wait_ge(feat_out[u], 16 * (NT // 2))
                for k in range(EARLY):
                    gather_feats(pool, k, P)
                pool.wait_ge(flag_done, 1)
                with pool.If(irregular(pool) == 1):
                    pool.wait_ge(scores_done, 2 * turns)
                    pool.wait_ge(er_done, TURNS2)
                    with pool.Fori(0, ET) as t:
                        pool.tensor_copy(idx_ring[:, 0:1], idx_r[:, ds(t, 1)]).then_inc(far_er_idx, 1)
                        pool.wait_ge(far_er_idx, t + 1)
                        pool.nop(nofuse=True)
                        pool.indirect_dma_start(score_ring[:, 0:H], None, er_tab[:, :],
                                                bass.IndirectOffsetOnAxis(ap=idx_ring[:, 0:1], axis=0))\
                            .then_inc(far_er_in, 16)
                        pool.wait_ge(far_er_in, t * 16 + 16)
                        pool.tensor_copy(er[:, ds(t * H, H)], score_ring[:, 0:H]).then_inc(far_er_done, 1)
                        pool.wait_ge(far_er_done, t + 1)

            @block.scalar
            def _(act):
                act.wait_ge(var_done, 1)
                act.activation(rstd[:, :], rstd[:, :], ACT.Sqrt).then_inc(std_done, 1)
                with act.Fori(0, NT // 2) as i:
                    for u in range(2):
                        act.wait_ge(xt_done, i * 2 + (u + 1))
                        act.activation(xT[:, u * D:(u + 1) * D], psum[4 + u][:, 0:D], ACT.Copy).then_inc(xt_copied, 1)
                    for u in range(2):
                        act.wait_ge(el_done, i * 2 + (u + 1))
                        act.activation(elr[:, ds(i * (4 * RH) + u * 2 * RH, 2 * RH)], psum[6 + u][:, 0:2 * RH],
                                       ACT.Copy).then_inc(el_copied, 1)

                def copy_xt(n, u):
                    act.wait_ge(xt_done2, n + 1)
                    act.activation(xT[:, u * D:(u + 1) * D], psum[6 + u][:, 0:D], ACT.Copy).then_inc(xt_copied2, 1)

                def turn(i, first, last):
                    for u in range(2):
                        if not first:
                            act.wait_ge(feat_out[u], i * 16)
                        for b in range(2):
                            act.wait_ge(feat_done, i * 8 + (4 * u + b + 1))
                            act.activation(fout[:, u * RHD + b * 512:u * RHD + (b + 1) * 512],
                                           psum[b][:, :], ACT.Copy).then_inc(feat_act, 1)
                        if not (last and u == 1):
                            copy_xt(i * 2 + (u + 1), (u + 1) % 2)

                copy_xt(0, 0)
                turn(0, True, False)
                with act.Fori(1, NT // 2 - 1) as i:
                    turn(i, False, False)
                turn(NT // 2 - 1, False, True)
                def hot_turn(i, first):
                    for u in range(2):
                        act.wait_ge(hotT_psum, i * 2 + (u + 1))
                        if not first:
                            act.wait_ge(er_psum, i * 2 + (u - 1))
                        act.activation(hotT[:, u * G * P:(u + 1) * G * P], psum[4 + u][:, 0:G * P], ACT.Copy)\
                           .then_inc(hotT_done, 1)

                hot_turn(0, True)
                with act.Fori(1, TURNS2 // 2) as i:
                    hot_turn(i, False)
                for b in range(4):
                    act.wait_ge(ebulk_psum, b + 1)
                    n = min(4, J - 4 * b) * P
                    act.activation(ebulk[:, b * 512:b * 512 + n], psum[b][:, 0:n], ACT.Copy).then_inc(ebulk_done, 1)
                act.wait_ge(shifted, 1)
                act.activation(bwd, ebulk, ACT.Exp).then_inc(exp_done, 1)

            @block.vector
            def _(dve):
                step = [0]

                def link(ins):
                    step[0] += 1
                    ins.then_inc(dve_step, 1)
                    dve.wait_ge(dve_step, step[0])

                dve.wait_ge(x_in, 32)
                with dve.Fori(0, NT - 1) as t:
                    dve.bn_stats(stats[:, ds(t * 6, 6)], x_sb[:, ds(t * D, D)])
                link(dve.bn_stats(stats[:, (NT - 1) * 6:], x_sb[:, (NT - 1) * D:]))
                for t in range(NT):
                    last = dve.bn_aggr(mv[:, t * 2:t * 2 + 2], stats[:, t * 6:t * 6 + 6])
                link(last)
                mvv = mv[:, :].rearrange("p (t two) -> p t two", two=2)
                dve.tensor_scalar(rstd[:, :], mvv[:, :, 1], EPS, None, ALU.add).then_inc(var_done, 1)
                dve.wait_ge(std_done, 1)
                link(dve.reciprocal(rstd[:, :], rstd[:, :]))
                dve.wait_ge(rows_in, 144)
                link(dve.tensor_copy(rowf, rowi))
                q = 4 * P
                dve.wait_ge(base_in, 32)
                link(dve.tensor_copy(base_f[:, :], base_i[:, 0:NG]))
                link(dve.scalar_tensor_tensor(rowx[:, 0:q], rowf[:, 0:q], float(R), rowf[:, 2 * q:3 * q],
                                              ALU.mult, ALU.add))
                dve.scalar_tensor_tensor(rowx[:, q:2 * q], rowf[:, q:2 * q], float(R), rowf[:, 2 * q:3 * q],
                                         ALU.mult, ALU.add).then_inc(rows_done, 1)
                dve.wait_ge(attn_in, 32)
                dve.wait_ge(w_in, 16 * R * KC)
                for k in range(KC):
                    for s, att in enumerate((att_l, att_r)):
                        link(dve.tensor_tensor(prod, wconv[:, k * RHD:(k + 1) * RHD], att, ALU.mult))
                        o = (k * 2 + s) * RH
                        link(dve.tensor_reduce(wa[:, o:o + RH], prod.rearrange("p (c d) -> p c d", d=HD), AX.X, ALU.add))

                def normalise(t, u, done):
                    dve.tensor_scalar(xn[:, u * D:(u + 1) * D], x_sb[:, ds(t * D, D)], mv[:, ds(t * 2, 1)],
                                      rstd[:, ds(t, 1)], ALU.subtract, ALU.mult).then_inc(done, 1)

                for u in range(2):
                    normalise(u, u, xn_done)
                with dve.Fori(1, NT // 2) as i:
                    for u in range(2):
                        dve.wait_ge(xt_done, i * 2 + (u - 1))
                        normalise(i * 2 + u, u, xn_done)
                dve.wait_ge(rowsT_done, 4)
                link(dve.tensor_copy(idx_l[:, :], psum[0][:, :]))
                dve.tensor_copy(feat_rows[:, :], idx_l[:, 0:FR]).then_inc(rows_copied, 1)
                dve.tensor_copy(idx_r[:, :], psum[1][:, :]).then_inc(idx_done, 1)
                link(dve.tensor_copy(dst_t[:, :], psum[2][:, :]))
                m = NG - 1
                dve.memset(rel[:, ET:], 0.0)
                link(dve.tensor_tensor(rel[:, 0:m * G].rearrange("p (g j) -> p g j", j=G),
                                       dst_t[:, 0:m * G].rearrange("p (g j) -> p g j", j=G),
                                       psum[3][:, 0:m].unsqueeze(2).to_broadcast([P, m, G]), ALU.subtract))
                dve.tensor_tensor(rel[:, m * G:ET], dst_t[:, m * G:ET], psum[3][:, m:NG], ALU.subtract)\
                   .then_inc(rel_done, 1)
                dve.wait_ge(rel_done, 1)
                dve.tensor_reduce(far_col[:, :], rel[:, 0:ET], AX.X, ALU.max).then_inc(far_col_done, 1)
                late = far_row[:, 1:1 + NS - 1]
                link(dve.scalar_tensor_tensor(late, iota_w[0:1, 1:NS], float(TOK),
                                              base_f[0:1, ST + LAG:(NS - 1) * ST + LAG + 1:ST], ALU.mult, ALU.subtract))
                link(dve.tensor_reduce(late[:, 0:1], late, AX.X, ALU.max))
                dve.wait_ge(far_psum, 1)
                link(dve.tensor_reduce(far_row[:, 0:1], psum[4][0:1, 0:P], AX.X, ALU.max))
                link(dve.tensor_scalar(far_row[:, 0:1], far_row[:, 0:1], float(1 - W), None, ALU.add))
                link(dve.tensor_tensor(far_row[:, 0:1], far_row[:, 0:1], late[:, 0:1], ALU.max))
                dve.tensor_scalar(far_i[:, :], far_row[:, 0:1], 0.0, None, ALU.is_gt).then_inc(flag_done, 1)
                dve.wait_ge(xt_done, NT)
                for u in range(2):
                    normalise(u, u, xn_done2)

                def turn(i, first, last):
                    for u in range(2):
                        if not last:
                            dve.wait_ge(xt_done2, i * 2 + (u + 1))
                            normalise(i * 2 + (u + 2), u, xn_done2)
                        if not first:
                            dve.wait_ge(feat_out[u], i * 16)
                        for b in range(2, 4):
                            dve.wait_ge(feat_done, i * 8 + (4 * u + b + 1))
                            dve.tensor_copy(fout[:, u * RHD + b * 512:u * RHD + (b + 1) * 512],
                                            psum[b][:, :]).then_inc(feat_dve, 1)

                turn(0, True, False)
                with dve.Fori(1, NT // 2 - 1) as i:
                    turn(i, False, False)
                turn(NT // 2 - 1, False, True)
                dve.memset(er_win, 0.0).then_inc(er_win_clear, 1)
                dve.wait_ge(typ_psum, 1)
                link(dve.tensor_copy(typ, psum[0][:, :]))

                def hot_build(n, u):
                    dve.tensor_tensor(hot_e[:, u * G * P:(u + 1) * G * P].rearrange("p (j s w) -> p j s w", j=G, w=W),
                                      iota_w[:, :].unsqueeze(1).unsqueeze(1).to_broadcast([P, G, GPI, W]),
                                      rel[:, ds(n * RING, RING)].rearrange("p (s j) -> p j s", j=G).unsqueeze(3)
                                      .to_broadcast([P, G, GPI, W]), ALU.is_equal).then_inc(hot_e_done, 1)

                def er_turn(i, first, last):
                    for u in range(2):
                        n = i * 2 + u
                        if not (last and u):
                            if not (first and u == 0):
                                dve.wait_ge(hotT_psum, n)
                            hot_build(n + 1, (u + 1) % 2)
                        dve.tensor_tensor(rel_mask.rearrange("p (j s r) -> p j s r", j=G, r=R),
                                          iota_w[:, 0:R].unsqueeze(1).unsqueeze(1).to_broadcast([P, G, GPI, R]),
                                          typ[:, ds(n * RING, RING)].rearrange("p (s j) -> p j s", j=G).unsqueeze(3)
                                          .to_broadcast([P, G, GPI, R]), ALU.is_equal).then_inc(mask_done, 1)
                        dve.wait_ge(mask_done, n + 1)
                        dve.wait_ge(er_psum, n + 1)
                        dve.tensor_tensor(er_all.rearrange("p (t r h) -> p t r h", r=R, h=H),
                                          psum[6 + u][:, 0:RING * RH].rearrange("p (t r h) -> p t r h", r=R, h=H),
                                          rel_mask.rearrange("p (t r) -> p t r", r=R).unsqueeze(3)
                                          .to_broadcast([P, RING, R, H]), ALU.mult).then_inc(er_picked, 1)
                        dve.wait_ge(er_picked, n + 1)
                        dve.tensor_reduce(er[:, ds(n * RING * H, RING * H)].rearrange("p (t h) -> p t h", h=H),
                                          er_all.rearrange("p (t r h) -> p t h r", r=R, h=H), AX.X, ALU.add)\
                           .then_inc(er_done, 1)

                hot_build(0, 0)
                er_turn(0, True, False)
                with dve.Fori(1, TURNS2 // 2 - 1) as i:
                    er_turn(i, False, False)
                er_turn(TURNS2 // 2 - 1, False, True)
                dve.wait_ge(er_done, TURNS2)
                dve.wait_ge(tab_out, 32)
                dve.wait_ge(xt_copied2, NT)
                dve.wait_ge(feat_act, 2 * NT)
                dve.memset(dsti, -1).then_inc(dstb_clear, 1)
                dve.wait_ge(dstb_in, 16 * 6 * H)
                link(dve.tensor_copy(dstf, dsti))
                link(dve.tensor_tensor(same[:, 0:L + 1], dstf[:, 0:L + 1], dstf[:, 1:L + 2], ALU.is_equal))
                link(dve.tensor_scalar(pen[:, 0:L + 1], same[:, 0:L + 1], -1.0, BIG, ALU.add, ALU.mult))
                dve.memset(acc[:, :], 0.0)
                dve.wait_ge(scores_done, (ET - 1) // SG)
                dve.wait_ge(gathered[0], 16 * ((ET - 1) // 2 + 1))
                flag = irregular(dve)
                with dve.If(flag == 0):
                    for j in range(G):
                        a = el[:, :].rearrange("p (i s j h) -> p i j s h", s=GPI, j=G, h=H)[:, :, j]
                        dve.tensor_tensor(a, a, er[:, :].rearrange("p (i j s h) -> p i j s h", s=GPI, j=G, h=H)[:, :, j],
                                          ALU.add).then_inc(score_sum, 1)
                    dve.wait_ge(score_sum, G)
                with dve.If(flag == 1):
                    dve.wait_ge(far_er_done, ET)
                    dve.tensor_tensor(el[:, 0:ET * H], el[:, 0:ET * H], er[:, 0:ET * H], ALU.add).then_inc(score_sum, G)
                    dve.wait_ge(score_sum, G)
                ev = el[:, :].rearrange("p (t h) -> p h t", h=H)
                dve.scalar_tensor_tensor(e_ht.rearrange("p (h t) -> p h t", h=H), ev, 0.2, ev, ALU.mult, ALU.max)\
                   .then_inc(eht_done, 1)
                dve.wait_ge(ebulk_done, 4)

                def segment_scans(n, near, data, op0, op1, start, fo, bo):
                    nxt = near[:, 1:L + 1]
                    link(dve.tensor_tensor_scan(fo, near[:, 0:L], data, start, op0, op1))
                    link(dve.tensor_tensor_scan(bo[:, ::-1], nxt[:, ::-1], data[:, ::-1], start, op0, op1))
                    link(dve.tensor_copy(edge_col[:, 0:1], fo[:, L - 1:L]))
                    link(dve.tensor_reduce(edge_col[:, 1:2], near[:, 0:L], AX.X, ALU.min))
                    link(dve.tensor_copy(edge_col[:, 2:3], bo[:, 0:1]))
                    dve.tensor_reduce(edge_col[:, 3:4], nxt, AX.X, ALU.min).then_inc(cols_done, 1)
                    dve.wait_ge(rows_psum, n)
                    link(dve.tensor_copy(edge_row[:, :], psum[4][0:1, :]))
                    r = edge_row[:, :].rearrange("o (k p) -> o k p", p=P)
                    link(dve.memset(scan_row[:, :], start))
                    link(dve.tensor_tensor_scan(scan_row[:, 1:P + 1], r[:, 1, :], r[:, 0, :], start, op0, op1))
                    back = scan_row[:, P + 2:2 * P + 2]
                    dve.tensor_tensor_scan(back[:, ::-1], r[:, 3, ::-1], r[:, 2, ::-1], start, op0, op1)\
                       .then_inc(srow_done, 1)
                    dve.wait_ge(carry_psum, n)
                    link(dve.tensor_copy(carry[:, :], psum[5][:, 0:2]))
                    link(dve.tensor_tensor_scan(fo, near[:, 0:L], data, carry[:, 0:1], op0, op1))
                    link(dve.tensor_tensor_scan(bo[:, ::-1], nxt[:, ::-1], data[:, ::-1], carry[:, 1:2], op0, op1))

                segment_scans(1, pen, ebulk, ALU.add, ALU.max, -BIG, fwd, bwd)
                link(dve.tensor_tensor(fwd, fwd, bwd, ALU.max))
                dve.tensor_tensor(ebulk, ebulk, fwd, ALU.subtract).then_inc(shifted, 1)
                dve.wait_ge(exp_done, 1)
                segment_scans(2, same, bwd, ALU.mult, ALU.add, 0.0, fwd, ebulk)
                link(dve.tensor_tensor(fwd, fwd, ebulk, ALU.add))
                link(dve.tensor_tensor(fwd, fwd, bwd, ALU.subtract))
                link(dve.reciprocal(ebulk, fwd))
                dve.tensor_tensor(fwd, bwd, ebulk, ALU.mult).then_inc(alpha_bulk, 1)
                av = alpha[:, :].rearrange("p (c j h) -> p j h c", j=J, h=H)
                for j in range(J):
                    dve.wait_ge(alpha_psum, j // 4 + 1)
                    ap = psum[j // 4][:, (j % 4) * P:(j % 4 + 1) * P].rearrange("p (h c) -> p h c", h=H)
                    dve.tensor_copy(av[:, j], ap)

            @block.tensor
            def _(pe):
                pe.wait_ge(const_done, 2)
                pe.wait_ge(rows_done, 1)
                for k, s in enumerate((rowx[:, 0:512], rowx[:, 512:1024], rowf[:, 512:1024])):
                    for b in range(4):
                        last = pe.transpose(psum[k][:, b * P:(b + 1) * P], s[:, b * P:(b + 1) * P], ident[:, :])
                    last.then_inc(rowsT_done, 1)
                pe.matmul(psum[3][:, 0:NG], ones[0:1, :], base_f[0:1, :], start=True, stop=True).then_inc(rowsT_done, 1)

                def el_turn(i, first):
                    for u in range(2):
                        pe.wait_ge(xn_done, i * 2 + (u + 1))
                        if not first:
                            pe.wait_ge(xt_copied, i * 2 + (u - 1))
                        for k in range(KC):
                            last = pe.transpose(psum[4 + u][:, k * P:(k + 1) * P],
                                                xn[:, u * D + k * P:u * D + (k + 1) * P], ident[:, :])
                        last.then_inc(xt_done, 1)
                    for u in range(2):
                        pe.wait_ge(xt_copied, i * 2 + (u + 1))
                        if not first:
                            pe.wait_ge(el_copied, i * 2 + (u - 1))
                        for k in range(KC):
                            last = pe.matmul(psum[6 + u][:, 0:2 * RH], xT[:, u * D + k * P:u * D + (k + 1) * P],
                                             wa[:, k * 2 * RH:(k + 1) * 2 * RH], start=k == 0, stop=k == KC - 1)
                        last.then_inc(el_done, 1)

                el_turn(0, True)
                with pe.Fori(1, NT // 2) as i:
                    el_turn(i, False)

                def transposes(n, u, first):
                    pe.wait_ge(xn_done2, n + 1)
                    if not first:
                        pe.wait_ge(xt_copied2, n - 1)
                    for k in range(KC):
                        last = pe.transpose(psum[6 + u][:, k * P:(k + 1) * P],
                                            xn[:, u * D + k * P:u * D + (k + 1) * P], ident[:, :])
                    last.then_inc(xt_done2, 1)

                def turn(i, first, last_turn):
                    for u in range(2):
                        pe.wait_ge(xt_copied2, i * 2 + (u + 1))
                        for b in range(4):
                            if b == 2 and not (last_turn and u == 1):
                                transposes(i * 2 + (u + 1), (u + 1) % 2, first and u == 0)
                            if not (first and u == 0):
                                pe.wait_ge(feat_act if b < 2 else feat_dve, i * 4 + (2 * u + b % 2 - 1))
                            for k in range(KC):
                                o = k * RHD + b * 512
                                last = pe.matmul(psum[b][:, :], xT[:, u * D + k * P:u * D + (k + 1) * P],
                                                 wconv[:, o:o + 512], start=k == 0, stop=k == KC - 1)
                            last.then_inc(feat_done, 1)

                pe.wait_ge(idx_done, 1)
                pe.wait_ge(rel_done, 1)
                pe.wait_ge(el_copied, NT)
                pe.wait_ge(far_col_done, 1)
                pe.transpose(psum[4][0:1, 0:P], far_col[:, :], ident[:, :]).then_inc(far_psum, 1)
                transposes(0, 0, True)
                turn(0, True, False)
                with pe.Fori(1, NT // 2 - 1) as i:
                    turn(i, False, False)
                turn(NT // 2 - 1, False, True)
                pe.wait_ge(feat_act, 2 * NT)
                pe.wait_ge(feat_dve, 2 * NT)
                for b in range(4):
                    last = pe.transpose(psum[0][:, b * P:(b + 1) * P], rowf[:, (8 + b) * P:(9 + b) * P], ident[:, :])
                last.then_inc(typ_psum, 1)

                def hot_transpose(n, u, first):
                    pe.wait_ge(hot_e_done, n + 1)
                    if not first:
                        pe.wait_ge(hotT_done, n - 1)
                    for j in range(G):
                        last = pe.transpose(psum[4 + u][:, j * P:(j + 1) * P],
                                            hot_e[:, (u * G + j) * P:(u * G + j + 1) * P], ident[:, :])
                    last.then_inc(hotT_psum, 1)

                def er_turn(i, first, last_turn):
                    for u in range(2):
                        n = i * 2 + u
                        if not (last_turn and u):
                            hot_transpose(n + 1, (u + 1) % 2, first and u == 0)
                        pe.wait_ge(hotT_done, n + 1)
                        pe.wait_ge(er_win_in[u], i * (16 * GPI) + 16 * GPI)
                        if not first:
                            pe.wait_ge(er_picked, n - 1)
                        for j in range(G):
                            last = pe.matmul(psum[6 + u][:, j * P:(j + 1) * P],
                                             hotT[:, (u * G + j) * P:(u * G + j + 1) * P], er_win[:, u * P:(u + 1) * P],
                                             start=True, stop=True)
                        last.then_inc(er_psum, 1)

                hot_transpose(0, 0, True)
                er_turn(0, True, False)
                with pe.Fori(1, TURNS2 // 2 - 1) as i:
                    er_turn(i, False, False)
                er_turn(TURNS2 // 2 - 1, False, True)
                pe.wait_ge(eht_done, 1)
                for j in range(J):
                    last = pe.transpose(psum[j // 4][:, (j % 4) * P:(j % 4 + 1) * P], e_ht[:, j::J], ident[:, :])
                    if j % 4 == 3 or j == J - 1:
                        last.then_inc(ebulk_psum, 1)
                for n in (1, 2):
                    pe.wait_ge(cols_done, n)
                    for k in range(4):
                        last = pe.transpose(psum[4][0:1, k * P:(k + 1) * P], edge_col[:, k:k + 1], ident[:, :])
                    last.then_inc(rows_psum, 1)
                    pe.wait_ge(srow_done, n)
                    pe.matmul(psum[5][:, 0:1], scan_row[0:1, 0:P], ones[0:1, 0:1], start=True, stop=True)
                    pe.matmul(psum[5][:, 1:2], scan_row[0:1, P + 3:2 * P + 3], ones[0:1, 0:1], start=True, stop=True)\
                      .then_inc(carry_psum, 1)
                pe.wait_ge(alpha_bulk, 1)
                pe.wait_ge(ebulk_done, 4)
                for j in range(J):
                    last = pe.transpose(psum[j // 4][:, (j % 4) * P:(j % 4 + 1) * P], fwd[:, j * P:(j + 1) * P], ident[:, :])
                    if j % 4 == 3 or j == J - 1:
                        last.then_inc(alpha_psum, 1)

        w1_sb, o = carve(0, X * KC * D)
        w2_sb, o = carve(o, X * KC * D)
        hot, o = carve(o, 2 * G * W)
        hot_a, o = carve(o, HOTS * G * H * W)
        xlT, o = carve(o, KC * TOK)
        xlT_next, o = carve(o, KC * TOK)
        hs = el[:, 0:KC * TOK]
        x2 = el[:, KC * TOK:KC * TOK + TC * D]
        xl, o = carve(o, TC * D)
        hT, o = carve(o, 4 * TOK)
        scT, o = carve(o, TOK)
        combT, o = carve(o, TOK)
        assert o <= WORK - (FR - EARLY) * D, o
        WIN = 480
        NW = NP_ // WIN
        far = weights[:, 2 * D:]
        iota_n = far[:, 0:WIN]
        hot_n = far[:, WIN:3 * WIN]
        far_a = far[:, 3 * WIN:3 * WIN + H]
        far_d = far[:, 4 * WIN:4 * WIN + NW]
        comb = er[:, 0:NT * X]
        expo, probs, top, top_f, pick = (er[:, NT * X + i * 32:NT * X + i * 32 + TC * X] for i in range(5))
        top_i = er[:, NT * X + 160:NT * X + 160 + TC * X].bitcast(U32)
        comb_c = er[:, NT * X + 224:NT * X + 224 + TC * X]
        mx = er[:, NT * X + 192:NT * X + 192 + TC]
        wt = er[:, NT * X + 200:NT * X + 200 + 2 * TC]
        mv2 = sb("mv2", [P, 2 * TC])
        st2 = sb("st2", [P, 6 * TC])
        rs2 = sb("rs2", [P, TC])
        accv = acc[:, :].rearrange("p (k n) -> p k n", k=KC)

        names = """xlT_kept experts_in feat_idx hot_done hot_a_done agg_done acc_step rwT_psum rwT_done hs_done x2_psum
            x2_done stats_done mv_done var2_done std2_done rs_done xl_done base_done xlT_psum xlT_done score_psum
            score_done scoreT_psum score_max score_shift score_exp router_step combine_step comb_done combT_psum combT_done b2_psum
            b2_done h_psum h_done y_psum y_done out_done far_in far_iota far_idx far_mask far_hot far_sum far_add"""
        (xlT_kept, experts_in, feat_idx, hot_done, hot_a_done, agg_done, acc_step, rwT_psum, rwT_done, hs_done, x2_psum,
         x2_done, stats_done, mv_done, var2_done, std2_done, rs_done, xl_done, base_done, xlT_psum, xlT_done, score_psum,
         score_done, scoreT_psum, score_max, score_shift, score_exp, router_step, combine_step, comb_done, combT_psum, combT_done, b2_psum,
         b2_done, h_psum, h_done, y_psum, y_done, out_done, far_in, far_iota, far_idx, far_mask, far_hot, far_sum,
         far_add) = [sem(n) for n in names.split()]

        def wait(eng, s, v):
            if not (isinstance(v, int) and v <= 0):
                eng.wait_ge(s, v)

        PREP = {4: ("h_copy",), 5: ("h_transpose", "x2"), 6: ("std",), 7: ("xl",), 8: ("xl_transpose", "xlT_copy"),
                9: ("scores", "score_copy"), 10: ("score_transpose", "shift", "exp"), 11: ("route",), 13: ("combine",),
                14: ("weight_transpose", "weight_copy"), 15: ("bias2", "bias2_add", "xlT_keep")}
        EXPERTS = [("up", 0), ("up", 1)]
        for e in range(X - 2):
            EXPERTS += [("down", e), ("up", e + 2)]
        EXPERTS += [("down", X - 2), ("down", X - 1)]

        def super_turn(steps, s=None, p=None, c=None, windows=ST, nodes_done=None):
            for n in range(ST):
                if s is not None and n < windows:
                    steps["window"](s, n)
                if s is not None and n == windows and "last_window" in steps:
                    steps["last_window"]()
                if p is not None:
                    for name in PREP.get(n, ()):
                        if name in steps:
                            steps[name](p, nodes_done) if name == "h_copy" else steps[name](p)
                if c is not None and EXPERTS[n][0] in steps:
                    steps[EXPERTS[n][0]](c, EXPERTS[n][1])

        ALL = 2 * NG
        FULL = NS - 1
        LASTW = NG - 1 - FULL * ST

        def late(p):
            return (p + 1) * (2 * ST) + 2 * LAG

        def schedule(eng, steps):
            super_turn(steps, 0)
            super_turn(steps, 1, 0, None, nodes_done=late(0))
            super_turn(steps, 2, 1, 0, nodes_done=late(1))
            with eng.Fori(3, FULL) as s:
                super_turn(steps, s, s - 1, s - 2, nodes_done=late(s - 1))
            super_turn(steps, FULL, FULL - 1, FULL - 2, LASTW, nodes_done=late(FULL - 1))
            super_turn(steps, None, NC - 1, NC - 2, nodes_done=ALL)
            super_turn(steps, None, None, NC - 1)

        def edges_only(eng, steps):
            super_turn(steps, 0)
            with eng.Fori(1, FULL) as s:
                super_turn(steps, s)
            super_turn(steps, FULL, windows=LASTW)

        def experts_only(eng, steps):
            super_turn(steps, None, 0, nodes_done=ALL)
            super_turn(steps, None, 1, 0, nodes_done=ALL)
            with eng.Fori(2, NC) as p:
                super_turn(steps, None, p, p - 1, nodes_done=ALL)
            super_turn(steps, None, None, NC - 1)

        with nc.Block() as block:
            @block.sync
            def _(sp):
                for e in range(X):
                    for w, to in ((w1, w1_sb), (w2, w2_sb)):
                        o = e * KC * D
                        sp.dma_start(to[:, o:o + KC * D].rearrange("p (k f) -> p k f", k=KC),
                                     w[e].rearrange("(k p) f -> p k f", p=P)).then_inc(experts_in, 16)
                with sp.Fori(0, NC - 1) as c:
                    sp.wait_ge(y_done, c * (X * TC) + X * TC)
                    sp.dma_start(out[ds(c * TOK, TOK), :].rearrange("(t p) d -> p t d", p=P),
                                 x_sb[:, ds(c * (TC * D), TC * D)].rearrange("p (t d) -> p t d", d=D)).then_inc(out_done, 16)
                sp.wait_ge(y_done, NC * X * TC)
                n = (NC - 1) * TC
                sp.dma_start(out[n * P:(NT - 1) * P, :].rearrange("(t p) d -> p t d", p=P),
                             x_sb[:, n * D:(NT - 1) * D].rearrange("p (t d) -> p t d", d=D)).then_inc(out_done, 16)
                sp.dma_start(out[(NT - 1) * P:N, :], x_sb[0:NLAST, (NT - 1) * D:NT * D]).then_inc(out_done, 16)
                sp.wait_ge(out_done, 16 * (NC + 1))
                sp.wait_ge(experts_in, 32 * X)

            @block.gpsimd
            def _(pool):
                for k in range(EARLY, FR):
                    gather_feats(pool, k, P)

                def gather_window(i, n, tiles=G, rows=P):
                    pool.wait_ge(feat_idx, (i - 1) * ST + n + 1)
                    pool.nop(nofuse=True)
                    for j in range(tiles):
                        gather_feats(pool, n * G + j, rows)

                with pool.Fori(1, FULL) as i:
                    for n in range(ST):
                        gather_window(i, n)
                for n in range(LASTW):
                    gather_window(FULL, n)
                gather_window(FULL, LASTW, 1, ELAST)
                with pool.If(irregular(pool) == 1):
                    pool.wait_ge(acc_step, ALL)
                    pool.iota(iota_n, pattern=[[1, WIN]], base=0, channel_multiplier=0,
                              allow_small_or_imprecise_dtypes=True).then_inc(far_iota, 1)
                    with pool.Fori(0, ET) as t:
                        pool.wait_ge(far_idx, t + 1)
                        pool.nop(nofuse=True)
                        pool.indirect_dma_start(feats(0), None, feat_tab[:, :],
                                                bass.IndirectOffsetOnAxis(ap=feat_rows[:, 0:1], axis=0))\
                            .then_inc(far_in, 16)

            @block.scalar
            def _(act):
                def window(s, n):
                    if isinstance(s, int) and s == FULL:
                        return
                    act.wait_ge(agg_done, s * ST + (n + 1))
                    act.activation(feat_rows[:, n * G:(n + 1) * G],
                                   idx_l[:, ds(s * FR + (n + ST) * G, G)], ACT.Copy).then_inc(feat_idx, 1)

                def h_copy(p, nodes_done):
                    act.wait_ge(acc_step, nodes_done)
                    wait(act, x2_psum, p)
                    for k in range(KC):
                        act.activation(hs[:, k * TOK:(k + 1) * TOK], acc[:, ds(p * TOK + k * NP_, TOK)],
                                       ACT.Identity, bias=hb[:, k:k + 1]).then_inc(hs_done, 1)

                def std(p):
                    act.wait_ge(var2_done, p + 1)
                    act.activation(rs2[:, :], rs2[:, :], ACT.Sqrt).then_inc(std2_done, 1)

                def xlT_copy(p):
                    act.wait_ge(xlT_psum, p + 1)
                    wait(act, score_psum, p)
                    wait(act, xlT_kept, p)
                    for k in range(KC):
                        act.activation(xlT_next[:, k * TOK:(k + 1) * TOK], psum[6 + k][:, 0:TOK], ACT.Copy)\
                           .then_inc(xlT_done, 1)

                def xlT_keep(p):
                    act.wait_ge(xlT_done, p * 2 + 2)
                    wait(act, h_psum, p * (2 * X))
                    act.activation(xlT, xlT_next, ACT.Copy).then_inc(xlT_kept, 1)

                def score_copy(p):
                    act.wait_ge(score_psum, p + 1)
                    wait(act, scoreT_psum, p)
                    act.activation(scT[0:X, :], psum[6][0:X, 0:TOK], ACT.Copy).then_inc(score_done, 1)

                def exp(p):
                    act.wait_ge(score_shift, p + 1)
                    act.activation(expo, expo, ACT.Exp).then_inc(score_exp, 1)

                def weight_copy(p):
                    act.wait_ge(combT_psum, p + 1)
                    wait(act, b2_psum, p)
                    act.activation(combT[0:X, :], psum[6][0:X, 0:TOK], ACT.Copy).then_inc(combT_done, 1)

                def up(c, e):
                    for f in range(KC):
                        act.wait_ge(h_psum, c * (2 * X) + (2 * e + f + 1))
                        wait(act, y_psum, c * (TC * X) + TC * (e - 1))
                        o = (e % 2 * 2 + f) * TOK
                        act.activation(hT[:, o:o + TOK], psum[2 + f][:, 0:TOK], ACT.Gelu,
                                       bias=b1_sb[:, e * KC + f:e * KC + f + 1]).then_inc(h_done, 1)

                steps = dict(window=window, h_copy=h_copy, std=std, xlT_copy=xlT_copy, score_copy=score_copy, exp=exp,
                             weight_copy=weight_copy,
                             xlT_keep=xlT_keep, up=up)
                act.wait_ge(rwT_psum, 1)
                act.activation(rwT[:, :], psum[6][:, 0:KC * X], ACT.Copy).then_inc(rwT_done, 1)
                flag = irregular(act)
                with act.If(flag == 0):
                    schedule(act, steps)
                with act.If(flag == 1):
                    edges_only(act, steps)
                    with act.Fori(0, ET) as t:
                        act.wait_ge(far_sum, t * (NW * H) + 1)
                        act.activation(feat_rows[:, 0:1], idx_l[:, ds(t, 1)], ACT.Copy).then_inc(far_idx, 1)
                    act.wait_ge(far_add, ET * NW * H + 1)
                    experts_only(act, steps)

            @block.vector
            def _(dve):
                def build(g, k):
                    wait(dve, agg_done, g - (HOTS - 1))
                    o = (k % 2) * G * W
                    hv = hot[:, o:o + G * W].rearrange("p (j w) -> p j w", j=G)
                    dve.tensor_tensor(hv, iota_w[:, :].unsqueeze(1).to_broadcast([P, G, W]),
                                      rel[:, ds(g * G, G)].unsqueeze(2).to_broadcast([P, G, W]), ALU.is_equal)\
                       .then_inc(hot_done, 1)
                    dve.wait_ge(hot_done, g + 1)
                    o = k * G * H * W
                    dve.tensor_tensor(hot_a[:, o:o + G * H * W].rearrange("p (j h w) -> p j h w", j=G, h=H),
                                      hv.unsqueeze(2).to_broadcast([P, G, H, W]),
                                      alpha[:, ds(g * (G * H), G * H)].rearrange("p (j h) -> p j h", h=H).unsqueeze(3)
                                      .to_broadcast([P, G, H, W]), ALU.mult).then_inc(hot_a_done, 1)

                def add_window(g, k):
                    base = dve.value_load(base_i[0:1, ds(g, 1)], min_val=0, max_val=N - 1)
                    dve.wait_ge(agg_done, g + 1)
                    wait(dve, acc_step, g * 2)
                    pv = psum[k % 2][:, 0:2 * KC * W].rearrange("p (k h w) -> p k h w", k=KC, h=2)
                    for half in range(2):
                        q = slice(half * HD, half * HD + HD)
                        dve.tensor_tensor(accv[q, :, ds(base, W)], accv[q, :, ds(base, W)], pv[q, :, half, :], ALU.add)\
                           .then_inc(acc_step, 1)

                def window(s, n):
                    if not (isinstance(s, int) and s * ST + n + 2 >= NG):
                        build(s * ST + (n + 2), (n + 2) % HOTS)
                    add_window(s * ST + n, n % 2)

                def last_window():
                    add_window(NG - 1, 0)

                def x2_(p):
                    dve.wait_ge(x2_psum, p + 1)
                    wait(dve, base_done, p)
                    for b, (j, m) in enumerate(((0, 2), (2, 1))):
                        dve.tensor_tensor(x2[:, j * D:(j + m) * D], psum[6 + b][:, 0:m * D],
                                          x_sb[:, ds(p * (TC * D) + j * D, m * D)], ALU.add).then_inc(x2_done, 1)
                    dve.wait_ge(x2_done, p * 2 + 2)
                    for j in range(TC):
                        dve.bn_stats(st2[:, 6 * j:6 * j + 6], x2[:, j * D:(j + 1) * D]).then_inc(stats_done, 1)
                    dve.wait_ge(stats_done, p * TC + TC)
                    dve.nop(nofuse=True)
                    for j in range(TC):
                        dve.bn_aggr(mv2[:, 2 * j:2 * j + 2], st2[:, 6 * j:6 * j + 6]).then_inc(mv_done, 1)
                    dve.wait_ge(mv_done, p * TC + TC)
                    dve.tensor_scalar(rs2[:, :], mv2[:, 1::2], EPS, None, ALU.add).then_inc(var2_done, 1)

                def xl_(p):
                    dve.wait_ge(std2_done, p + 1)
                    dve.reciprocal(rs2[:, :], rs2[:, :]).then_inc(rs_done, 1)
                    dve.wait_ge(rs_done, p + 1)
                    wait(dve, xlT_psum, p)
                    for j in range(TC):
                        dve.tensor_scalar(xl[:, j * D:(j + 1) * D], x2[:, j * D:(j + 1) * D], mv2[:, 2 * j:2 * j + 1],
                                          rs2[:, j:j + 1], ALU.subtract, ALU.mult).then_inc(xl_done, 1)
                    dve.wait_ge(xl_done, p * TC + TC)
                    dve.tensor_tensor(x_sb[:, ds(p * (TC * D), TC * D)], x2, xl, ALU.add).then_inc(base_done, 1)

                def v(a):
                    return a.rearrange("p (t e) -> p t e", e=X)

                def wide(a):
                    return a.unsqueeze(2).to_broadcast([P, TC, X])

                def shift(p):
                    sc = v(psum[7][:, 0:TC * X])
                    dve.wait_ge(scoreT_psum, p + 1)
                    dve.tensor_reduce(mx, sc, AX.X, ALU.max).then_inc(score_max, 1)
                    dve.wait_ge(score_max, p + 1)
                    dve.tensor_tensor(v(expo), sc, wide(mx), ALU.subtract).then_inc(score_shift, 1)

                def links(counter, per, p):
                    n = [0]

                    def link(ins):
                        n[0] += 1
                        assert n[0] <= per
                        ins.then_inc(counter, 1)
                        dve.wait_ge(counter, p * per + n[0])
                        dve.nop(nofuse=True)
                    return link

                def route(p):
                    link = links(router_step, 5, p)
                    dve.wait_ge(score_exp, p + 1)
                    link(dve.tensor_reduce(mx, v(expo), AX.X, ALU.add))
                    link(dve.reciprocal(mx, mx))
                    link(dve.tensor_tensor(v(probs), v(expo), wide(mx), ALU.mult))
                    for t in range(TC):
                        last = dve.max(top[:, t * X:(t + 1) * X], probs[:, t * X:(t + 1) * X])
                    link(last)
                    for t in range(TC):
                        last = dve.max_index(top_i[:, t * X:(t + 1) * X], top[:, t * X:(t + 1) * X],
                                             probs[:, t * X:(t + 1) * X])
                    link(last)

                def combine(p):
                    link = links(combine_step, 6, p)
                    tv, iv = v(top), v(top_f)
                    dve.tensor_copy(top_f, top_i)
                    link(dve.tensor_tensor(mx, tv[:, :, 0], tv[:, :, 1], ALU.add))
                    link(dve.tensor_scalar(mx, mx, 1e-12, None, ALU.max))
                    link(dve.reciprocal(mx, mx))
                    for k in range(2):
                        last = dve.tensor_tensor(wt[:, k * TC:(k + 1) * TC], tv[:, :, k], mx, ALU.mult)
                    link(last)
                    for k, c in enumerate((expo, pick)):
                        last = dve.tensor_tensor(v(c), iota_w[:, 0:X].unsqueeze(1).to_broadcast([P, TC, X]),
                                                 wide(iv[:, :, k]), ALU.is_equal)
                    link(last)
                    for k, c in enumerate((expo, pick)):
                        last = dve.tensor_tensor(v(c), v(c), wide(wt[:, k * TC:(k + 1) * TC]), ALU.mult)
                    link(last)
                    wait(dve, combT_psum, p)
                    dve.tensor_tensor(comb[:, ds(p * (TC * X), TC * X)], expo, pick, ALU.add)
                    dve.tensor_tensor(comb_c, expo, pick, ALU.add).then_inc(comb_done, 1)

                def bias2_add(p):
                    dve.wait_ge(b2_psum, p + 1)
                    wait(dve, base_done, p + 1)
                    for b, (j, m) in enumerate(((0, 2), (2, 1))):
                        to = x_sb[:, ds(p * (TC * D) + j * D, m * D)]
                        dve.tensor_tensor(to, psum[6 + b][:, 0:m * D], to, ALU.add).then_inc(b2_done, 1)

                def down(c, e):
                    if e == 0:
                        dve.wait_ge(b2_done, c * 2 + 2)
                    for j in range(TC):
                        q = TC * e + j
                        dve.wait_ge(y_psum, c * (TC * X) + (q + 1))
                        if e:
                            dve.wait_ge(y_done, c * (TC * X) + (q - TC + 1))
                        to = x_sb[:, ds(c * (TC * D) + j * D, D)]
                        dve.scalar_tensor_tensor(to, psum[4 + q % 2][:, 0:D], comb[:, ds(c * (TC * X) + (j * X + e), 1)],
                                                 to, ALU.mult, ALU.add).then_inc(y_done, 1)

                steps = dict(window=window, last_window=last_window, x2=x2_, xl=xl_, shift=shift, route=route,
                             combine=combine,
                             bias2_add=bias2_add, down=down)
                build(0, 0)
                build(1, 1)
                flag = irregular(dve)
                with dve.If(flag == 0):
                    schedule(dve, steps)
                with dve.If(flag == 1):
                    edges_only(dve, steps)
                    dve.wait_ge(acc_step, ALL)
                    with dve.Fori(0, ET) as t:
                        dve.wait_ge(far_sum, t * (NW * H) + 1)
                        dve.tensor_scalar(far_d[:, 0:1], rel[:, ds(t, 1)], float(W), None, ALU.is_ge).then_inc(far_mask, 1)
                        dve.wait_ge(far_mask, t * (NW + 2) + 1)
                        dve.tensor_scalar(far_a, alpha[:, ds(t * H, H)], far_d[:, 0:1], None, ALU.mult)\
                           .then_inc(far_mask, 1)
                        dve.wait_ge(far_mask, t * (NW + 2) + 2)
                        for w in range(NW):
                            dve.tensor_scalar(far_d[:, w:w + 1], dst_t[:, ds(t, 1)], float(-w * WIN), None, ALU.add)\
                               .then_inc(far_mask, 1)
                        dve.wait_ge(far_mask, t * (NW + 2) + (NW + 2))
                        dve.wait_ge(far_iota, 1)
                        for w in range(NW):
                            for h in range(H):
                                n = w * H + h
                                b = n % 2
                                if n >= 2:
                                    dve.wait_ge(far_sum, t * (NW * H) + n)
                                dve.tensor_scalar(hot_n[:, b * WIN:(b + 1) * WIN], iota_n, far_d[:, w:w + 1],
                                                  far_a[:, h:h + 1], ALU.is_equal, ALU.mult).then_inc(far_hot, 1)
                                dve.wait_ge(far_sum, t * (NW * H) + (n + 2))
                                q = slice((h % 2) * HD, (h % 2 + 1) * HD)
                                to = accv[q, h // 2, w * WIN:(w + 1) * WIN]
                                dve.wait_ge(far_add, t * (NW * H) + (n + 1))
                                dve.tensor_tensor(to, to, psum[b][q, 0:WIN], ALU.add).then_inc(far_add, 1)
                    experts_only(dve, steps)

            @block.tensor
            def _(pe):
                def window(s, n, tiles=G, rows=P):
                    g = s * ST + n
                    pe.wait_ge(hot_a_done, g + 1)
                    pe.wait_ge(feats_in[n], s * (16 * G) + 16 * tiles)
                    wait(pe, acc_step, g * 2 - 2)
                    for q in range(KC):
                        for j in range(tiles):
                            o = ((n % HOTS * G + j) * H + 2 * q) * W
                            last = pe.matmul(psum[n % 2][:, q * 2 * W:(q + 1) * 2 * W],
                                             feats(n * G + j)[0:rows, q * P:(q + 1) * P],
                                             hot_a[0:rows, o:o + 2 * W], start=j == 0, stop=j == tiles - 1)
                    last.then_inc(agg_done, 1)

                def last_window():
                    window(FULL, LASTW, 1, ELAST)

                def h_transpose(p):
                    pe.wait_ge(hs_done, p * 2 + 2)
                    wait(pe, b2_done, p * 2)
                    for j in range(TC):
                        for k in range(KC):
                            o = (j % 2) * D + k * P
                            last = pe.transpose(psum[6 + j // 2][:, o:o + P], hs[:, k * TOK + j * P:k * TOK + (j + 1) * P],
                                                ident[:, :])
                    last.then_inc(x2_psum, 1)

                def xl_transpose(p):
                    pe.wait_ge(xl_done, p * TC + TC)
                    pe.wait_ge(x2_done, p * 2 + 2)
                    for k in range(KC):
                        for j in range(TC):
                            last = pe.transpose(psum[6 + k][:, j * P:(j + 1) * P], xl[:, j * D + k * P:j * D + (k + 1) * P],
                                                ident[:, :])
                    last.then_inc(xlT_psum, 1)

                def scores(p):
                    pe.wait_ge(xlT_done, p * 2 + 2)
                    for k in range(KC):
                        last = pe.matmul(psum[6][0:X, 0:TOK], rwT[:, k * X:(k + 1) * X], xlT_next[:, k * TOK:(k + 1) * TOK],
                                         start=k == 0, stop=k == KC - 1)
                    last.then_inc(score_psum, 1)

                def score_transpose(p):
                    pe.wait_ge(score_done, p + 1)
                    pe.nop(nofuse=True)
                    for t in range(TC):
                        last = pe.transpose(psum[7][:, t * X:(t + 1) * X], scT[0:X, t * P:(t + 1) * P], ident[0:X, 0:X])
                    last.then_inc(scoreT_psum, 1)

                def weight_transpose(p):
                    pe.wait_ge(comb_done, p + 1)
                    for t in range(TC):
                        last = pe.transpose(psum[6][0:X, t * P:(t + 1) * P], comb_c[:, t * X:(t + 1) * X], ident[:, :])
                    last.then_inc(combT_psum, 1)

                def bias2(p):
                    pe.wait_ge(combT_done, p + 1)
                    pe.wait_ge(score_shift, p + 1)
                    for t in range(TC):
                        last = pe.matmul(psum[6 + t // 2][:, (t % 2) * D:(t % 2 + 1) * D], combT[0:X, t * P:(t + 1) * P],
                                         b2_sb[:, :], start=True, stop=True)
                    last.then_inc(b2_psum, 1)

                def up(c, e):
                    if e == 0:
                        pe.wait_ge(xlT_kept, c + 1)
                        pe.wait_ge(experts_in, 32 * X)
                    for f in range(KC):
                        wait(pe, h_done, c * (2 * X) + (2 * e + f - 1))
                        for k in range(KC):
                            o = (e * KC + k) * D + f * P
                            last = pe.matmul(psum[2 + f][:, 0:TOK], w1_sb[:, o:o + P], xlT[:, k * TOK:(k + 1) * TOK],
                                             start=k == 0, stop=k == KC - 1)
                        last.then_inc(h_psum, 1)

                def down(c, e):
                    pe.wait_ge(h_done, c * (2 * X) + (2 * e + 2))
                    for j in range(TC):
                        q = TC * e + j
                        wait(pe, y_done, c * (TC * X) + (q - 1))
                        for f in range(KC):
                            o = (e % 2 * 2 + f) * TOK + j * P
                            last = pe.matmul(psum[4 + q % 2][:, 0:D], hT[:, o:o + P],
                                             w2_sb[:, (e * KC + f) * D:(e * KC + f + 1) * D],
                                             start=f == 0, stop=f == KC - 1)
                        last.then_inc(y_psum, 1)

                steps = dict(window=window, last_window=last_window, h_transpose=h_transpose, xl_transpose=xl_transpose,
                             scores=scores, score_transpose=score_transpose, weight_transpose=weight_transpose,
                             bias2=bias2, up=up, down=down)
                for k in range(KC):
                    last = pe.transpose(psum[6][:, k * X:(k + 1) * X], rw_sb[:, k * P:(k + 1) * P], ident[0:X, 0:X])
                last.then_inc(rwT_psum, 1)
                pe.wait_ge(rwT_done, 1)
                flag = irregular(pe)
                with pe.If(flag == 0):
                    schedule(pe, steps)
                with pe.If(flag == 1):
                    edges_only(pe, steps)
                    pe.wait_ge(acc_step, ALL)
                    pe.transpose(psum[0][0:1, 0:P], far_col[:, :], ident[:, :]).then_inc(far_sum, 1)
                    pe.wait_ge(far_sum, 1)
                    pe.transpose(psum[0][0:1, 0:P], far_col[:, :], ident[:, :]).then_inc(far_add, 1)
                    with pe.Fori(0, ET) as t:
                        pe.wait_ge(far_in, t * 16 + 16)
                        for w in range(NW):
                            for h in range(H):
                                n = w * H + h
                                b = n % 2
                                pe.wait_ge(far_hot, t * (NW * H) + (n + 1))
                                pe.wait_ge(far_add, t * (NW * H) + (n if n else 1))
                                o = (h // 2) * P
                                pe.matmul(psum[b][:, 0:WIN], feats(0)[:, o:o + P], hot_n[:, b * WIN:(b + 1) * WIN],
                                          start=True, stop=True).then_inc(far_sum, 1)
                    experts_only(pe, steps)
    return nc


_INS = ["x", "src", "dst", "edge_type_8", "L0_gnn_conv_weights", "L0_gnn_attn_l", "L0_gnn_attn_r", "L0_gnn_h_bias",
        "L0_ffn_router_w", "L0_ffn_w1", "L0_ffn_b1", "L0_ffn_w2", "L0_ffn_b2"]


def kernel(**inputs):
    import numpy as _np
    import concourse.bacc as _bacc
    from concourse import mybir as _mybir
    from concourse.bass_utils import run_bass_kernel_spmd as _run

    nc = _bacc.Bacc("TRN2", target_bir_lowering=False, num_devices=1)
    arrays, args = {}, []
    for name in _INS:
        a = _np.ascontiguousarray(inputs[name])
        arrays[f"in_{name}_dram"] = a
        args.append(nc.dram_tensor(f"in_{name}_dram", a.shape, _mybir.dt.from_np(a.dtype), kind="ExternalInput").ap())
    args.append(nc.dram_tensor("out_0_dram", (N, D), _mybir.dt.float32, kind="ExternalOutput").ap())
    gnn_moe(nc, *args)
    r = _run(nc, [arrays], core_ids=[0])
    return r.results[0]["out_0_dram"]
```

```python
import concourse.bass as bass
from concourse import mybir
from contextlib import ExitStack

F32 = mybir.dt.float32
I32 = mybir.dt.int32
U32 = mybir.dt.uint32
ALU = mybir.AluOpType
ACT = mybir.ActivationFunctionType
AX = mybir.AxisListType

P = 128
N, D = 3750, 256
NT = (N + P - 1) // P
NP_ = NT * P
NLAST = N - (NT - 1) * P
E = 60000
R, H, HD = 8, 4, 64
RH, RHD = R * H, R * H * HD
KC = D // P
ET = (E + P - 1) // P
ELAST = E - (ET - 1) * P
C, J = 32, 15
ETP = C * J
L = J * P
G = 3
W = 32
NG = (ET + G - 1) // G
GPI = 4
RING = GPI * G
TURNS2 = ETP // RING
HOTS = 4
ST = 16
NS = (NG + ST - 1) // ST
LAG = 4
FR = ST * G
NEAR = 32
EPS = 1e-5
BIG = 1e30
X = 8
TC = 3
NC = NT // TC
TOK = TC * P
SG = 39
WORK = 18640


def gnn_moe(nc, x, src, dst, etype, conv_w, attn_l, attn_r, h_bias, router_w, w1, b1, w2, b2, out):
    assert TURNS2 % 2 == 0 and GPI * W == P and (ET - 1) % G == 0 and NT % 6 == 0 and ETP >= ET
    ctx = ExitStack()
    with ctx:
        ctx.enter_context(nc.allow_non_contiguous_dma(reason="a few hundred window bases and small weights"))

        def sb(name, shape, dt=F32):
            return ctx.enter_context(nc.sbuf_tensor(name, shape, dt))

        def sem(name):
            return ctx.enter_context(nc.semaphore(name))

        ds = bass.ds
        feat_tab = nc.dram_tensor("feat_tab", [NP_ * R, D], F32)
        el_tab = nc.dram_tensor("el_tab", [NP_ * R, H], F32)
        er_tab = nc.dram_tensor("er_tab", [NP_ * R, H], F32)

        ident = sb("ident", [P, P])
        ones = sb("ones", [P, P])
        x_sb = sb("x_sb", [P, NT * D])
        acc = sb("acc", [P, KC * NP_])
        weights = sb("weights", [P, KC * RHD + 2 * RHD])
        work = sb("work", [P, WORK])
        alpha = sb("alpha", [P, ETP * H])
        feat_rows = sb("feat_rows", [P, FR], I32)
        el = sb("el", [P, ETP * H])
        er = sb("er", [P, ETP * H])
        far_col = sb("far_col", [P, 1])
        far_row = sb("far_row", [1, NS])
        far_i = sb("far_i", [1, 1], I32)
        score_ring = sb("score_ring", [P, 2 * SG * H])
        idx_l = sb("idx_l", [P, 4 * P], I32)
        idx_r = sb("idx_r", [P, 4 * P], I32)
        idx_ring = sb("idx_ring", [P, 2 * SG], I32)
        dst_t = sb("dst_t", [P, 4 * P])
        rel = sb("rel", [P, ETP])
        base_i = sb("base_i", [1, TURNS2 * GPI], I32)
        base_f = sb("base_f", [1, NG])
        stats = sb("stats", [P, NT * 6])
        mv = sb("mv", [P, NT * 2])
        rstd = sb("rstd", [P, NT])
        iota_w = sb("iota_w", [P, W])
        hb = sb("hb", [P, KC])
        b1_sb = sb("b1_sb", [P, X * KC])
        b2_sb = sb("b2_sb", [X, D])
        rw_sb = sb("rw_sb", [X, D])
        rwT = sb("rwT", [P, KC * X])

        psum = [ctx.enter_context(nc.psum_tensor(f"bank{i}", [P, 512], F32)) for i in range(8)]

        def carve(start, n):
            return work[:, start:start + n], start + n

        late_feats, _ = carve(WORK - (FR - NEAR) * D, (FR - NEAR) * D)

        wconv = weights[:, 0:KC * RHD]
        fout = weights[:, KC * RHD:KC * RHD + 2 * RHD]
        att_l, o = carve(0, RHD)
        att_r, o = carve(o, RHD)
        prods = [acc[:, k * RHD:(k + 1) * RHD] for k in range(KC)]
        prod, o = carve(o, RHD)
        wa, o = carve(o, KC * 2 * RH)
        rowi_f, o = carve(o, 3 * 4 * P)
        rowi = rowi_f.bitcast(I32)
        rowf, o = carve(o, 3 * 4 * P)
        rowx, o = carve(o, 2 * 4 * P)
        xn, o = carve(o, 4 * D)
        xT, o = carve(o, 4 * D)
        elr, o = carve(o, NT * 2 * RH)
        hot_e, o = carve(o, 2 * G * P)
        hotT, o = carve(o, 2 * G * P)
        er_win, o = carve(o, 2 * P)
        rel_mask, o = carve(o, RING * R)
        er_all, o = carve(o, RING * RH)
        typ, o = carve(o, 4 * P)
        assert o <= WORK, o
        dstf, o = carve(0, L + 2)
        same, o = carve(o, L + 2)
        pen, o = carve(o, L + 2)
        ebulk, o = carve(o, L)
        dsti_f, _ = carve(o, L + 2)
        dsti = dsti_f.bitcast(I32)
        fwd, o = carve(o, L)
        bwd, o = carve(o, L)
        e_ht, o = carve(o, L)
        assert o <= WORK - (FR - NEAR) * D, o
        edge_col = sb("edge_col", [P, 8])
        edge_row = sb("edge_row", [1, 4 * P])
        scan_row = sb("scan_row", [1, 2 * (P + 2)])
        carry = sb("carry", [P, 2])

        const_done = sem("const_done")
        pool_step = sem("pool_step")
        XS = NT // 3
        x_in = [sem(f"x_in{i}") for i in range(3)]
        prod_done = sem("prod_done")
        w_in = [sem(f"w_in{k}") for k in range(KC)]
        attn_in = sem("attn_in")
        rows_in = sem("rows_in")
        base_in = sem("base_in")
        dstb_in = sem("dstb_in")
        small_in = sem("small_in")
        dve_step = sem("dve_step")
        xn_done = sem("xn_done")
        var_done = sem("var_done")
        std_done = sem("std_done")
        rows_done = sem("rows_done")
        rowsT_done = sem("rowsT_done")
        idx_done = sem("idx_done")
        rel_done = sem("rel_done")
        far_col_done = sem("far_col_done")
        far_psum = sem("far_psum")
        flag_done = sem("flag_done")
        wa_done = sem("wa_done")
        xn_done2 = sem("xn_done2")
        xt_done2 = sem("xt_done2")
        xt_copied2 = sem("xt_copied2")
        xt_done = sem("xt_done")
        xt_copied = sem("xt_copied")
        el_done = sem("el_done")
        el_copied = sem("el_copied")
        el_tab_out = sem("el_tab_out")
        er_tab_out = sem("er_tab_out")
        feat_done = sem("feat_done")
        feat_act = sem("feat_act")
        feat_dve = sem("feat_dve")
        feat_out = [sem(f"feat_out{u}") for u in range(2)]
        (er_win_clear, typ_psum, hot_e_done, hotT_psum, hotT_done, er_psum, mask_done, er_picked, er_done, score_sum,
         far_er_idx, far_er_in, far_er_done) = [sem(n) for n in """er_win_clear typ_psum hot_e_done hotT_psum hotT_done
            er_psum mask_done er_picked er_done score_sum far_er_idx far_er_in far_er_done""".split()]
        er_win_in = [sem(f"er_win_in{u}") for u in range(2)]
        gathered = [sem(f"gathered{s}") for s in range(2)]
        scores_done = sem("scores_done")
        idx_copied = sem("idx_copied")
        dstb_clear = sem("dstb_clear")
        eht_done = sem("eht_done")
        ebulk_psum = sem("ebulk_psum")
        ebulk_done = sem("ebulk_done")
        cols_done = sem("cols_done")
        rows_psum = sem("rows_psum")
        srow_done = sem("srow_done")
        carry_psum = sem("carry_psum")
        shifted = sem("shifted")
        exp_done = sem("exp_done")
        last_el_in = sem("last_el_in")
        alpha_bulk = sem("alpha_bulk")
        alpha_psum = sem("alpha_psum")

        rows_copied = sem("rows_copied")
        feats_in = [sem(f"feats_in{k}") for k in range(ST)]

        def feats(k):
            if k < NEAR:
                return weights[:, k * D:(k + 1) * D]
            return late_feats[:, (k - NEAR) * D:(k - NEAR + 1) * D]

        def gather_feats(pool, k, n):
            pool.indirect_dma_start(feats(k)[0:n, :], None, feat_tab[:, :],
                                    bass.IndirectOffsetOnAxis(ap=feat_rows[0:n, k:k + 1], axis=0))\
                .then_inc(feats_in[k // G], 16)

        x_tiles = x[0:(NT - 1) * P, :].rearrange("(t p) d -> p t d", p=P)

        def irregular(eng):
            return eng.value_load(far_i[0:1, 0:1], min_val=0, max_val=1)

        PAIRS = NT // 2
        with nc.Block() as block:
            @block.sync
            def _(sp):
                for i in range(3):
                    a, b = i * XS, min((i + 1) * XS, NT - 1)
                    sp.dma_start(x_sb[:, a * D:b * D].rearrange("p (t d) -> p t d", d=D), x_tiles[:, a:b])\
                      .then_inc(x_in[i], 16)
                sp.wait_ge(const_done, 1)
                sp.dma_start(x_sb[0:NLAST, (NT - 1) * D:NT * D], x[(NT - 1) * P:N, :]).then_inc(x_in[2], 16)
                for s, a in enumerate((src, dst, etype)):
                    full = rowi[:, s * 4 * P:s * 4 * P + 3 * P].rearrange("t (b p) -> t b p", p=P)
                    sp.dma_start(full, a[0:3 * P * P].rearrange("(b t p) -> t b p", b=3, p=P)).then_inc(rows_in, 16)
                    rest = ET - 1 - 3 * P
                    last = rowi[:, (s * 4 + 3) * P:(s * 4 + 4) * P]
                    sp.dma_start(last[0:rest, :], a[3 * P * P:(ET - 1) * P].rearrange("(t p) -> t p", p=P))\
                      .then_inc(rows_in, 16)
                    sp.dma_start(last[rest:rest + 1, 0:ELAST], a[(ET - 1) * P:E].rearrange("(t p) -> t p", t=1))\
                      .then_inc(rows_in, 16)
                step = G * P
                sp.dma_start(base_i[0:1, 0:NG - 1], dst[0:(NG - 1) * step].rearrange("(g e) -> e g", e=step)[0:1, :])\
                  .then_inc(base_in, 16)
                sp.dma_start(base_i[0:1, NG - 1:NG], dst[(NG - 1) * step:(NG - 1) * step + 1]
                             .rearrange("(a b) -> a b", a=1)).then_inc(base_in, 16)
                sp.dma_start(hb[:, :], h_bias.rearrange("(k p) -> p k", p=P)).then_inc(small_in, 16)
                sp.dma_start(b1_sb[:, :].rearrange("p (e k) -> p e k", k=KC), b1.rearrange("e (k p) -> p e k", p=P))\
                  .then_inc(small_in, 16)
                sp.dma_start(b2_sb[:, :], b2).then_inc(small_in, 16)
                sp.dma_start(rw_sb[:, :], router_w).then_inc(small_in, 16)
                sp.wait_ge(small_in, 64)
                tabs = elr.rearrange("p (t s c) -> p t s c", s=2, c=RH)
                for a, b in ((0, NT - 2), (NT - 2, NT)):
                    sp.wait_ge(el_copied, b // 2)
                    sp.dma_start(el_tab[a * P * R:b * P * R, :].rearrange("(t p r) h -> p t (r h)", p=P, r=R),
                                 tabs[:, a:b, 0, :]).then_inc(el_tab_out, 16)
                sp.dma_start(er_tab[:, :].rearrange("(t p r) h -> p t (r h)", p=P, r=R), tabs[:, :, 1, :])\
                  .then_inc(er_tab_out, 16)
                with sp.Fori(0, NT // 2) as i:
                    for u in range(2):
                        sp.wait_ge(feat_act, i * 4 + 2 * u + 2)
                        sp.wait_ge(feat_dve, i * 4 + 2 * u + 2)
                        sp.dma_start(feat_tab[ds(i * (2 * P * R) + u * P * R, P * R), :]
                                     .rearrange("(p r) d -> p (r d)", r=R),
                                     fout[:, u * RHD:(u + 1) * RHD]).then_inc(feat_out[u], 16)
                for u in range(2):
                    sp.wait_ge(feat_out[u], 16 * (NT // 2))
                sp.wait_ge(er_tab_out, 16)
                sp.wait_ge(er_win_clear, 1)

                def er_windows(i, first):
                    for u in range(2):
                        if not first:
                            sp.wait_ge(er_psum, i * 2 + (u - 1))
                        for s in range(GPI):
                            base = sp.value_load(base_i[0:1, ds(i * (2 * GPI) + (u * GPI + s), 1)], min_val=0, max_val=N - 1)
                            sp.dma_start(er_win[s * W:(s + 1) * W, u * P + s * W:u * P + (s + 1) * W],
                                         er_tab[:, :].rearrange("(n r) h -> n (r h)", r=R)[ds(base, W), :])\
                              .then_inc(er_win_in[u], 16)

                er_windows(0, True)
                with sp.Fori(1, TURNS2 // 2) as i:
                    er_windows(i, False)
                sp.wait_ge(dstb_clear, 1)

                def row(a, b):
                    return dst[a:b].rearrange("(o n) -> o n", o=1)

                for h in range(H):
                    p = h * C
                    for to, frm in (
                        (dsti[p:p + 1, 1:L + 2], row(0, L + 1)),
                        (dsti[p + 1:p + C - 1, 0:L], dst[L - 1:(C - 1) * L - 1].rearrange("(c l) -> c l", l=L)),
                        (dsti[p + 1:p + C - 1, L:L + 1],
                         dst[L:(C - 1) * L].rearrange("(c l) -> c l", l=L)[:, L - 1:L]),
                        (dsti[p + 1:p + C - 2, L + 1:L + 2],
                         dst[2 * L:(C - 1) * L].rearrange("(c l) -> c l", l=L)[:, 0:1]),
                        (dsti[p + C - 2:p + C - 1, L + 1:L + 2], row((C - 1) * L, (C - 1) * L + 1)),
                        (dsti[p + C - 1:p + C, 0:E - (C - 1) * L + 1], row((C - 1) * L - 1, E)),
                    ):
                        sp.dma_start(to, frm).then_inc(dstb_in, 16)

            @block.gpsimd
            def _(pool):
                pool.memset(x_sb[:, (NT - 1) * D:NT * D], 0.0)
                pool.memset(base_i[:, :], 0)
                pool.memset(rowi, 0).then_inc(const_done, 1)
                pool.memset(ident[:, :], 0.0).then_inc(pool_step, 1)
                pool.memset(ones[:, :], 1.0)
                pool.iota(iota_w[:, :], pattern=[[1, W]], base=0, channel_multiplier=0,
                          allow_small_or_imprecise_dtypes=True)
                pool.wait_ge(pool_step, 1)
                pool.affine_select(out=ident[:, :], in_=ident[:, :], compare_op=ALU.not_equal, fill=1.0, base=0,
                                   pattern=[[-1, P]], channel_multiplier=1)
                tail = (ET - 1) * H
                pool.memset(el[:, tail:], 0.0).then_inc(const_done, 1)
                pool.wait_ge(const_done, 2)
                pool.wait_ge(attn_in, 32)
                for k in range(KC):
                    pool.wait_ge(w_in[k], 16 * R)
                    pool.tensor_tensor(prods[k], wconv[:, k * RHD:(k + 1) * RHD], att_r, ALU.mult).then_inc(prod_done, 1)
                pool.wait_ge(el_tab_out, 32)
                pool.wait_ge(idx_done, 1)


                def gather_turn(i, first):
                    for s in range(2):
                        n = i * (2 * SG) + s * SG
                        o = s * SG
                        if not first:
                            keep_scores(i, s, n - 2 * SG)
                        pool.tensor_copy(idx_ring[:, o:o + SG], idx_l[:, ds(n, SG)]).then_inc(idx_copied, 1)
                        pool.wait_ge(idx_copied, i * 2 + (s + 1))
                        pool.nop(nofuse=True)
                        for j in range(SG):
                            c = o + j
                            pool.indirect_dma_start(score_ring[:, c * H:(c + 1) * H], None, el_tab[:, :],
                                                    bass.IndirectOffsetOnAxis(ap=idx_ring[:, c:c + 1], axis=0))\
                                .then_inc(gathered[s], 16)

                def keep_scores(i, s, n):
                    pool.wait_ge(gathered[s], i * (16 * SG))
                    pool.tensor_copy(el[:, ds(n * H, SG * H)], score_ring[:, s * SG * H:(s + 1) * SG * H])\
                        .then_inc(scores_done, 1)

                turns = (ET - 1) // (2 * SG)
                gather_turn(0, True)
                with pool.Fori(1, turns) as i:
                    gather_turn(i, False)
                pool.indirect_dma_start(el[0:ELAST, tail:tail + H], None, el_tab[:, :],
                                        bass.IndirectOffsetOnAxis(ap=idx_l[0:ELAST, ET - 1:ET], axis=0))\
                    .then_inc(last_el_in, 16)
                for s in range(2):
                    keep_scores(turns, s, ET - 1 - 2 * SG + s * SG)
                pool.wait_ge(rows_copied, 1)
                for u in range(2):
                    pool.wait_ge(feat_out[u], 16 * (NT // 2))
                pool.wait_ge(er_done, TURNS2)
                for k in range(FR):
                    gather_feats(pool, k, P)
                pool.wait_ge(flag_done, 1)
                with pool.If(irregular(pool) == 1):
                    pool.wait_ge(scores_done, 2 * turns)
                    pool.wait_ge(er_done, TURNS2)
                    with pool.Fori(0, ET) as t:
                        pool.tensor_copy(idx_ring[:, 0:1], idx_r[:, ds(t, 1)]).then_inc(far_er_idx, 1)
                        pool.wait_ge(far_er_idx, t + 1)
                        pool.nop(nofuse=True)
                        pool.indirect_dma_start(score_ring[:, 0:H], None, er_tab[:, :],
                                                bass.IndirectOffsetOnAxis(ap=idx_ring[:, 0:1], axis=0))\
                            .then_inc(far_er_in, 16)
                        pool.wait_ge(far_er_in, t * 16 + 16)
                        pool.tensor_copy(er[:, ds(t * H, H)], score_ring[:, 0:H]).then_inc(far_er_done, 1)
                        pool.wait_ge(far_er_done, t + 1)

            @block.scalar
            def _(act):
                act.dma_start(att_l, attn_l.rearrange("r h d -> (r h d)").partition_broadcast(P)).then_inc(attn_in, 16)
                act.dma_start(att_r, attn_r.rearrange("r h d -> (r h d)").partition_broadcast(P)).then_inc(attn_in, 16)
                for k in range(KC):
                    for r in range(R):
                        o = k * RHD + r * H * HD
                        act.dma_start(wconv[:, o:o + H * HD].rearrange("p (h d) -> p h d", d=HD),
                                     conv_w[r, :, k * P:(k + 1) * P, :].rearrange("h p d -> p h d")).then_inc(w_in[k], 16)
                act.wait_ge(var_done, 1)
                act.activation(rstd[:, :], rstd[:, :], ACT.Sqrt).then_inc(std_done, 1)
                def copy_xt_pair(g, b):
                    act.wait_ge(xt_done, g + 1)
                    if not isinstance(g, int) or g >= 2:
                        act.wait_ge(el_done, g - 1)
                    act.activation(xT[:, b * 2 * D:(b + 1) * 2 * D], psum[4 + b][:, :], ACT.Copy).then_inc(xt_copied, 1)

                def copy_el(g, b):
                    act.wait_ge(el_done, g + 1)
                    act.activation(elr[:, ds(g * (4 * RH), 4 * RH)], psum[6 + b][:, 0:4 * RH], ACT.Copy)\
                       .then_inc(el_copied, 1)

                copy_xt_pair(0, 0)
                copy_xt_pair(1, 1)
                copy_el(0, 0)
                copy_xt_pair(2, 0)
                copy_el(1, 1)
                with act.Fori(0, (PAIRS - 3) // 2) as i:
                    for u in range(2):
                        copy_xt_pair(i * 2 + (u + 3), (u + 1) % 2)
                        copy_el(i * 2 + (u + 2), u)
                copy_el(PAIRS - 1, 0)

                def copy_xt(n, u):
                    act.wait_ge(xt_done2, n + 1)
                    act.activation(xT[:, u * D:(u + 1) * D], psum[6 + u][:, 0:D], ACT.Copy).then_inc(xt_copied2, 1)

                def turn(i, first, last):
                    for u in range(2):
                        if not first:
                            act.wait_ge(feat_out[u], i * 16)
                        for b in range(2):
                            act.wait_ge(feat_done, i * 8 + (4 * u + b + 1))
                            act.activation(fout[:, u * RHD + b * 512:u * RHD + (b + 1) * 512],
                                           psum[b][:, :], ACT.Copy).then_inc(feat_act, 1)
                        if not (last and u == 1):
                            copy_xt(i * 2 + (u + 1), (u + 1) % 2)

                copy_xt(0, 0)
                turn(0, True, False)
                with act.Fori(1, NT // 2 - 1) as i:
                    turn(i, False, False)
                turn(NT // 2 - 1, False, True)
                def hot_turn(i, first):
                    for u in range(2):
                        act.wait_ge(hotT_psum, i * 2 + (u + 1))
                        if not first:
                            act.wait_ge(er_psum, i * 2 + (u - 1))
                        act.activation(hotT[:, u * G * P:(u + 1) * G * P], psum[4 + u][:, 0:G * P], ACT.Copy)\
                           .then_inc(hotT_done, 1)

                hot_turn(0, True)
                with act.Fori(1, TURNS2 // 2) as i:
                    hot_turn(i, False)
                for b in range(4):
                    act.wait_ge(ebulk_psum, b + 1)
                    n = min(4, J - 4 * b) * P
                    act.activation(ebulk[:, b * 512:b * 512 + n], psum[b][:, 0:n], ACT.Copy).then_inc(ebulk_done, 1)
                act.wait_ge(shifted, 1)
                act.activation(bwd, ebulk, ACT.Exp).then_inc(exp_done, 1)
                av = alpha[:, :].rearrange("p (c j h) -> p j h c", j=J, h=H)
                for j in range(J):
                    act.wait_ge(alpha_psum, j // 4 + 1)
                    ap = psum[j // 4][:, (j % 4) * P:(j % 4 + 1) * P].rearrange("p (h c) -> p h c", h=H)
                    act.activation(av[:, j], ap, ACT.Copy)

            @block.vector
            def _(dve):
                step = [0]

                def link(ins):
                    step[0] += 1
                    ins.then_inc(dve_step, 1)
                    dve.wait_ge(dve_step, step[0])

                for i in range(3):
                    dve.wait_ge(x_in[i], 32 if i == 2 else 16)
                    for t in range(i * XS, (i + 1) * XS):
                        last = dve.bn_stats(stats[:, t * 6:t * 6 + 6], x_sb[:, t * D:(t + 1) * D])
                link(last)
                for t in range(NT):
                    last = dve.bn_aggr(mv[:, t * 2:t * 2 + 2], stats[:, t * 6:t * 6 + 6])
                link(last)
                mvv = mv[:, :].rearrange("p (t two) -> p t two", two=2)
                dve.tensor_scalar(rstd[:, :], mvv[:, :, 1], EPS, None, ALU.add).then_inc(var_done, 1)
                dve.wait_ge(std_done, 1)
                link(dve.reciprocal(rstd[:, :], rstd[:, :]))
                def fold(prod, k, s):
                    return dve.tensor_reduce(wa[:, (k * 2 + s) * RH:(k * 2 + s + 1) * RH],
                                             prod.rearrange("p (c d) -> p c d", d=HD), AX.X, ALU.add)

                dve.wait_ge(attn_in, 32)
                for k in range(KC):
                    dve.wait_ge(w_in[k], 16 * R)
                    link(dve.tensor_tensor(prod, wconv[:, k * RHD:(k + 1) * RHD], att_l, ALU.mult))
                    link(fold(prod, k, 0))
                    dve.wait_ge(prod_done, k + 1)
                    last = fold(prods[k], k, 1)
                link(last)

                def normalise(t, u, done):
                    dve.tensor_scalar(xn[:, u * D:(u + 1) * D], x_sb[:, ds(t * D, D)], mv[:, ds(t * 2, 1)],
                                      rstd[:, ds(t, 1)], ALU.subtract, ALU.mult).then_inc(done, 1)

                def normalise_pair(g, b):
                    if not isinstance(g, int) or g >= 2:
                        dve.wait_ge(xt_done, g - 1)
                    for u in range(2):
                        normalise(g * 2 + u, b * 2 + u, xn_done)

                normalise_pair(0, 0)
                normalise_pair(1, 1)
                with dve.Fori(1, PAIRS // 2) as i:
                    for b in range(2):
                        normalise_pair(i * 2 + b, b)
                normalise_pair(PAIRS - 1, 0)
                dve.wait_ge(rows_in, 144)
                link(dve.tensor_copy(rowf, rowi))
                q = 4 * P
                dve.wait_ge(base_in, 32)
                link(dve.tensor_copy(base_f[:, :], base_i[:, 0:NG]))
                link(dve.scalar_tensor_tensor(rowx[:, 0:q], rowf[:, 0:q], float(R), rowf[:, 2 * q:3 * q],
                                              ALU.mult, ALU.add))
                dve.scalar_tensor_tensor(rowx[:, q:2 * q], rowf[:, q:2 * q], float(R), rowf[:, 2 * q:3 * q],
                                         ALU.mult, ALU.add).then_inc(rows_done, 1)
                dve.wait_ge(rowsT_done, 4)
                link(dve.tensor_copy(idx_l[:, :], psum[0][:, :]))
                dve.tensor_copy(feat_rows[:, :], idx_l[:, 0:FR]).then_inc(rows_copied, 1)
                dve.tensor_copy(idx_r[:, :], psum[1][:, :]).then_inc(idx_done, 1)
                link(dve.tensor_copy(dst_t[:, :], psum[2][:, :]))
                m = NG - 1
                dve.memset(rel[:, ET:], 0.0)
                link(dve.tensor_tensor(rel[:, 0:m * G].rearrange("p (g j) -> p g j", j=G),
                                       dst_t[:, 0:m * G].rearrange("p (g j) -> p g j", j=G),
                                       psum[3][:, 0:m].unsqueeze(2).to_broadcast([P, m, G]), ALU.subtract))
                dve.tensor_tensor(rel[:, m * G:ET], dst_t[:, m * G:ET], psum[3][:, m:NG], ALU.subtract)\
                   .then_inc(rel_done, 1)
                dve.wait_ge(rel_done, 1)
                dve.tensor_reduce(far_col[:, :], rel[:, 0:ET], AX.X, ALU.max).then_inc(far_col_done, 1)
                late = far_row[:, 1:1 + NS - 1]
                link(dve.scalar_tensor_tensor(late, iota_w[0:1, 1:NS], float(TOK),
                                              base_f[0:1, ST + LAG:(NS - 1) * ST + LAG + 1:ST], ALU.mult, ALU.subtract))
                link(dve.tensor_reduce(late[:, 0:1], late, AX.X, ALU.max))
                dve.wait_ge(far_psum, 1)
                link(dve.tensor_reduce(far_row[:, 0:1], psum[4][0:1, 0:P], AX.X, ALU.max))
                link(dve.tensor_scalar(far_row[:, 0:1], far_row[:, 0:1], float(1 - W), None, ALU.add))
                link(dve.tensor_tensor(far_row[:, 0:1], far_row[:, 0:1], late[:, 0:1], ALU.max))
                dve.tensor_scalar(far_i[:, :], far_row[:, 0:1], 0.0, None, ALU.is_gt).then_inc(flag_done, 1)
                dve.wait_ge(xt_done, PAIRS)
                for u in range(2):
                    normalise(u, u, xn_done2)

                def turn(i, first, last):
                    for u in range(2):
                        if not last:
                            dve.wait_ge(xt_done2, i * 2 + (u + 1))
                            normalise(i * 2 + (u + 2), u, xn_done2)
                        if not first:
                            dve.wait_ge(feat_out[u], i * 16)
                        for b in range(2, 4):
                            dve.wait_ge(feat_done, i * 8 + (4 * u + b + 1))
                            dve.tensor_copy(fout[:, u * RHD + b * 512:u * RHD + (b + 1) * 512],
                                            psum[b][:, :]).then_inc(feat_dve, 1)

                turn(0, True, False)
                with dve.Fori(1, NT // 2 - 1) as i:
                    turn(i, False, False)
                turn(NT // 2 - 1, False, True)
                dve.memset(er_win, 0.0).then_inc(er_win_clear, 1)
                dve.wait_ge(typ_psum, 1)
                link(dve.tensor_copy(typ, psum[0][:, :]))

                def hot_build(n, u):
                    dve.tensor_tensor(hot_e[:, u * G * P:(u + 1) * G * P].rearrange("p (j s w) -> p j s w", j=G, w=W),
                                      iota_w[:, :].unsqueeze(1).unsqueeze(1).to_broadcast([P, G, GPI, W]),
                                      rel[:, ds(n * RING, RING)].rearrange("p (s j) -> p j s", j=G).unsqueeze(3)
                                      .to_broadcast([P, G, GPI, W]), ALU.is_equal).then_inc(hot_e_done, 1)

                def er_turn(i, first, last):
                    for u in range(2):
                        n = i * 2 + u
                        if not (last and u):
                            if not (first and u == 0):
                                dve.wait_ge(hotT_psum, n)
                            hot_build(n + 1, (u + 1) % 2)
                        dve.tensor_tensor(rel_mask.rearrange("p (j s r) -> p j s r", j=G, r=R),
                                          iota_w[:, 0:R].unsqueeze(1).unsqueeze(1).to_broadcast([P, G, GPI, R]),
                                          typ[:, ds(n * RING, RING)].rearrange("p (s j) -> p j s", j=G).unsqueeze(3)
                                          .to_broadcast([P, G, GPI, R]), ALU.is_equal).then_inc(mask_done, 1)
                        dve.wait_ge(mask_done, n + 1)
                        dve.wait_ge(er_psum, n + 1)
                        dve.tensor_tensor(er_all.rearrange("p (t r h) -> p t r h", r=R, h=H),
                                          psum[6 + u][:, 0:RING * RH].rearrange("p (t r h) -> p t r h", r=R, h=H),
                                          rel_mask.rearrange("p (t r) -> p t r", r=R).unsqueeze(3)
                                          .to_broadcast([P, RING, R, H]), ALU.mult).then_inc(er_picked, 1)
                        dve.wait_ge(er_picked, n + 1)
                        dve.tensor_reduce(er[:, ds(n * RING * H, RING * H)].rearrange("p (t h) -> p t h", h=H),
                                          er_all.rearrange("p (t r h) -> p t h r", r=R, h=H), AX.X, ALU.add)\
                           .then_inc(er_done, 1)

                hot_build(0, 0)
                er_turn(0, True, False)
                with dve.Fori(1, TURNS2 // 2 - 1) as i:
                    er_turn(i, False, False)
                er_turn(TURNS2 // 2 - 1, False, True)
                dve.wait_ge(er_done, TURNS2)
                dve.wait_ge(el_tab_out, 32)
                dve.wait_ge(er_tab_out, 16)
                dve.wait_ge(xt_copied2, NT)
                dve.wait_ge(feat_act, 2 * NT)
                dve.memset(dsti, -1).then_inc(dstb_clear, 1)
                dve.wait_ge(dstb_in, 16 * 6 * H)
                link(dve.tensor_copy(dstf, dsti))
                link(dve.tensor_tensor(same[:, 0:L + 1], dstf[:, 0:L + 1], dstf[:, 1:L + 2], ALU.is_equal))
                link(dve.tensor_scalar(pen[:, 0:L + 1], same[:, 0:L + 1], -1.0, BIG, ALU.add, ALU.mult))
                for n, near in enumerate((pen, same)):
                    for k in range(2):
                        last = dve.tensor_reduce(edge_col[:, 4 * n + 1 + 2 * k:4 * n + 2 + 2 * k], near[:, k:L + k], AX.X,
                                                 ALU.min)
                link(last)
                dve.memset(acc[:, :], 0.0)
                dve.wait_ge(scores_done, (ET - 1) // SG)
                dve.wait_ge(last_el_in, 16)
                flag = irregular(dve)
                with dve.If(flag == 0):
                    for j in range(G):
                        a = el[:, :].rearrange("p (i s j h) -> p i j s h", s=GPI, j=G, h=H)[:, :, j]
                        dve.tensor_tensor(a, a, er[:, :].rearrange("p (i j s h) -> p i j s h", s=GPI, j=G, h=H)[:, :, j],
                                          ALU.add).then_inc(score_sum, 1)
                    dve.wait_ge(score_sum, G)
                with dve.If(flag == 1):
                    dve.wait_ge(far_er_done, ET)
                    dve.tensor_tensor(el[:, 0:ET * H], el[:, 0:ET * H], er[:, 0:ET * H], ALU.add).then_inc(score_sum, G)
                    dve.wait_ge(score_sum, G)
                ev = el[:, :].rearrange("p (t h) -> p h t", h=H)
                dve.scalar_tensor_tensor(e_ht.rearrange("p (h t) -> p h t", h=H), ev, 0.2, ev, ALU.mult, ALU.max)\
                   .then_inc(eht_done, 1)
                dve.wait_ge(ebulk_done, 4)

                def segment_scans(n, near, data, op0, op1, start, fo, bo, both=False):
                    nxt = near[:, 1:L + 1]
                    dve.tensor_tensor_scan(fo, near[:, 0:L], data, start, op0, op1)
                    link(dve.tensor_tensor_scan(bo[:, ::-1], nxt[:, ::-1], data[:, ::-1], start, op0, op1))
                    c = 4 * (n - 1)
                    dve.tensor_copy(edge_col[:, c:c + 1], fo[:, L - 1:L])
                    dve.tensor_copy(edge_col[:, c + 2:c + 3], bo[:, 0:1]).then_inc(cols_done, 1)
                    dve.wait_ge(rows_psum, n)
                    dve.memset(scan_row[:, :], start)
                    link(dve.tensor_copy(edge_row[:, :], psum[4][0:1, :]))
                    r = edge_row[:, :].rearrange("o (k p) -> o k p", p=P)
                    dve.tensor_tensor_scan(scan_row[:, 1:P + 1], r[:, 1, :], r[:, 0, :], start, op0, op1)
                    back = scan_row[:, P + 2:2 * P + 2]
                    dve.tensor_tensor_scan(back[:, ::-1], r[:, 3, ::-1], r[:, 2, ::-1], start, op0, op1)\
                       .then_inc(srow_done, 1)
                    dve.wait_ge(carry_psum, n)
                    link(dve.tensor_copy(carry[:, :], psum[5][:, 0:2]))
                    link(dve.tensor_tensor_scan(fo, near[:, 0:L], data, carry[:, 0:1], op0, op1))
                    rest = fo if both else data
                    link(dve.tensor_tensor_scan(bo[:, ::-1], nxt[:, ::-1], rest[:, ::-1], carry[:, 1:2], op0, op1))

                segment_scans(1, pen, ebulk, ALU.add, ALU.max, -BIG, fwd, bwd, both=True)
                dve.tensor_tensor(ebulk, ebulk, bwd, ALU.subtract).then_inc(shifted, 1)
                dve.wait_ge(exp_done, 1)
                segment_scans(2, same, bwd, ALU.mult, ALU.add, 0.0, fwd, ebulk)
                link(dve.tensor_tensor(fwd, fwd, ebulk, ALU.add))
                link(dve.tensor_tensor(fwd, fwd, bwd, ALU.subtract))
                for b in range(0, L, 512):
                    n = min(512, L - b)
                    link(dve.reciprocal(ebulk[:, b:b + n], fwd[:, b:b + n]))
                    dve.tensor_tensor(fwd[:, b:b + n], bwd[:, b:b + n], ebulk[:, b:b + n], ALU.mult)\
                       .then_inc(alpha_bulk, 1)

            @block.tensor
            def _(pe):
                pe.wait_ge(const_done, 2)
                def transpose_pair(g, b):
                    pe.wait_ge(xn_done, g * 2 + 2)
                    if not isinstance(g, int) or g >= 2:
                        pe.wait_ge(xt_copied, g - 1)
                    for u in range(2):
                        for k in range(KC):
                            o = (b * 2 + u) * D + k * P
                            last = pe.transpose(psum[4 + b][:, u * D + k * P:u * D + (k + 1) * P], xn[:, o:o + P],
                                                ident[:, :])
                    last.then_inc(xt_done, 1)

                def el_pair(g, b):
                    pe.wait_ge(xt_copied, g + 1)
                    if not isinstance(g, int) or g >= 2:
                        pe.wait_ge(el_copied, g - 1)
                    for u in range(2):
                        for k in range(KC):
                            o = (b * 2 + u) * D + k * P
                            last = pe.matmul(psum[6 + b][:, u * 2 * RH:(u + 1) * 2 * RH], xT[:, o:o + P],
                                             wa[:, k * 2 * RH:(k + 1) * 2 * RH], start=k == 0, stop=k == KC - 1)
                    last.then_inc(el_done, 1)

                assert PAIRS % 2 == 1
                transpose_pair(0, 0)
                transpose_pair(1, 1)
                el_pair(0, 0)
                transpose_pair(2, 0)
                el_pair(1, 1)
                with pe.Fori(0, (PAIRS - 3) // 2) as i:
                    for u in range(2):
                        transpose_pair(i * 2 + (u + 3), (u + 1) % 2)
                        el_pair(i * 2 + (u + 2), u)
                el_pair(PAIRS - 1, 0)

                def transposes(n, u, first):
                    pe.wait_ge(xn_done2, n + 1)
                    if not first:
                        pe.wait_ge(xt_copied2, n - 1)
                    for k in range(KC):
                        last = pe.transpose(psum[6 + u][:, k * P:(k + 1) * P],
                                            xn[:, u * D + k * P:u * D + (k + 1) * P], ident[:, :])
                    last.then_inc(xt_done2, 1)

                def turn(i, first, last_turn):
                    for u in range(2):
                        pe.wait_ge(xt_copied2, i * 2 + (u + 1))
                        for b in range(4):
                            if b == 2 and not (last_turn and u == 1):
                                transposes(i * 2 + (u + 1), (u + 1) % 2, first and u == 0)
                            if not (first and u == 0):
                                pe.wait_ge(feat_act if b < 2 else feat_dve, i * 4 + (2 * u + b % 2 - 1))
                            for k in range(KC):
                                o = k * RHD + b * 512
                                last = pe.matmul(psum[b][:, :], xT[:, u * D + k * P:u * D + (k + 1) * P],
                                                 wconv[:, o:o + 512], start=k == 0, stop=k == KC - 1)
                            last.then_inc(feat_done, 1)

                pe.wait_ge(rows_done, 1)
                for k, s in enumerate((rowx[:, 0:512], rowx[:, 512:1024], rowf[:, 512:1024])):
                    for b in range(4):
                        last = pe.transpose(psum[k][:, b * P:(b + 1) * P], s[:, b * P:(b + 1) * P], ident[:, :])
                    last.then_inc(rowsT_done, 1)
                pe.matmul(psum[3][:, 0:NG], ones[0:1, :], base_f[0:1, :], start=True, stop=True).then_inc(rowsT_done, 1)

                pe.wait_ge(idx_done, 1)
                pe.wait_ge(rel_done, 1)
                pe.wait_ge(el_copied, PAIRS)
                pe.wait_ge(far_col_done, 1)
                pe.transpose(psum[4][0:1, 0:P], far_col[:, :], ident[:, :]).then_inc(far_psum, 1)
                transposes(0, 0, True)
                turn(0, True, False)
                with pe.Fori(1, NT // 2 - 1) as i:
                    turn(i, False, False)
                turn(NT // 2 - 1, False, True)
                pe.wait_ge(feat_act, 2 * NT)
                pe.wait_ge(feat_dve, 2 * NT)
                for b in range(4):
                    last = pe.transpose(psum[0][:, b * P:(b + 1) * P], rowf[:, (8 + b) * P:(9 + b) * P], ident[:, :])
                last.then_inc(typ_psum, 1)

                def hot_transpose(n, u, first):
                    pe.wait_ge(hot_e_done, n + 1)
                    if not first:
                        pe.wait_ge(hotT_done, n - 1)
                    for j in range(G):
                        last = pe.transpose(psum[4 + u][:, j * P:(j + 1) * P],
                                            hot_e[:, (u * G + j) * P:(u * G + j + 1) * P], ident[:, :])
                    last.then_inc(hotT_psum, 1)

                def er_turn(i, first, last_turn):
                    for u in range(2):
                        n = i * 2 + u
                        if not (last_turn and u):
                            hot_transpose(n + 1, (u + 1) % 2, first and u == 0)
                        pe.wait_ge(hotT_done, n + 1)
                        pe.wait_ge(er_win_in[u], i * (16 * GPI) + 16 * GPI)
                        if not first:
                            pe.wait_ge(er_picked, n - 1)
                        for j in range(G):
                            last = pe.matmul(psum[6 + u][:, j * P:(j + 1) * P],
                                             hotT[:, (u * G + j) * P:(u * G + j + 1) * P], er_win[:, u * P:(u + 1) * P],
                                             start=True, stop=True)
                        last.then_inc(er_psum, 1)

                hot_transpose(0, 0, True)
                er_turn(0, True, False)
                with pe.Fori(1, TURNS2 // 2 - 1) as i:
                    er_turn(i, False, False)
                er_turn(TURNS2 // 2 - 1, False, True)
                pe.wait_ge(eht_done, 1)
                for j in range(J):
                    last = pe.transpose(psum[j // 4][:, (j % 4) * P:(j % 4 + 1) * P], e_ht[:, j::J], ident[:, :])
                    if j % 4 == 3 or j == J - 1:
                        last.then_inc(ebulk_psum, 1)
                for n in (1, 2):
                    pe.wait_ge(cols_done, n)
                    for k in range(4):
                        last = pe.transpose(psum[4][0:1, k * P:(k + 1) * P], edge_col[:, 4 * (n - 1) + k:4 * (n - 1) + k + 1], ident[:, :])
                    last.then_inc(rows_psum, 1)
                    pe.wait_ge(srow_done, n)
                    pe.matmul(psum[5][:, 0:1], scan_row[0:1, 0:P], ones[0:1, 0:1], start=True, stop=True)
                    pe.matmul(psum[5][:, 1:2], scan_row[0:1, P + 3:2 * P + 3], ones[0:1, 0:1], start=True, stop=True)\
                      .then_inc(carry_psum, 1)
                pe.wait_ge(ebulk_done, 4)
                for j in range(J):
                    if j % 4 == 0:
                        pe.wait_ge(alpha_bulk, j // 4 + 1)
                    last = pe.transpose(psum[j // 4][:, (j % 4) * P:(j % 4 + 1) * P], fwd[:, j * P:(j + 1) * P], ident[:, :])
                    if j % 4 == 3 or j == J - 1:
                        last.then_inc(alpha_psum, 1)

        w1_sb, o = carve(0, X * KC * D)
        w2_sb, o = carve(o, X * KC * D)
        hot, o = carve(o, 2 * G * W)
        hot_a, o = carve(o, HOTS * G * H * W)
        xlT, o = carve(o, KC * TOK)
        xlT_next, o = carve(o, KC * TOK)
        hs = el[:, 0:KC * TOK]
        x2 = el[:, KC * TOK:KC * TOK + TC * D]
        xl, o = carve(o, TC * D)
        hT, o = carve(o, 4 * TOK)
        combT, o = carve(o, TOK)
        assert o <= WORK - (FR - NEAR) * D, o
        WIN = 480
        NW = NP_ // WIN
        far = weights[:, 2 * D:]
        iota_n = far[:, 0:WIN]
        hot_n = far[:, WIN:3 * WIN]
        far_a = far[:, 3 * WIN:3 * WIN + H]
        far_d = far[:, 4 * WIN:4 * WIN + NW]
        comb = er[:, 0:NT * X]
        expo, probs, top, top_f, pick = (er[:, NT * X + i * 32:NT * X + i * 32 + TC * X] for i in range(5))
        top_i = er[:, NT * X + 160:NT * X + 160 + TC * X].bitcast(U32)
        comb_c = er[:, NT * X + 224:NT * X + 224 + TC * X]
        mx = er[:, NT * X + 192:NT * X + 192 + TC]
        wt = er[:, NT * X + 200:NT * X + 200 + 2 * TC]
        mv2 = sb("mv2", [P, 2 * TC])
        st2 = sb("st2", [P, 6 * TC])
        rs2 = sb("rs2", [P, TC])
        accv = acc[:, :].rearrange("p (k n) -> p k n", k=KC)

        names = """xlT_kept experts_in feat_idx hot_done hot_a_done agg_done acc_step rwT_psum rwT_done hs_done x2_psum
            x2_done stats_done mv_done var2_done std2_done rs_done xl_done base_done xlT_psum xlT_done
            scores_psum score_max score_shift score_exp router_step combine_step comb_done combT_psum combT_done b2_psum
            b2_done h_psum h_done y_psum y_done out_done far_in far_iota far_idx far_mask far_hot far_sum far_add"""
        (xlT_kept, experts_in, feat_idx, hot_done, hot_a_done, agg_done, acc_step, rwT_psum, rwT_done, hs_done, x2_psum,
         x2_done, stats_done, mv_done, var2_done, std2_done, rs_done, xl_done, base_done, xlT_psum, xlT_done,
         scores_psum, score_max, score_shift, score_exp, router_step, combine_step, comb_done, combT_psum, combT_done, b2_psum,
         b2_done, h_psum, h_done, y_psum, y_done, out_done, far_in, far_iota, far_idx, far_mask, far_hot, far_sum,
         far_add) = [sem(n) for n in names.split()]

        def wait(eng, s, v):
            if not (isinstance(v, int) and v <= 0):
                eng.wait_ge(s, v)

        PREP = {4: ("h_copy",), 5: ("h_transpose", "x2"), 6: ("std",), 7: ("xl",), 8: ("xl_transpose", "xlT_copy"),
                9: ("scores",), 10: ("shift", "exp"), 11: ("route",), 13: ("combine",),
                14: ("weight_transpose", "weight_copy"), 15: ("bias2", "bias2_add", "xlT_keep")}
        EXPERTS = [("up", 0), ("up", 1)]
        for e in range(X - 2):
            EXPERTS += [("down", e), ("up", e + 2)]
        EXPERTS += [("down", X - 2), ("down", X - 1)]

        def super_turn(steps, s=None, p=None, c=None, windows=ST, nodes_done=None):
            for n in range(ST):
                if s is not None and n < windows:
                    steps["window"](s, n)
                if s is not None and n == windows and "last_window" in steps:
                    steps["last_window"]()
                if p is not None:
                    for name in PREP.get(n, ()):
                        if name in steps:
                            steps[name](p, nodes_done) if name == "h_copy" else steps[name](p)
                if c is not None and EXPERTS[n][0] in steps:
                    steps[EXPERTS[n][0]](c, EXPERTS[n][1])

        def dense(s):
            return isinstance(s, int) and s < 2

        ALL = 2 * NG
        FULL = NS - 1
        LASTW = NG - 1 - FULL * ST

        def late(p):
            return (p + 1) * (2 * ST) + 2 * LAG

        def schedule(eng, steps):
            super_turn(steps, 0)
            super_turn(steps, 1, 0, None, nodes_done=late(0))
            super_turn(steps, 2, 1, 0, nodes_done=late(1))
            with eng.Fori(3, FULL) as s:
                super_turn(steps, s, s - 1, s - 2, nodes_done=late(s - 1))
            super_turn(steps, FULL, FULL - 1, FULL - 2, LASTW, nodes_done=late(FULL - 1))
            super_turn(steps, None, NC - 1, NC - 2, nodes_done=ALL)
            super_turn(steps, None, None, NC - 1)

        def edges_only(eng, steps):
            super_turn(steps, 0)
            with eng.Fori(1, FULL) as s:
                super_turn(steps, s)
            super_turn(steps, FULL, windows=LASTW)

        def experts_only(eng, steps):
            super_turn(steps, None, 0, nodes_done=ALL)
            super_turn(steps, None, 1, 0, nodes_done=ALL)
            with eng.Fori(2, NC) as p:
                super_turn(steps, None, p, p - 1, nodes_done=ALL)
            super_turn(steps, None, None, NC - 1)

        with nc.Block() as block:
            @block.sync
            def _(sp):
                for e in range(X):
                    for w, to in ((w1, w1_sb), (w2, w2_sb)):
                        o = e * KC * D
                        sp.dma_start(to[:, o:o + KC * D].rearrange("p (k f) -> p k f", k=KC),
                                     w[e].rearrange("(k p) f -> p k f", p=P)).then_inc(experts_in, 16)
                with sp.Fori(0, NC - 1) as c:
                    sp.wait_ge(y_done, c * (X * TC) + X * TC)
                    sp.dma_start(out[ds(c * TOK, TOK), :].rearrange("(t p) d -> p t d", p=P),
                                 x_sb[:, ds(c * (TC * D), TC * D)].rearrange("p (t d) -> p t d", d=D)).then_inc(out_done, 16)
                sp.wait_ge(y_done, NC * X * TC)
                n = (NC - 1) * TC
                sp.dma_start(out[n * P:(NT - 1) * P, :].rearrange("(t p) d -> p t d", p=P),
                             x_sb[:, n * D:(NT - 1) * D].rearrange("p (t d) -> p t d", d=D)).then_inc(out_done, 16)
                sp.dma_start(out[(NT - 1) * P:N, :], x_sb[0:NLAST, (NT - 1) * D:NT * D]).then_inc(out_done, 16)
                sp.wait_ge(out_done, 16 * (NC + 1))
                sp.wait_ge(experts_in, 32 * X)

            @block.gpsimd
            def _(pool):
                def gather_window(i, n, tiles=G, rows=P):
                    pool.wait_ge(feat_idx, (i - 1) * ST + n + 1)
                    pool.nop(nofuse=True)
                    for j in range(tiles):
                        gather_feats(pool, n * G + j, rows)

                with pool.Fori(1, FULL) as i:
                    for n in range(ST):
                        gather_window(i, n)
                for n in range(LASTW):
                    gather_window(FULL, n)
                gather_window(FULL, LASTW, 1, ELAST)
                with pool.If(irregular(pool) == 1):
                    pool.wait_ge(acc_step, ALL)
                    pool.iota(iota_n, pattern=[[1, WIN]], base=0, channel_multiplier=0,
                              allow_small_or_imprecise_dtypes=True).then_inc(far_iota, 1)
                    with pool.Fori(0, ET) as t:
                        pool.wait_ge(far_idx, t + 1)
                        pool.nop(nofuse=True)
                        pool.indirect_dma_start(feats(0), None, feat_tab[:, :],
                                                bass.IndirectOffsetOnAxis(ap=feat_rows[:, 0:1], axis=0))\
                            .then_inc(far_in, 16)

            @block.scalar
            def _(act):
                def window(s, n):
                    if isinstance(s, int) and s == FULL:
                        return
                    act.wait_ge(agg_done, s * ST + (n + 1))
                    act.activation(feat_rows[:, n * G:(n + 1) * G],
                                   idx_l[:, ds(s * FR + (n + ST) * G, G)], ACT.Copy).then_inc(feat_idx, 1)

                def h_copy(p, nodes_done):
                    act.wait_ge(acc_step, nodes_done)
                    wait(act, x2_psum, p)
                    for k in range(KC):
                        act.activation(hs[:, k * TOK:(k + 1) * TOK], acc[:, ds(p * TOK + k * NP_, TOK)],
                                       ACT.Identity, bias=hb[:, k:k + 1]).then_inc(hs_done, 1)

                def std(p):
                    act.wait_ge(var2_done, p + 1)
                    act.activation(rs2[:, :], rs2[:, :], ACT.Sqrt).then_inc(std2_done, 1)

                def xlT_copy(p):
                    act.wait_ge(xlT_psum, p + 1)
                    wait(act, scores_psum, p)
                    wait(act, xlT_kept, p)
                    for k in range(KC):
                        act.activation(xlT_next[:, k * TOK:(k + 1) * TOK], psum[6 + k][:, 0:TOK], ACT.Copy)\
                           .then_inc(xlT_done, 1)

                def xlT_keep(p):
                    act.wait_ge(xlT_done, p * 2 + 2)
                    wait(act, h_psum, p * (2 * X))
                    act.activation(xlT, xlT_next, ACT.Copy).then_inc(xlT_kept, 1)

                def exp(p):
                    act.wait_ge(score_shift, p + 1)
                    act.activation(expo, expo, ACT.Exp).then_inc(score_exp, 1)

                def weight_copy(p):
                    act.wait_ge(combT_psum, p + 1)
                    wait(act, b2_psum, p)
                    act.activation(combT[0:X, :], psum[6][0:X, 0:TOK], ACT.Copy).then_inc(combT_done, 1)

                def up(c, e):
                    for f in range(KC):
                        act.wait_ge(h_psum, c * (2 * X) + (2 * e + f + 1))
                        wait(act, y_psum, c * (TC * X) + TC * (e - 1))
                        o = (e % 2 * 2 + f) * TOK
                        act.activation(hT[:, o:o + TOK], psum[2 + f][:, 0:TOK], ACT.Gelu,
                                       bias=b1_sb[:, e * KC + f:e * KC + f + 1]).then_inc(h_done, 1)

                steps = dict(window=window, h_copy=h_copy, std=std, xlT_copy=xlT_copy, exp=exp,
                             weight_copy=weight_copy,
                             xlT_keep=xlT_keep, up=up)
                act.wait_ge(rwT_psum, 1)
                act.activation(rwT[:, :], psum[6][:, 0:KC * X], ACT.Copy).then_inc(rwT_done, 1)
                flag = irregular(act)
                with act.If(flag == 0):
                    schedule(act, steps)
                with act.If(flag == 1):
                    edges_only(act, steps)
                    with act.Fori(0, ET) as t:
                        act.wait_ge(far_sum, t * (NW * H) + 1)
                        act.activation(feat_rows[:, 0:1], idx_l[:, ds(t, 1)], ACT.Copy).then_inc(far_idx, 1)
                    act.wait_ge(far_add, ET * NW * H + 1)
                    experts_only(act, steps)

            @block.vector
            def _(dve):
                def build(g, k):
                    wait(dve, agg_done, g - (HOTS - 1))
                    o = (k % 2) * G * W
                    hv = hot[:, o:o + G * W].rearrange("p (j w) -> p j w", j=G)
                    dve.tensor_tensor(hv, iota_w[:, :].unsqueeze(1).to_broadcast([P, G, W]),
                                      rel[:, ds(g * G, G)].unsqueeze(2).to_broadcast([P, G, W]), ALU.is_equal)\
                       .then_inc(hot_done, 1)
                    dve.wait_ge(hot_done, g + 1)
                    o = k * G * H * W
                    dve.tensor_tensor(hot_a[:, o:o + G * H * W].rearrange("p (j h w) -> p j h w", j=G, h=H),
                                      hv.unsqueeze(2).to_broadcast([P, G, H, W]),
                                      alpha[:, ds(g * (G * H), G * H)].rearrange("p (j h) -> p j h", h=H).unsqueeze(3)
                                      .to_broadcast([P, G, H, W]), ALU.mult).then_inc(hot_a_done, 1)

                def add_window(g, k, all_heads=False):
                    base = dve.value_load(base_i[0:1, ds(g, 1)], min_val=0, max_val=N - 1)
                    dve.wait_ge(agg_done, g + 1)
                    wait(dve, acc_step, g * 2)
                    step = (H + 2) * W if all_heads else 2 * W
                    pv = psum[k % 2][:, 0:KC * step].rearrange("p (k h w) -> p k h w", k=KC, w=W)
                    for half in range(2):
                        q = slice(half * HD, half * HD + HD)
                        dve.tensor_tensor(accv[q, :, ds(base, W)], accv[q, :, ds(base, W)], pv[q, :, half, :], ALU.add)\
                           .then_inc(acc_step, 1)

                def window(s, n):
                    if not (isinstance(s, int) and s * ST + n + 2 >= NG):
                        build(s * ST + (n + 2), (n + 2) % HOTS)
                    add_window(s * ST + n, n % 2, dense(s))

                def last_window():
                    add_window(NG - 1, 0)

                def x2_(p):
                    dve.wait_ge(x2_psum, p + 1)
                    wait(dve, base_done, p)
                    for b, (j, m) in enumerate(((0, 2), (2, 1))):
                        dve.tensor_tensor(x2[:, j * D:(j + m) * D], psum[6 + b][:, 0:m * D],
                                          x_sb[:, ds(p * (TC * D) + j * D, m * D)], ALU.add).then_inc(x2_done, 1)
                    dve.wait_ge(x2_done, p * 2 + 2)
                    for j in range(TC):
                        dve.bn_stats(st2[:, 6 * j:6 * j + 6], x2[:, j * D:(j + 1) * D]).then_inc(stats_done, 1)
                    dve.wait_ge(stats_done, p * TC + TC)
                    dve.nop(nofuse=True)
                    for j in range(TC):
                        dve.bn_aggr(mv2[:, 2 * j:2 * j + 2], st2[:, 6 * j:6 * j + 6]).then_inc(mv_done, 1)
                    dve.wait_ge(mv_done, p * TC + TC)
                    dve.tensor_scalar(rs2[:, :], mv2[:, 1::2], EPS, None, ALU.add).then_inc(var2_done, 1)

                def xl_(p):
                    dve.wait_ge(std2_done, p + 1)
                    dve.reciprocal(rs2[:, :], rs2[:, :]).then_inc(rs_done, 1)
                    dve.wait_ge(rs_done, p + 1)
                    wait(dve, xlT_psum, p)
                    for j in range(TC):
                        dve.tensor_scalar(xl[:, j * D:(j + 1) * D], x2[:, j * D:(j + 1) * D], mv2[:, 2 * j:2 * j + 1],
                                          rs2[:, j:j + 1], ALU.subtract, ALU.mult).then_inc(xl_done, 1)
                    dve.wait_ge(xl_done, p * TC + TC)
                    dve.tensor_tensor(x_sb[:, ds(p * (TC * D), TC * D)], x2, xl, ALU.add).then_inc(base_done, 1)

                def v(a):
                    return a.rearrange("p (t e) -> p t e", e=X)

                def wide(a):
                    return a.unsqueeze(2).to_broadcast([P, TC, X])

                def shift(p):
                    sc = v(psum[7][:, 0:TC * X])
                    dve.wait_ge(scores_psum, p + 1)
                    dve.tensor_reduce(mx, sc, AX.X, ALU.max).then_inc(score_max, 1)
                    dve.wait_ge(score_max, p + 1)
                    dve.tensor_tensor(v(expo), sc, wide(mx), ALU.subtract).then_inc(score_shift, 1)

                def links(counter, per, p):
                    n = [0]

                    def link(ins):
                        n[0] += 1
                        assert n[0] <= per
                        ins.then_inc(counter, 1)
                        dve.wait_ge(counter, p * per + n[0])
                        dve.nop(nofuse=True)
                    return link

                def route(p):
                    link = links(router_step, 5, p)
                    dve.wait_ge(score_exp, p + 1)
                    link(dve.tensor_reduce(mx, v(expo), AX.X, ALU.add))
                    link(dve.reciprocal(mx, mx))
                    link(dve.tensor_tensor(v(probs), v(expo), wide(mx), ALU.mult))
                    for t in range(TC):
                        last = dve.max(top[:, t * X:(t + 1) * X], probs[:, t * X:(t + 1) * X])
                    link(last)
                    for t in range(TC):
                        last = dve.max_index(top_i[:, t * X:(t + 1) * X], top[:, t * X:(t + 1) * X],
                                             probs[:, t * X:(t + 1) * X])
                    link(last)

                def combine(p):
                    link = links(combine_step, 6, p)
                    tv, iv = v(top), v(top_f)
                    dve.tensor_copy(top_f, top_i)
                    link(dve.tensor_tensor(mx, tv[:, :, 0], tv[:, :, 1], ALU.add))
                    link(dve.tensor_scalar(mx, mx, 1e-12, None, ALU.max))
                    link(dve.reciprocal(mx, mx))
                    for k in range(2):
                        last = dve.tensor_tensor(wt[:, k * TC:(k + 1) * TC], tv[:, :, k], mx, ALU.mult)
                    link(last)
                    for k, c in enumerate((expo, pick)):
                        last = dve.tensor_tensor(v(c), iota_w[:, 0:X].unsqueeze(1).to_broadcast([P, TC, X]),
                                                 wide(iv[:, :, k]), ALU.is_equal)
                    link(last)
                    for k, c in enumerate((expo, pick)):
                        last = dve.tensor_tensor(v(c), v(c), wide(wt[:, k * TC:(k + 1) * TC]), ALU.mult)
                    link(last)
                    wait(dve, combT_psum, p)
                    dve.tensor_tensor(comb[:, ds(p * (TC * X), TC * X)], expo, pick, ALU.add)
                    dve.tensor_tensor(comb_c, expo, pick, ALU.add).then_inc(comb_done, 1)

                def bias2_add(p):
                    dve.wait_ge(b2_psum, p + 1)
                    wait(dve, base_done, p + 1)
                    for b, (j, m) in enumerate(((0, 2), (2, 1))):
                        to = x_sb[:, ds(p * (TC * D) + j * D, m * D)]
                        dve.tensor_tensor(to, psum[6 + b][:, 0:m * D], to, ALU.add).then_inc(b2_done, 1)

                def down(c, e):
                    if e == 0:
                        dve.wait_ge(b2_done, c * 2 + 2)
                    for j in range(TC):
                        q = TC * e + j
                        dve.wait_ge(y_psum, c * (TC * X) + (q + 1))
                        if e:
                            dve.wait_ge(y_done, c * (TC * X) + (q - TC + 1))
                        to = x_sb[:, ds(c * (TC * D) + j * D, D)]
                        dve.scalar_tensor_tensor(to, psum[4 + q % 2][:, 0:D], comb[:, ds(c * (TC * X) + (j * X + e), 1)],
                                                 to, ALU.mult, ALU.add).then_inc(y_done, 1)

                steps = dict(window=window, last_window=last_window, x2=x2_, xl=xl_, shift=shift, route=route,
                             combine=combine,
                             bias2_add=bias2_add, down=down)
                build(0, 0)
                build(1, 1)
                flag = irregular(dve)
                with dve.If(flag == 0):
                    schedule(dve, steps)
                with dve.If(flag == 1):
                    edges_only(dve, steps)
                    dve.wait_ge(acc_step, ALL)
                    with dve.Fori(0, ET) as t:
                        dve.wait_ge(far_sum, t * (NW * H) + 1)
                        dve.tensor_scalar(far_d[:, 0:1], rel[:, ds(t, 1)], float(W), None, ALU.is_ge).then_inc(far_mask, 1)
                        dve.wait_ge(far_mask, t * (NW + 2) + 1)
                        dve.tensor_scalar(far_a, alpha[:, ds(t * H, H)], far_d[:, 0:1], None, ALU.mult)\
                           .then_inc(far_mask, 1)
                        dve.wait_ge(far_mask, t * (NW + 2) + 2)
                        for w in range(NW):
                            dve.tensor_scalar(far_d[:, w:w + 1], dst_t[:, ds(t, 1)], float(-w * WIN), None, ALU.add)\
                               .then_inc(far_mask, 1)
                        dve.wait_ge(far_mask, t * (NW + 2) + (NW + 2))
                        dve.wait_ge(far_iota, 1)
                        for w in range(NW):
                            for h in range(H):
                                n = w * H + h
                                b = n % 2
                                if n >= 2:
                                    dve.wait_ge(far_sum, t * (NW * H) + n)
                                dve.tensor_scalar(hot_n[:, b * WIN:(b + 1) * WIN], iota_n, far_d[:, w:w + 1],
                                                  far_a[:, h:h + 1], ALU.is_equal, ALU.mult).then_inc(far_hot, 1)
                                dve.wait_ge(far_sum, t * (NW * H) + (n + 2))
                                q = slice((h % 2) * HD, (h % 2 + 1) * HD)
                                to = accv[q, h // 2, w * WIN:(w + 1) * WIN]
                                dve.wait_ge(far_add, t * (NW * H) + (n + 1))
                                dve.tensor_tensor(to, to, psum[b][q, 0:WIN], ALU.add).then_inc(far_add, 1)
                    experts_only(dve, steps)

            @block.tensor
            def _(pe):
                def window(s, n, tiles=G, rows=P):
                    g = s * ST + n
                    pe.wait_ge(hot_a_done, g + 1)
                    pe.wait_ge(feats_in[n], s * (16 * G) + 16 * tiles)
                    wait(pe, acc_step, g * 2 - 2)
                    for q in range(KC):
                        for j in range(tiles):
                            m = (H if dense(s) else 2) * W
                            o = ((n % HOTS * G + j) * H + (0 if dense(s) else 2 * q)) * W
                            last = pe.matmul(psum[n % 2][:, q * m:(q + 1) * m],
                                             feats(n * G + j)[0:rows, q * P:(q + 1) * P],
                                             hot_a[0:rows, o:o + m], start=j == 0, stop=j == tiles - 1)
                    last.then_inc(agg_done, 1)

                def last_window():
                    window(FULL, LASTW, 1, ELAST)

                def h_transpose(p):
                    pe.wait_ge(hs_done, p * 2 + 2)
                    wait(pe, b2_done, p * 2)
                    for j in range(TC):
                        for k in range(KC):
                            o = (j % 2) * D + k * P
                            last = pe.transpose(psum[6 + j // 2][:, o:o + P], hs[:, k * TOK + j * P:k * TOK + (j + 1) * P],
                                                ident[:, :])
                    last.then_inc(x2_psum, 1)

                def xl_transpose(p):
                    pe.wait_ge(xl_done, p * TC + TC)
                    pe.wait_ge(x2_done, p * 2 + 2)
                    for k in range(KC):
                        for j in range(TC):
                            last = pe.transpose(psum[6 + k][:, j * P:(j + 1) * P], xl[:, j * D + k * P:j * D + (k + 1) * P],
                                                ident[:, :])
                    last.then_inc(xlT_psum, 1)

                def scores(p):
                    pe.wait_ge(xlT_done, p * 2 + 2)
                    for t in range(TC):
                        for k in range(KC):
                            o = k * TOK + t * P
                            last = pe.matmul(psum[7][:, t * X:(t + 1) * X], xlT_next[:, o:o + P], rwT[:, k * X:(k + 1) * X],
                                             start=k == 0, stop=k == KC - 1)
                    last.then_inc(scores_psum, 1)

                def weight_transpose(p):
                    pe.wait_ge(comb_done, p + 1)
                    for t in range(TC):
                        last = pe.transpose(psum[6][0:X, t * P:(t + 1) * P], comb_c[:, t * X:(t + 1) * X], ident[:, :])
                    last.then_inc(combT_psum, 1)

                def bias2(p):
                    pe.wait_ge(combT_done, p + 1)
                    pe.wait_ge(score_shift, p + 1)
                    for t in range(TC):
                        last = pe.matmul(psum[6 + t // 2][:, (t % 2) * D:(t % 2 + 1) * D], combT[0:X, t * P:(t + 1) * P],
                                         b2_sb[:, :], start=True, stop=True)
                    last.then_inc(b2_psum, 1)

                def up(c, e):
                    if e == 0:
                        pe.wait_ge(xlT_kept, c + 1)
                        pe.wait_ge(experts_in, 32 * X)
                    for f in range(KC):
                        wait(pe, h_done, c * (2 * X) + (2 * e + f - 1))
                        for k in range(KC):
                            o = (e * KC + k) * D + f * P
                            last = pe.matmul(psum[2 + f][:, 0:TOK], w1_sb[:, o:o + P], xlT[:, k * TOK:(k + 1) * TOK],
                                             start=k == 0, stop=k == KC - 1)
                        last.then_inc(h_psum, 1)

                def down(c, e):
                    pe.wait_ge(h_done, c * (2 * X) + (2 * e + 2))
                    for j in range(TC):
                        q = TC * e + j
                        wait(pe, y_done, c * (TC * X) + (q - 1))
                        for f in range(KC):
                            o = (e % 2 * 2 + f) * TOK + j * P
                            last = pe.matmul(psum[4 + q % 2][:, 0:D], hT[:, o:o + P],
                                             w2_sb[:, (e * KC + f) * D:(e * KC + f + 1) * D],
                                             start=f == 0, stop=f == KC - 1)
                        last.then_inc(y_psum, 1)

                steps = dict(window=window, last_window=last_window, h_transpose=h_transpose, xl_transpose=xl_transpose,
                             scores=scores, weight_transpose=weight_transpose,
                             bias2=bias2, up=up, down=down)
                for k in range(KC):
                    last = pe.transpose(psum[6][:, k * X:(k + 1) * X], rw_sb[:, k * P:(k + 1) * P], ident[0:X, 0:X])
                last.then_inc(rwT_psum, 1)
                pe.wait_ge(rwT_done, 1)
                flag = irregular(pe)
                with pe.If(flag == 0):
                    schedule(pe, steps)
                with pe.If(flag == 1):
                    edges_only(pe, steps)
                    pe.wait_ge(acc_step, ALL)
                    pe.transpose(psum[0][0:1, 0:P], far_col[:, :], ident[:, :]).then_inc(far_sum, 1)
                    pe.wait_ge(far_sum, 1)
                    pe.transpose(psum[0][0:1, 0:P], far_col[:, :], ident[:, :]).then_inc(far_add, 1)
                    with pe.Fori(0, ET) as t:
                        pe.wait_ge(far_in, t * 16 + 16)
                        for w in range(NW):
                            for h in range(H):
                                n = w * H + h
                                b = n % 2
                                pe.wait_ge(far_hot, t * (NW * H) + (n + 1))
                                pe.wait_ge(far_add, t * (NW * H) + (n if n else 1))
                                o = (h // 2) * P
                                pe.matmul(psum[b][:, 0:WIN], feats(0)[:, o:o + P], hot_n[:, b * WIN:(b + 1) * WIN],
                                          start=True, stop=True).then_inc(far_sum, 1)
                    experts_only(pe, steps)
    return nc


_INS = ["x", "src", "dst", "edge_type_8", "L0_gnn_conv_weights", "L0_gnn_attn_l", "L0_gnn_attn_r", "L0_gnn_h_bias",
        "L0_ffn_router_w", "L0_ffn_w1", "L0_ffn_b1", "L0_ffn_w2", "L0_ffn_b2"]


def kernel(**inputs):
    import numpy as _np
    import concourse.bacc as _bacc
    from concourse import mybir as _mybir
    from concourse.bass_utils import run_bass_kernel_spmd as _run

    nc = _bacc.Bacc("TRN2", target_bir_lowering=False, num_devices=1)
    arrays, args = {}, []
    for name in _INS:
        a = _np.ascontiguousarray(inputs[name])
        arrays[f"in_{name}_dram"] = a
        args.append(nc.dram_tensor(f"in_{name}_dram", a.shape, _mybir.dt.from_np(a.dtype), kind="ExternalInput").ap())
    args.append(nc.dram_tensor("out_0_dram", (N, D), _mybir.dt.float32, kind="ExternalOutput").ap())
    gnn_moe(nc, *args)
    r = _run(nc, [arrays], core_ids=[0])
    return r.results[0]["out_0_dram"]
```
